# Optimizing a Trainium2 kernel written in Bass

```python
import numpy as np
import jax
import jax.numpy as jnp

def _softmax(x, axis=-1):
    return jax.nn.softmax(x, axis=axis)

def _gelu(x):
    return jax.nn.gelu(x, approximate=True)

def _silu(x):
    return jax.nn.silu(x)

def _sigmoid(x):
    return jax.nn.sigmoid(x)

def _layernorm(x, axis=-1, eps=1e-05):
    m = jnp.mean(x, axis=axis, keepdims=True)
    v = jnp.var(x, axis=axis, keepdims=True)
    return (x - m) / jnp.sqrt(v + eps)

def _scatter_add(tgt, idx, src, axis=0):
    return tgt.at[idx].add(src)

def _segment_sum(src, seg, n):
    return jax.ops.segment_sum(src, seg, n)
kernel_name = 'mk_hybrid_d1_jaxref_r4_1ec242'

def setup_inputs(seed: int=0):
    np.random.seed(seed)
    _w = jnp.asarray

    def _L0_attn_a_setup():
        import jax, jax.numpy as jnp
        import numpy as np
        EMBED_DIM = 256
        NUM_HEADS = 16
        NUM_GLOBAL = 4
        NUM_LOCAL = NUM_HEADS - NUM_GLOBAL
        WINDOW = 64
        HEAD_DIM = EMBED_DIM // NUM_HEADS

        def _masks(seq_len):
            i = jnp.arange(seq_len)[:, None]
            j = jnp.arange(seq_len)[None, :]
            diff = i - j
            global_mask = diff < 0
            local_mask = (diff < 0) | (diff > WINDOW)
            return (global_mask, local_mask)

        def _attend(q, k, v, mask):
            scores = jnp.einsum('bhqd,bhkd->bhqk', q, k) * HEAD_DIM ** (-0.5)
            scores = jnp.where(mask[None, None], -jnp.inf, scores)
            w = jax.nn.softmax(scores, axis=-1)
            return jnp.einsum('bhqk,bhkd->bhqd', w, v)
        key = jax.random.key(seed)
        k1, k2, k3 = jax.random.split(key, 3)
        B, S = (4, 512)
        x = jax.random.normal(k1, (B, S, EMBED_DIM), dtype=jnp.float32)
        w_qkv = jax.random.normal(k2, (EMBED_DIM, 3 * EMBED_DIM), dtype=jnp.float32) * EMBED_DIM ** (-0.5)
        b_qkv = jnp.zeros((3 * EMBED_DIM,), dtype=jnp.float32)
        w_out = jax.random.normal(k3, (EMBED_DIM, EMBED_DIM), dtype=jnp.float32) * EMBED_DIM ** (-0.5)
        b_out = jnp.zeros((EMBED_DIM,), dtype=jnp.float32)
        return {'x': x, 'w_qkv': w_qkv, 'b_qkv': b_qkv, 'w_out': w_out, 'b_out': b_out}
    _L0_attn_a_in = _L0_attn_a_setup()

    def _L0_attn_b_setup():
        import jax, jax.numpy as jnp
        import numpy as np
        import math
        CHUNK = 128
        key = jax.random.key(seed)
        ks = jax.random.split(key, 12)
        B, S, H, D = (2, 1024, 256, 512)
        std = 0.02
        inp = {'hidden_states': jax.random.normal(ks[0], (B, S, H), jnp.float32), 'Wq': jax.random.normal(ks[1], (H, D), jnp.float32) * std, 'bq': jnp.zeros((D,), jnp.float32), 'Wk': jax.random.normal(ks[2], (H, D), jnp.float32) * std, 'bk': jnp.zeros((D,), jnp.float32), 'Wv': jax.random.normal(ks[3], (H, D), jnp.float32) * std, 'bv': jnp.zeros((D,), jnp.float32), 'Wg': jax.random.normal(ks[4], (H, D), jnp.float32) * std, 'bg': jnp.zeros((D,), jnp.float32), 'Wo': jax.random.normal(ks[5], (D, H), jnp.float32) * std, 'bo': jnp.zeros((H,), jnp.float32)}
        return inp
    _L0_attn_b_in = _L0_attn_b_setup()

    def _L0_ffn_setup():
        import jax, jax.numpy as jnp
        import numpy as np
        H = 256
        I = 128
        IS = 256
        E = 16
        G = 4
        TOPK_G = 2
        TOPK = 4
        SCALE = 2.5
        B, S = (2, 256)

        def _relu2(x):
            r = jax.nn.relu(x)
            return r * r

        def _route(scores, bias_corr):
            T = scores.shape[0]
            s_choice = scores + bias_corr
            gs = s_choice.reshape(T, G, E // G)
            group_scores = jnp.sum(jax.lax.top_k(gs, 2)[0], axis=-1)
            gidx = jax.lax.top_k(group_scores, TOPK_G)[1]
            gmask = jnp.sum(jax.nn.one_hot(gidx, G, dtype=scores.dtype), axis=1)
            smask = jnp.repeat(gmask, E // G, axis=1)
            masked = jnp.where(smask > 0, s_choice, 0.0)
            topk_idx = jax.lax.top_k(masked, TOPK)[1]
            topk_w = jnp.take_along_axis(scores, topk_idx, axis=1)
            topk_w = topk_w / (jnp.sum(topk_w, axis=-1, keepdims=True) + 1e-20)
            topk_w = topk_w * SCALE
            return (topk_idx, topk_w)
        key = jax.random.key(seed)
        ks = jax.random.split(key, 8)
        sd = 0.02
        return {'hidden_states': jax.random.normal(ks[0], (B, S, H), jnp.float32), 'Wg': jax.random.normal(ks[1], (E, H), jnp.float32) * sd, 'bias_corr': jax.random.normal(ks[2], (E,), jnp.float32) * 0.01, 'W1': jax.random.normal(ks[3], (E, I, H), jnp.float32) * sd, 'W2': jax.random.normal(ks[4], (E, H, I), jnp.float32) * sd, 'Ws1': jax.random.normal(ks[5], (IS, H), jnp.float32) * sd, 'Ws2': jax.random.normal(ks[6], (H, IS), jnp.float32) * sd}
    _L0_ffn_in = _L0_ffn_setup()
    _d = {'L0_attn_a_x': _L0_attn_a_in['x'], 'L0_attn_a_w_qkv': _L0_attn_a_in['w_qkv'], 'L0_attn_a_b_qkv': _L0_attn_a_in['b_qkv'], 'L0_attn_a_w_out': _L0_attn_a_in['w_out'], 'L0_attn_a_b_out': _L0_attn_a_in['b_out'], 'L0_attn_b_Wq': _L0_attn_b_in['Wq'], 'L0_attn_b_bq': _L0_attn_b_in['bq'], 'L0_attn_b_Wk': _L0_attn_b_in['Wk'], 'L0_attn_b_bk': _L0_attn_b_in['bk'], 'L0_attn_b_Wv': _L0_attn_b_in['Wv'], 'L0_attn_b_bv': _L0_attn_b_in['bv'], 'L0_attn_b_Wg': _L0_attn_b_in['Wg'], 'L0_attn_b_bg': _L0_attn_b_in['bg'], 'L0_attn_b_Wo': _L0_attn_b_in['Wo'], 'L0_attn_b_bo': _L0_attn_b_in['bo'], 'L0_ffn_Wg': _L0_ffn_in['Wg'], 'L0_ffn_bias_corr': _L0_ffn_in['bias_corr'], 'L0_ffn_W1': _L0_ffn_in['W1'], 'L0_ffn_W2': _L0_ffn_in['W2'], 'L0_ffn_Ws1': _L0_ffn_in['Ws1'], 'L0_ffn_Ws2': _L0_ffn_in['Ws2']}
    _x0 = _d['L0_attn_a_x']
    _d['L0_attn_a_x'] = jax.random.normal(jax.random.fold_in(jax.random.key(seed), 1), (16, 512, 256), dtype=_x0.dtype)
    del _x0
    return _d

def reference(L0_attn_a_x, L0_attn_a_w_qkv, L0_attn_a_b_qkv, L0_attn_a_w_out, L0_attn_a_b_out, L0_attn_b_Wq, L0_attn_b_bq, L0_attn_b_Wk, L0_attn_b_bk, L0_attn_b_Wv, L0_attn_b_bv, L0_attn_b_Wg, L0_attn_b_bg, L0_attn_b_Wo, L0_attn_b_bo, L0_ffn_Wg, L0_ffn_bias_corr, L0_ffn_W1, L0_ffn_W2, L0_ffn_Ws1, L0_ffn_Ws2):

    def _L0_attn_a_ref(x, w_qkv, b_qkv, w_out, b_out):
        import jax, jax.numpy as jnp
        import numpy as np
        EMBED_DIM = 256
        NUM_HEADS = 16
        NUM_GLOBAL = 4
        NUM_LOCAL = NUM_HEADS - NUM_GLOBAL
        WINDOW = 64
        HEAD_DIM = EMBED_DIM // NUM_HEADS

        def _masks(seq_len):
            i = jnp.arange(seq_len)[:, None]
            j = jnp.arange(seq_len)[None, :]
            diff = i - j
            global_mask = diff < 0
            local_mask = (diff < 0) | (diff > WINDOW)
            return (global_mask, local_mask)

        def _attend(q, k, v, mask):
            scores = jnp.einsum('bhqd,bhkd->bhqk', q, k) * HEAD_DIM ** (-0.5)
            scores = jnp.where(mask[None, None], -jnp.inf, scores)
            w = jax.nn.softmax(scores, axis=-1)
            return jnp.einsum('bhqk,bhkd->bhqd', w, v)
        B, S, _ = x.shape
        qkv = x @ w_qkv + b_qkv
        q, k, v = jnp.split(qkv, 3, axis=-1)

        def heads(t):
            return t.reshape(B, S, NUM_HEADS, HEAD_DIM).transpose(0, 2, 1, 3)
        q, k, v = (heads(q), heads(k), heads(v))
        gmask, lmask = _masks(S)
        ctx_g = _attend(q[:, :NUM_GLOBAL], k[:, :NUM_GLOBAL], v[:, :NUM_GLOBAL], gmask)
        ctx_l = _attend(q[:, NUM_GLOBAL:], k[:, NUM_GLOBAL:], v[:, NUM_GLOBAL:], lmask)
        ctx = jnp.concatenate([ctx_g, ctx_l], axis=1)
        ctx = ctx.transpose(0, 2, 1, 3).reshape(B, S, EMBED_DIM)
        return ctx @ w_out + b_out

    def _L0_attn_b_ref(hidden_states, Wq, bq, Wk, bk, Wv, bv, Wg, bg, Wo, bo):
        import jax, jax.numpy as jnp
        import numpy as np
        import math
        CHUNK = 128
        B, S, H = hidden_states.shape
        D = Wq.shape[1]
        cs = CHUNK
        nC = S // cs
        q = hidden_states @ Wq + bq
        k = hidden_states @ Wk + bk
        v = hidden_states @ Wv + bv
        gate = jax.nn.sigmoid(hidden_states @ Wg + bg)
        qc = q.reshape(B, nC, cs, D)
        kc = k.reshape(B, nC, cs, D)
        vc = v.reshape(B, nC, cs, D)
        gc = gate.reshape(B, nC, cs, D)
        scale = 1.0 / math.sqrt(D)
        attn = jnp.einsum('bncd,bnkd->bnck', qc, kc) * scale
        causal = jnp.tril(jnp.ones((cs, cs), bool))
        attn = jnp.where(causal, attn, -jnp.inf)
        attn = jax.nn.softmax(attn, axis=-1)
        local = jnp.einsum('bnck,bnkd->bncd', attn, vc)

        def step(state, xs):
            qi, ki, vi = xs
            cross = jnp.einsum('bcd,bde->bce', qi, state)
            state = state + jnp.einsum('bcd,bce->bde', ki, vi)
            return (state, cross)
        state0 = jnp.zeros((B, D, D), hidden_states.dtype)
        _, cross = jax.lax.scan(step, state0, (qc.transpose(1, 0, 2, 3), kc.transpose(1, 0, 2, 3), vc.transpose(1, 0, 2, 3)))
        cross = cross.transpose(1, 0, 2, 3)
        out = (local + cross) * gc
        out = out.reshape(B, S, D)
        return out @ Wo + bo

    def _L0_ffn_ref(hidden_states, Wg, bias_corr, W1, W2, Ws1, Ws2):
        import jax, jax.numpy as jnp
        import numpy as np
        H = 256
        I = 128
        IS = 256
        E = 16
        G = 4
        TOPK_G = 2
        TOPK = 4
        SCALE = 2.5
        B, S = (2, 256)

        def _relu2(x):
            r = jax.nn.relu(x)
            return r * r

        def _route(scores, bias_corr):
            T = scores.shape[0]
            s_choice = scores + bias_corr
            gs = s_choice.reshape(T, G, E // G)
            group_scores = jnp.sum(jax.lax.top_k(gs, 2)[0], axis=-1)
            gidx = jax.lax.top_k(group_scores, TOPK_G)[1]
            gmask = jnp.sum(jax.nn.one_hot(gidx, G, dtype=scores.dtype), axis=1)
            smask = jnp.repeat(gmask, E // G, axis=1)
            masked = jnp.where(smask > 0, s_choice, 0.0)
            topk_idx = jax.lax.top_k(masked, TOPK)[1]
            topk_w = jnp.take_along_axis(scores, topk_idx, axis=1)
            topk_w = topk_w / (jnp.sum(topk_w, axis=-1, keepdims=True) + 1e-20)
            topk_w = topk_w * SCALE
            return (topk_idx, topk_w)
        b, s, h = hidden_states.shape
        flat = hidden_states.reshape(-1, h)
        T = flat.shape[0]
        logits = flat.astype(jnp.float32) @ Wg.T
        scores = jax.nn.sigmoid(logits)
        topk_idx, topk_w = _route(scores, bias_corr)
        topk_w = topk_w.astype(hidden_states.dtype)
        cw = jnp.zeros((T, E), flat.dtype)
        cw = cw.at[jnp.arange(T)[:, None], topk_idx].add(topk_w)
        hid = _relu2(jnp.einsum('th,eih->eti', flat, W1))
        y = jnp.einsum('eti,ehi->eth', hid, W2)
        out = jnp.einsum('eth,te->th', y, cw)
        shared = _relu2(flat @ Ws1.T) @ Ws2.T
        return (out + shared).reshape(b, s, h)
    x = L0_attn_a_x
    x = x + _L0_attn_a_ref(_layernorm(x, axis=-1), L0_attn_a_w_qkv, L0_attn_a_b_qkv, L0_attn_a_w_out, L0_attn_a_b_out)
    x = x + _L0_ffn_ref(_layernorm(x, axis=-1), L0_ffn_Wg, L0_ffn_bias_corr, L0_ffn_W1, L0_ffn_W2, L0_ffn_Ws1, L0_ffn_Ws2)
    x = x + _L0_attn_b_ref(_layernorm(x, axis=-1), L0_attn_b_Wq, L0_attn_b_bq, L0_attn_b_Wk, L0_attn_b_bk, L0_attn_b_Wv, L0_attn_b_bv, L0_attn_b_Wg, L0_attn_b_bg, L0_attn_b_Wo, L0_attn_b_bo)
    x = x + _L0_ffn_ref(_layernorm(x, axis=-1), L0_ffn_Wg, L0_ffn_bias_corr, L0_ffn_W1, L0_ffn_W2, L0_ffn_Ws1, L0_ffn_Ws2)
    return x

_drawn_inputs = setup_inputs


def setup_inputs(seed=0):
    import zlib

    import numpy as np

    out = dict(_drawn_inputs(seed))
    spreads = {'L0_attn_a_b_qkv': (0.0, 0.1),
     'L0_attn_a_b_out': (0.0, 0.1),
     'L0_attn_b_bq': (0.0, 0.1),
     'L0_attn_b_bk': (0.0, 0.1),
     'L0_attn_b_bv': (0.0, 0.1),
     'L0_attn_b_bg': (0.0, 0.1),
     'L0_attn_b_bo': (0.0, 0.458)}
    factors = {'L0_ffn_bias_corr': 4.364}
    for name, (base, spread) in spreads.items():
        noise = np.random.default_rng([zlib.crc32(name.encode()), seed]).standard_normal(out[name].shape)
        drawn = base * np.exp(spread * noise) if base else spread * noise
        out[name] = jnp.asarray(drawn.astype(out[name].dtype))
    for name, factor in factors.items():
        out[name] = (out[name] * factor).astype(out[name].dtype)
    return out
```

```python
from contextlib import ExitStack

import concourse.bass as bass
from concourse import mybir

P = 128
F32 = mybir.dt.float32
BF16 = mybir.dt.bfloat16
ALU = mybir.AluOpType
ACT = mybir.ActivationFunctionType
AX = mybir.AxisListType

H = 256
KT = H // P
SEQ = 512
TB = SEQ // P
EPS = 1e-5
MASKED = -1e30


def at_least(eng, sem, value):
    if isinstance(value, int) and value <= 0:
        return
    eng.wait_ge(sem, value)


def in_register(eng, value):
    return value if isinstance(value, int) else eng.to_reg(value)


def wait_apart(eng, sem, value, past, past_value):
    value = in_register(eng, value)
    if isinstance(value, int) and value <= 0:
        return
    eng.wait_ge(past, past_value)
    eng.wait_ge(sem, value)


def ev(s, per_seq, i):
    if isinstance(s, int) and s < 0:
        return 0
    return s * per_seq + (i + 1)


def seq_rows(eng, dram, s):
    row = s * SEQ if isinstance(s, int) else eng.snap(s * SEQ)
    return dram[bass.ds(row, SEQ), :].rearrange("(b p) h -> p b h", p=P)


def row_broadcast(vec):
    return vec.partition_broadcast(P)


HEADS, GLOBAL, DH, WINDOW = 16, 4, 16, 64
HT = 6
ONES = HT * DH
QT = -(-HEADS // HT)
BAND = P + WINDOW
VW = 32


def units_of_scores():
    out = []
    for kb in range(TB):
        for half in range(2):
            out.append((0, kb, (2 * half, 2 * half + 1), SEQ - P * kb))
    for t in range(1, HEADS // 4):
        for kb in range(TB):
            out.append((t, kb, tuple(range(4 * t, 4 * t + 4)), min(BAND, SEQ - P * kb)))
    return out


def units_of_max():
    glob, loc = [], []
    for qb in range(TB):
        n = P * (qb + 1)
        per = SEQ // n
        for h in range(0, GLOBAL, per):
            glob.append((tuple(range(h, h + per)), qb, 0, n))
    for qb in range(TB):
        n = P if qb == 0 else BAND
        per = 4 if qb == 0 else 2
        for h in range(GLOBAL, HEADS, per):
            loc.append((tuple(range(h, h + per)), qb, P * (qb + 1) - n, n))
    return glob, loc


def phase_a(nc, x_in, x_out, w_qkv, b_qkv, w_out, b_out, nseq):
    UNITS = units_of_scores()
    NU = len(UNITS)
    MAXG, MAXL = units_of_max()
    FRONT = ([("T", k) for k in range(KT)] + [(c, t) for t in range(QT) for c in ("q", "k")] +
             [("v", 0), ("v", 1)] + [("m", u) for u in MAXG] + [("mT", 0)] +
             [("m", u) for u in MAXL] + [("mT", 1)])
    NF = len(FRONT)
    assert NF % 2 == 0 and NU % 4 == 0
    by_act = [kind in ("T", "q", "k") for kind, _ in FRONT]
    act_no = [sum(by_act[:i]) for i in range(NF)]
    dve_no = [i - act_no[i] for i in range(NF)]
    NFA, NFD = sum(by_act), NF - sum(by_act)
    first = {}
    for i, (kind, _) in enumerate(FRONT):
        first.setdefault(kind, i)
    slot_front = {u: [] for u in range(NU)}
    seq_slots = ([5] * KT + [6, 6, 7, 7, 8, 8] + [9, 9] +
                 [10 + (i * 3) // len(MAXG) for i in range(len(MAXG))] + [13] +
                 [14 + (i * 6) // len(MAXL) for i in range(len(MAXL))] + [19])
    for i, u in enumerate(seq_slots):
        slot_front[u].append(i)
    TAIL = [("N", 0), ("N", 1), ("C", 0), ("N", 2), ("N", 3), ("C", 1), ("O", 0), ("O", 1)]
    NTAIL = len(TAIL)
    TAIL_AT = {10: [0], 14: [1], 16: [2], 18: [3]}
    LATE_AT = {2: [4], 3: [5], 4: [6], 5: [7]}
    t_first = {0: 0, 1: 8, 2: 12, 3: 16}
    t_last = {0: 7, 1: 11, 2: 15, 3: 19}

    with ExitStack() as ctx:
        def sb(name, shape, dt=F32):
            return ctx.enter_context(nc.sbuf_tensor("a_" + name, shape, dt))

        def sem(name):
            return ctx.enter_context(nc.semaphore("a_" + name))

        ident = sb("ident", [P, P])
        identb = sb("identb", [P, P], BF16)
        mask_g = sb("mask_g", [P, P], BF16)
        mask_l = sb("mask_l", [P, BAND], BF16)
        headmask = sb("headmask", [P, HT])
        wq = sb("wq", [P, KT, QT, P])
        wk = sb("wk", [P, KT, QT, P])
        wv = sb("wv", [P, KT, H])
        wo = sb("wo", [P, KT, H])
        bq = sb("bq", [P, QT])
        bk = sb("bk", [P, QT])
        bv = sb("bv", [P, H])
        bo = sb("bo", [P, H])
        xin = sb("xin", [P, 2, TB, H])
        xres = sb("xres", [P, 2, TB, H])
        stats = sb("stats", [P, TB, 6])
        mean = sb("mean", [P, TB])
        var, guess, yy, rstd = sb("var", [P, TB]), sb("guess", [P, TB]), sb("yy", [P, TB]), sb("rstd", [P, TB])
        lnv = sb("lnv", [P, TB])
        xn = sb("xn", [P, TB, H])
        xT = sb("xT", [P, KT, SEQ])
        qf = sb("qf", [P, QT, SEQ])
        kf = sb("kf", [P, 2, QT, SEQ])
        qm = sb("qm", [P, 2, HEADS, SEQ])
        qb16 = sb("qb16", [P, HEADS, SEQ], BF16)
        kb16 = sb("kb16", [P, QT, SEQ], BF16)
        vv = sb("vv", [P, 2, TB, HEADS, VW])
        pt = sb("pt", [P, 4, 1024])
        pvs = sb("pvs", [P, 2, SEQ])
        rden = sb("rden", [P, TB, 4])
        ctxn = sb("ctxn", [P, TB, HEADS, DH])
        ctxT = sb("ctxT", [P, KT, SEQ])
        mx = sb("mx", [P, HEADS, TB])
        mTg = sb("mTg", [GLOBAL, SEQ])
        mTl = sb("mTl", [HEADS - GLOBAL, SEQ])

        S = ctx.enter_context(nc.psum_tensor("a_S", [P, 2, 2, 512], F32))
        FB = ctx.enter_context(nc.psum_tensor("a_FB", [P, 2, 512], F32))
        PV = ctx.enter_context(nc.psum_tensor("a_PV", [P, 512], F32))
        TL = ctx.enter_context(nc.psum_tensor("a_TL", [P, 512], F32))

        w_loaded, zeroed, w_ready = sem("w_loaded"), sem("zeroed"), sem("w_ready")
        dve_ready = sem("dve_ready")
        x_loaded = sem("x_loaded")
        res_ready = sem("res_ready")
        ln_stat = sem("ln_stat")
        ln_var = sem("ln_var")
        ln_log = sem("ln_log")
        ln_guess = sem("ln_guess")
        ln_done = sem("ln_done")
        f_done = sem("f_done")
        f_act = sem("f_act")
        f_dve = sem("f_dve")
        q_masked = sem("q_masked")
        k_half = sem("k_half")
        m_row = sem("m_row")
        s_done = sem("s_done")
        e_done = sem("e_done")
        p_first = sem("p_first")
        p_done = sem("p_done")
        pv_done = sem("pv_done")
        pv_out = sem("pv_out")
        t_done = sem("t_done")
        t_act = sem("t_act")
        t_dve = sem("t_dve")
        r_done = sem("r_done")
        x_stored = sem("x_stored")

        N_AT = [TAIL.index(("N", t)) for t in range(4)]
        C_AT = [TAIL.index(("C", t)) for t in range(2)]
        LN_SLOT, RES_SLOT = 3, 7
        NLOC = NU - 8
        NSTAT = TB + 10
        W_DMAS = 16 * (2 * KT * QT + 2 * QT + 4)
        NTA, NTD = 2, 6
        t_act_no = [0, 0, 0, 1, 1, 1, 2, 2]
        mt_at = [FRONT.index(("mT", g)) for g in range(2)]

        with nc.Block() as block:
            @block.sync
            def _(sp):
                sp.wait_ge(zeroed, 1)
                for w, c0 in ((wq, 0), (wk, H)):
                    for k in range(KT):
                        for t in range(QT):
                            n = min(ONES, H - t * ONES)
                            sp.dma_start(w[:, k, t, 0:n],
                                         w_qkv[k * P:(k + 1) * P, c0 + t * ONES:c0 + t * ONES + n]
                                         ).then_inc(w_loaded, 16)
                for b, c0 in ((bq, 0), (bk, H)):
                    for t in range(QT):
                        n = min(ONES, H - t * ONES)
                        sp.dma_start(b[0:n, t:t + 1],
                                     b_qkv[c0 + t * ONES:c0 + t * ONES + n].rearrange("(p o) -> p o", o=1)
                                     ).then_inc(w_loaded, 16)
                sp.dma_start(wv[:], w_qkv[:, 2 * H:3 * H].rearrange("(k p) n -> p k n", p=P)).then_inc(w_loaded, 16)
                sp.dma_start(wo[:], w_out.rearrange("(k p) n -> p k n", p=P)).then_inc(w_loaded, 16)
                sp.dma_start(bv[:], row_broadcast(b_qkv[2 * H:3 * H])).then_inc(w_loaded, 16)
                sp.dma_start(bo[:], row_broadcast(b_out)).then_inc(w_loaded, 16)
                sp.wait_ge(w_loaded, W_DMAS)

            @block.gpsimd
            def _(pool):
                nc.gpsimd.memset(ident[:], 0.0).then_inc(w_ready, 1)
                nc.gpsimd.memset(mask_g[:], 0.0).then_inc(w_ready, 1)
                nc.gpsimd.memset(mask_l[:], 0.0).then_inc(w_ready, 1)
                nc.gpsimd.memset(headmask[:], DH ** -0.5).then_inc(w_ready, 1)
                pool.wait_ge(w_ready, 4)
                nc.gpsimd.affine_select(out=ident[:], in_=ident[:], compare_op=ALU.not_equal, fill=1.0,
                                        base=0, pattern=[[-1, P]], channel_multiplier=1).then_inc(w_ready, 1)
                nc.gpsimd.affine_select(out=mask_g[:], in_=mask_g[:], compare_op=ALU.is_ge, fill=MASKED,
                                        base=0, pattern=[[-1, P]], channel_multiplier=1).then_inc(w_ready, 1)
                nc.gpsimd.affine_select(out=mask_l[:], in_=mask_l[:], compare_op=ALU.is_ge, fill=MASKED,
                                        base=WINDOW, pattern=[[-1, BAND]], channel_multiplier=1).then_inc(w_ready, 1)
                nc.gpsimd.affine_select(out=headmask[:], in_=headmask[:], compare_op=ALU.is_ge, fill=0.0,
                                        base=0, pattern=[[-DH, HT]], channel_multiplier=1).then_inc(w_ready, 1)
                pool.wait_ge(w_ready, 8)
                nc.gpsimd.affine_select(out=mask_l[:], in_=mask_l[:], compare_op=ALU.is_ge, fill=MASKED,
                                        base=0, pattern=[[1, BAND]], channel_multiplier=-1).then_inc(w_ready, 1)
                nc.gpsimd.affine_select(out=headmask[:], in_=headmask[:], compare_op=ALU.is_ge, fill=0.0,
                                        base=DH - 1, pattern=[[DH, HT]], channel_multiplier=-1).then_inc(w_ready, 1)
                nc.gpsimd.tensor_copy(identb[:], ident[:]).then_inc(w_ready, 1)
                nc.gpsimd.memset(vv[:, :, :, :, DH:VW], 1.0).then_inc(w_ready, 1)
                pool.wait_ge(w_ready, 12)

            @block.vector
            def _(dve):
                nc.vector.memset(wq[:], 0.0).then_inc(dve_ready, 1)
                nc.vector.memset(wk[:], 0.0).then_inc(dve_ready, 1)
                nc.vector.memset(bq[:], 0.0).then_inc(dve_ready, 1)
                nc.vector.memset(bk[:], 0.0).then_inc(dve_ready, 1)
                dve.wait_ge(dve_ready, 4)
                nc.vector.memset(bk[ONES:ONES + 1, :], 1.0).then_inc(zeroed, 1)
                dve.wait_ge(zeroed, 1)


        with nc.Block() as block:

            def iterations(eng, body):
                body(-1, 1, False, False, True)
                body(0, 0, False, True, True)
                with eng.Fori(1, nseq - 3, 2) as r:
                    body(r, 1, True, True, True)
                    body(r + 1, 0, True, True, True)
                body(nseq - 3, 1, True, True, True)
                body(nseq - 2, 0, True, True, True)
                body(nseq - 1, 1, True, True, False)
                body(nseq, 0, True, False, False)

            @block.sync
            def _(sp):
                def load(s, par):
                    rows = seq_rows(sp, x_in, s)
                    need = [in_register(sp, v) for v in (ev(s - 2, 1, 0), ev(s - 2, 1, 0), 16 * s,)]
                    at_least(sp, ln_done, need[0])
                    at_least(sp, res_ready, need[1])
                    at_least(sp, x_loaded, need[2])
                    sp.dma_start(xin[:, par], rows).then_inc(x_loaded, 16)

                def m_rows(s, par, g):
                    src, h0, h1 = (mTg, 0, GLOBAL) if g == 0 else (mTl, GLOBAL, HEADS)
                    need = [in_register(sp, v) for v in (ev(s, NFD, dve_no[mt_at[g]]), ev(s - 2, NU, NU - 1), 16 * (2 * s + g),)]
                    at_least(sp, f_dve, need[0])
                    at_least(sp, s_done, need[1])
                    at_least(sp, m_row, need[2])
                    sp.dma_start(qm[ONES:ONES + 1, par, h0:h1, :], src[:]).then_inc(m_row, 16)

                def body(s, par, tail, core, front):
                    if tail:
                        rows = seq_rows(sp, x_out, s - 1)
                        summed, stored = in_register(sp, ev(s - 1, NTD, NTD - 1)), in_register(sp, 16 * s)
                    if isinstance(s, int) and s == -1:
                        load(0, 0)
                        load(1, 1)
                    elif not isinstance(s, int) or s + 2 < nseq:
                        load(s + 2, par)
                    if tail:
                        at_least(sp, t_dve, summed)
                        sp.dma_start(rows, xres[:, 1 - par]).then_inc(x_stored, 16)
                        at_least(sp, x_stored, stored)
                    if front:
                        m_rows(s + 1, 1 - par, 0)
                        m_rows(s + 1, 1 - par, 1)

                iterations(sp, body)
                sp.wait_ge(x_stored, 16 * nseq)

            @block.gpsimd
            def _(pool):
                def select(s, u):
                    t, kb, heads, n = UNITS[u]
                    wait_apart(pool, e_done, ev(s, NU, u), w_ready, 12)
                    nh = len(heads)
                    v = pt[:, u % 4, 0:nh * n].rearrange("p (h q) -> p h q", q=n)
                    ins = nc.gpsimd.affine_select(out=v[:, :, 0:P], in_=v[:, :, 0:P], compare_op=ALU.is_ge,
                                                  fill=0.0, base=0, pattern=[[0, nh], [1, P]],
                                                  channel_multiplier=-1)
                    if t > 0:
                        ins.then_inc(p_first, 1)
                        wait_apart(pool, p_first, ev(s, NLOC, u - 8), w_ready, 12)
                        ins = nc.gpsimd.affine_select(out=v[:, :, WINDOW:n], in_=v[:, :, WINDOW:n],
                                                      compare_op=ALU.is_ge, fill=0.0, base=0,
                                                      pattern=[[0, nh], [-1, n - WINDOW]],
                                                      channel_multiplier=1)
                    ins.then_inc(p_done, 1)

                def residual(s, par):
                    at_least(pool, x_loaded, 16 * (s + 1))
                    at_least(pool, x_stored, 16 * (s - 1))
                    nc.gpsimd.tensor_tensor(xres[:, par], xin[:, par],
                                            bo[:].unsqueeze(1).to_broadcast([P, TB, H]),
                                            ALU.add).then_inc(res_ready, 1)

                def body(s, par, tail, core, front):
                    for u in range(NU):
                        if core:
                            select(s, u)
                        if front and u == RES_SLOT:
                            residual(s + 1, 1 - par)

                iterations(pool, body)

            @block.scalar
            def _(act):
                def front_use(s, par, i):
                    kind, k = FRONT[i]
                    if not by_act[i]:
                        return
                    at_least(act, f_done, ev(s, NF, i))
                    src = FB[:, i % 2, :]
                    if kind == "T":
                        at_least(act, f_done, ev(s - 1, NF, first["v"] + 1))
                        nc.scalar.copy(xT[:, k, :], src).then_inc(f_act, 1)
                    elif kind == "q":
                        at_least(act, q_masked, ev(s - 1, QT, k))
                        nc.scalar.activation(qf[0:ONES, k, :], src[0:ONES], ACT.Identity,
                                             bias=bq[0:ONES, k:k + 1]).then_inc(f_act, 1)
                    else:
                        at_least(act, s_done, ev(s - 2, NU, NU - 1))
                        at_least(act, k_half, ev(s - 2, QT, k))
                        nc.scalar.activation(kf[0:ONES + 1, par, k, :], src[0:ONES + 1], ACT.Identity,
                                             bias=bk[0:ONES + 1, k:k + 1]).then_inc(f_act, 1)

                def rsqrt_guess(s):
                    at_least(act, ln_var, ev(s, 1, 0))
                    nc.scalar.activation(lnv[:], var[:], ACT.Ln).then_inc(ln_log, 1)
                    at_least(act, ln_log, ev(s, 1, 0))
                    nc.scalar.activation(guess[:], lnv[:], ACT.Exp, scale=-0.5).then_inc(ln_guess, 1)

                def exps(s, u):
                    _, _, heads, n = UNITS[u]
                    nh = len(heads)
                    w = nh * n // 2
                    at_least(act, s_done, ev(s, NU, u))
                    at_least(act, pv_done, ev(s, NU, u - 4))
                    nc.scalar.activation(pt[:, u % 4, 0:2 * w].rearrange("p (b c) -> p b c", b=2),
                                         S[:, u % 2, :, 0:w], ACT.Exp).then_inc(e_done, 1)

                def pv_copy(s, t):
                    at_least(act, pv_done, ev(s, NU, t_last[t]))
                    at_least(act, t_done, ev(s, NTAIL, N_AT[t - 2]) if t >= 2 else ev(s - 1, NTAIL, N_AT[t + 2]))
                    nc.scalar.copy(pvs[:, t % 2, :], PV[:]).then_inc(pv_out, 1)

                def tail_use(s, i):
                    kind, k = TAIL[i]
                    if kind != "C":
                        return
                    at_least(act, t_done, ev(s, NTAIL, i))
                    nc.scalar.copy(ctxT[:, k, :], TL[:]).then_inc(t_act, 1)

                def body(s, par, tail, core, front):
                    for u in range(NU):
                        if tail and u == 1:
                            pv_copy(s - 1, 3)
                        if front and u == LN_SLOT:
                            rsqrt_guess(s + 1)
                        if core:
                            exps(s, u)
                            for t in range(3):
                                if u == t_last[t] + 2:
                                    pv_copy(s, t)
                        for i in TAIL_AT.get(u, ()) if core else ():
                            tail_use(s, i)
                        for i in LATE_AT.get(u, ()) if tail else ():
                            tail_use(s - 1, i)
                        if front:
                            for i in slot_front[u]:
                                front_use(s + 1, 1 - par, i)

                iterations(act, body)

            @block.vector
            def _(dve):
                def layer_norm(s, par):
                    at_least(dve, x_loaded, 16 * (s + 1))
                    for b in range(TB):
                        nc.vector.bn_stats(stats[:, b, :], xin[:, par, b, :]).then_inc(ln_stat, 1)
                    m0, m1, q0, q1 = (stats[:, :, c] for c in (1, 4, 2, 5))
                    dve.wait_ge(ln_stat, ev(s, NSTAT, TB - 1))
                    nc.vector.tensor_tensor(mean[:], m0, m1, ALU.add).then_inc(ln_stat, 1)
                    nc.vector.tensor_tensor(yy[:], m0, m1, ALU.subtract).then_inc(ln_stat, 1)
                    nc.vector.tensor_tensor(var[:], q0, q1, ALU.add).then_inc(ln_stat, 1)
                    dve.wait_ge(ln_stat, ev(s, NSTAT, TB + 2))
                    nc.vector.tensor_scalar(mean[:], mean[:], 0.5, None, ALU.mult).then_inc(ln_stat, 1)
                    nc.vector.tensor_tensor(yy[:], yy[:], yy[:], ALU.mult).then_inc(ln_stat, 1)
                    nc.vector.tensor_scalar(var[:], var[:], 1.0 / H, EPS, ALU.mult, ALU.add).then_inc(ln_stat, 1)
                    dve.wait_ge(ln_stat, ev(s, NSTAT, TB + 5))
                    nc.vector.scalar_tensor_tensor(out=var[:], in0=yy[:], scalar=0.25, in1=var[:],
                                                   op0=ALU.mult, op1=ALU.add).then_inc(ln_var, 1)

                def normalise(s, par):
                    at_least(dve, ln_guess, ev(s, 1, 0))
                    nc.vector.tensor_tensor(yy[:], guess[:], guess[:], ALU.mult).then_inc(ln_stat, 1)
                    dve.wait_ge(ln_stat, ev(s, NSTAT, TB + 6))
                    nc.vector.tensor_tensor(yy[:], yy[:], var[:], ALU.mult).then_inc(ln_stat, 1)
                    dve.wait_ge(ln_stat, ev(s, NSTAT, TB + 7))
                    nc.vector.tensor_scalar(yy[:], yy[:], -0.5, 1.5, ALU.mult, ALU.add).then_inc(ln_stat, 1)
                    dve.wait_ge(ln_stat, ev(s, NSTAT, TB + 8))
                    nc.vector.tensor_tensor(rstd[:], guess[:], yy[:], ALU.mult).then_inc(ln_stat, 1)
                    dve.wait_ge(ln_stat, ev(s, NSTAT, TB + 9))
                    at_least(dve, f_done, ev(s - 1, NF, KT - 1))
                    for b in range(TB):
                        ins = nc.vector.tensor_scalar(xn[:, b, :], xin[:, par, b, :], mean[:, b:b + 1],
                                                      rstd[:, b:b + 1], ALU.subtract, ALU.mult)
                    ins.then_inc(ln_done, 1)

                def mask_q(s, par, t):
                    n = min(HT, HEADS - t * HT)
                    at_least(dve, f_act, ev(s, NFA, act_no[FRONT.index(("q", t))]))
                    at_least(dve, s_done, ev(s - 2, NU, NU - 1))
                    at_least(dve, f_done, ev(s - 1, NF, mt_at[1]))
                    for j in range(n):
                        nc.vector.tensor_scalar(qm[0:ONES, par, t * HT + j, :], qf[0:ONES, t, :],
                                                headmask[0:ONES, j:j + 1], None, ALU.mult)
                        ins = nc.vector.tensor_scalar(qb16[0:ONES, t * HT + j, :], qf[0:ONES, t, :],
                                                      headmask[0:ONES, j:j + 1], None, ALU.mult)
                    ins.then_inc(q_masked, 1)

                def half_k(s, par, t):
                    at_least(dve, f_act, ev(s, NFA, act_no[FRONT.index(("k", t))]))
                    at_least(dve, f_done, ev(s - 1, NF, mt_at[1]))
                    nc.vector.tensor_copy(kb16[0:ONES, t, :], kf[0:ONES, par, t, :]).then_inc(k_half, 1)

                def front_use(s, par, i):
                    kind, k = FRONT[i]
                    if kind == "q":
                        mask_q(s, par, k)
                    if kind == "k":
                        half_k(s, par, k)
                    if by_act[i]:
                        return
                    at_least(dve, f_done, ev(s, NF, i))
                    src = FB[:, i % 2, :]
                    if kind == "v":
                        at_least(dve, pv_done, ev(s - 2, NU, NU - 1))
                        for b in range(2):
                            ins = nc.vector.tensor_tensor(
                                vv[:, par, 2 * k + b, :, 0:DH],
                                src[:, b * H:(b + 1) * H].rearrange("p (h d) -> p h d", d=DH),
                                bv[:].rearrange("p (h d) -> p h d", d=DH), ALU.add)
                        ins.then_inc(f_dve, 1)
                    elif kind == "m":
                        heads, qb, _, n = k
                        nh = len(heads)
                        at_least(dve, f_done, ev(s - 1, NF, mt_at[1]))
                        nc.vector.tensor_reduce(mx[:, heads[0]:heads[0] + nh, qb],
                                                src[:, 0:nh * n].rearrange("p (h c) -> p h c", c=n),
                                                AX.X, ALU.max).then_inc(f_dve, 1)
                    else:
                        dst, n = (mTg, GLOBAL) if k == 0 else (mTl, HEADS - GLOBAL)
                        at_least(dve, m_row, 16 * (2 * (s - 1) + k + 1))
                        nc.vector.tensor_scalar(dst[:], src[0:n, :], -1.0, None, ALU.mult).then_inc(f_dve, 1)

                def tail_use(s, par, i):
                    kind, k = TAIL[i]
                    if kind == "C":
                        return
                    at_least(dve, t_done, ev(s, NTAIL, i))
                    if kind == "N":
                        v = TL[:].rearrange("p (b h c) -> p b h c", b=TB, h=4)
                        nc.vector.reciprocal(rden[:], v[:, :, :, DH]).then_inc(r_done, 1)
                        dve.wait_ge(r_done, ev(s, 4, k))
                        nc.vector.tensor_tensor(ctxn[:, :, 4 * k:4 * k + 4, :], v[:, :, :, 0:DH],
                                                rden[:].unsqueeze(3).to_broadcast([P, TB, 4, DH]),
                                                ALU.mult).then_inc(t_dve, 1)
                    else:
                        at_least(dve, res_ready, ev(s, 1, 0))
                        nc.vector.tensor_tensor(xres[:, par, 2 * k:2 * k + 2, :],
                                                TL[:].rearrange("p (b h) -> p b h", b=2),
                                                xres[:, par, 2 * k:2 * k + 2, :], ALU.add).then_inc(t_dve, 1)

                def body(s, par, tail, core, front):
                    for u in range(NU):
                        if front and u == LN_SLOT:
                            layer_norm(s + 1, 1 - par)
                        if front and u == LN_SLOT + 1:
                            normalise(s + 1, 1 - par)
                        for i in TAIL_AT.get(u, ()) if core else ():
                            tail_use(s, par, i)
                        for i in LATE_AT.get(u, ()) if tail else ():
                            tail_use(s - 1, 1 - par, i)
                        if front:
                            for i in slot_front[u]:
                                front_use(s + 1, 1 - par, i)

                iterations(dve, body)

            @block.tensor
            def _(pe):
                def front_use(s, par, i):
                    kind, k = FRONT[i]
                    dst = FB[:, i % 2, :]
                    j, sj = (i - 2, s) if i >= 2 else (i - 2 + NF, s - 1)
                    if by_act[j]:
                        at_least(pe, f_act, ev(sj, NFA, act_no[j]))
                    else:
                        at_least(pe, f_dve, ev(sj, NFD, dve_no[j]))
                    if kind == "T":
                        at_least(pe, ln_done, ev(s, 1, 0))
                        for b in range(TB):
                            ins = pe.transpose(dst[:, b * P:(b + 1) * P], xn[:, b, k * P:(k + 1) * P], ident[:])
                    elif kind in "qk":
                        at_least(pe, f_act, ev(s, NFA, KT - 1))
                        w, m = (wq, ONES) if kind == "q" else (wk, ONES + 1)
                        for c in range(KT):
                            ins = pe.matmul(dst[0:m, :], w[:, c, k, 0:m], xT[:, c, :], start=(c == 0), stop=(c == KT - 1))
                    elif kind == "v":
                        for b in range(2):
                            for c in range(KT):
                                ins = pe.matmul(dst[:, b * H:(b + 1) * H],
                                                xT[:, c, (2 * k + b) * P:(2 * k + b + 1) * P], wv[:, c, :],
                                                start=(c == 0), stop=(c == KT - 1))
                    elif kind == "m":
                        heads, qb, k0, n = k
                        at_least(pe, q_masked, ev(s, QT, heads[-1] // HT))
                        at_least(pe, k_half, ev(s, QT, heads[-1] // HT))
                        for j, h in enumerate(heads):
                            o = dst[:, j * n:(j + 1) * n]
                            pe.matmul(o, qb16[0:ONES, h, qb * P:(qb + 1) * P], kb16[0:ONES, h // HT, k0:k0 + n],
                                      start=True, stop=(h < GLOBAL))
                            if h < GLOBAL:
                                ins = pe.matmul(o[:, n - P:n], identb[:], mask_g[:], start=False, stop=True,
                                                skip_group_check=True)
                            else:
                                ins = pe.matmul(o, identb[:], mask_l[:, BAND - n:BAND], start=False, stop=True)
                    else:
                        h0, h1 = (0, GLOBAL) if k == 0 else (GLOBAL, HEADS)
                        at_least(pe, f_dve, ev(s, NFD, dve_no[i] - 1))
                        for b in range(TB):
                            ins = pe.transpose(dst[0:h1 - h0, b * P:(b + 1) * P], mx[:, h0:h1, b], ident[:])
                    ins.then_inc(f_done, 1)

                def scores(s, par, u):
                    t, kb, heads, n = UNITS[u]
                    if u >= 2:
                        at_least(pe, e_done, ev(s, NU, u - 2))
                    else:
                        at_least(pe, e_done, ev(s - 1, NU, NU + u - 2))
                    at_least(pe, m_row, 16 * (2 * s + (1 if heads[0] < GLOBAL else 2)))
                    per = len(heads) // 2
                    for j, h in enumerate(heads):
                        ins = pe.matmul(S[:, u % 2, j // per, (j % per) * n:(j % per + 1) * n],
                                        kf[0:ONES + 1, par, h // HT, kb * P:(kb + 1) * P],
                                        qm[0:ONES + 1, par, h, kb * P:kb * P + n], start=True, stop=True)
                    ins.then_inc(s_done, 1)

                def context(s, par, u):
                    t, kb, heads, n = UNITS[u]
                    at_least(pe, p_done, ev(s, NU, u))
                    if u == t_first[t]:
                        at_least(pe, pv_out, ev(s, 4, t - 1) if t else ev(s - 1, 4, 3))
                    at_least(pe, f_dve, ev(s, NFD, dve_no[first["v"] + 1]))
                    for j, h in enumerate(heads):
                        r = VW * (h % 4)
                        ins = pe.matmul(PV[r:r + VW, kb * P:kb * P + n], vv[:, par, kb, h, :],
                                        pt[:, u % 4, j * n:(j + 1) * n], start=(kb == 0), stop=(kb == TB - 1),
                                        skip_group_check=True)
                    ins.then_inc(pv_done, 1)

                def tail_use(s, i):
                    kind, k = TAIL[i]
                    j, sj = (i - 1, s) if i else (NTAIL - 1, s - 1)
                    if TAIL[j][0] == "C":
                        at_least(pe, t_act, ev(sj, NTA, TAIL[j][1]))
                    else:
                        at_least(pe, t_dve, ev(sj, NTD, j - t_act_no[j]))
                    if kind == "N":
                        at_least(pe, pv_out, ev(s, 4, k))
                        for b in range(TB):
                            ins = pe.transpose(TL[:, b * P:(b + 1) * P], pvs[:, k % 2, b * P:(b + 1) * P], ident[:])
                    elif kind == "C":
                        cn = ctxn[:].rearrange("p b h d -> p b (h d)")
                        at_least(pe, t_dve, ev(s, NTD, 2 * k + 1))
                        for b in range(TB):
                            ins = pe.transpose(TL[:, b * P:(b + 1) * P], cn[:, b, k * P:(k + 1) * P], ident[:])
                    else:
                        at_least(pe, t_act, ev(s, NTA, 1))
                        for b in range(2):
                            for c in range(KT):
                                ins = pe.matmul(TL[:, b * H:(b + 1) * H], ctxT[:, c, (2 * k + b) * P:(2 * k + b + 1) * P],
                                                wo[:, c, :], start=(c == 0), stop=(c == KT - 1))
                    ins.then_inc(t_done, 1)

                def body(s, par, tail, core, front):
                    for u in range(NU):
                        if core:
                            scores(s, par, u)
                        if tail and u < 2:
                            context(s - 1, 1 - par, NU - 2 + u)
                        if core and u >= 2:
                            context(s, par, u - 2)
                        for i in TAIL_AT.get(u, ()) if core else ():
                            tail_use(s, i)
                        for i in LATE_AT.get(u, ()) if tail else ():
                            tail_use(s - 1, i)
                        if front:
                            for i in slot_front[u]:
                                front_use(s + 1, 1 - par, i)

                iterations(pe, body)


F32R = mybir.dt.float32r

EXPERTS, GROUPS, TOP_GROUPS, TOP_K, SCALE = 16, 4, 2, 4, 2.5
NE = EXPERTS + 2
PER_GROUP = EXPERTS // GROUPS
LO_ROW = 32


def phase_f(nc, tag, x_in, x_out, w_gate, bias_corr, w1, w2, nseq):
    with ExitStack() as ctx:
        def sb(name, shape, dt=F32):
            return ctx.enter_context(nc.sbuf_tensor(tag + name, shape, dt))

        def ps(name, shape):
            return ctx.enter_context(nc.psum_tensor(tag + name, shape, F32))

        def sem(name):
            return ctx.enter_context(nc.semaphore(tag + name))

        ident = sb("ident", [P, P])
        raw = sb("raw", [P, 2, 1152])
        w1h, w1l = sb("w1h", [P, KT, NE * P], F32R), sb("w1l", [P, KT, NE * P], F32R)
        w2h, w2l = sb("w2h", [P, NE * H], F32R), sb("w2l", [P, NE * H], F32R)
        graw = sb("graw", [P, KT, EXPERTS])
        wgh, wgl = sb("wgh", [P, KT, EXPERTS], F32R), sb("wgl", [P, KT, EXPERTS], F32R)
        bias = sb("bias", [P, EXPERTS])
        spread0 = sb("spread0", [P, EXPERTS, P])
        spread = sb("spread", [P, EXPERTS, P], F32R)
        tri = sb("tri", [P, EXPERTS, EXPERTS])
        xin, xres = sb("xin", [P, 2, TB, H]), sb("xres", [P, 2, TB, H])
        stats, mean, var = sb("stats", [P, TB, 6]), sb("mean", [P, TB]), sb("var", [P, TB])
        lnv, guess, yy, rstd = sb("lnv", [P, TB]), sb("guess", [P, TB]), sb("yy", [P, TB]), sb("rstd", [P, TB])
        xn = sb("xn", [P, TB, H])
        xh, xl = sb("xh", [P, 2, KT, SEQ], F32R), sb("xl", [P, 2, KT, SEQ], F32R)
        logT = sb("logT", [P, SEQ])
        sc = sb("sc", [P, TB, EXPERTS])
        choice = sb("choice", [P, TB, EXPERTS])
        pair_hi, pair_lo = sb("pair_hi", [P, TB * GROUPS, 2]), sb("pair_lo", [P, TB * GROUPS, 2])
        g1, g2, g3 = sb("g1", [P, TB * GROUPS]), sb("g2", [P, TB * GROUPS]), sb("g3", [P, TB * GROUPS])
        gcmp, geq = sb("gcmp", [P, TB * GROUPS, GROUPS]), sb("geq", [P, TB * GROUPS, GROUPS])
        gsel = sb("gsel", [P, TB * GROUPS])
        cmp_, eq = sb("cmp", [P, TB * EXPERTS, EXPERTS]), sb("eq", [P, TB * EXPERTS, EXPERTS])
        rank = sb("rank", [P, TB, EXPERTS])
        wsum, winv = sb("wsum", [P, TB]), sb("winv", [P, TB])
        cw = sb("cw", [P, TB, EXPERTS])
        cT0 = sb("cT0", [P, SEQ])
        cT = sb("cT", [P, 2, SEQ], F32R)
        r = sb("r", [P, 2, SEQ])
        u = sb("u", [P, 2, SEQ])
        g = sb("g", [P, 2, SEQ])
        gh, gl = sb("gh", [P, 3, SEQ], F32R), sb("gl", [P, 3, SEQ], F32R)
        yT = sb("yT", [P, KT, SEQ])

        Z = ps("Z", [P, 2, 512])
        B = ps("B", [P, 2, 512])
        Y = ps("Y", [P, KT, 512])
        FB = ps("FB", [P, 2, 512])

        names = ("w_loaded w_split const dconst x_loaded res_ready ln_stat ln_var ln_log ln_guess ln_done t_done "
                 "xh_done xl_done l_done lT_done lt_done ex_done route cw_done ct_done ch_done cl_done z_done "
                 "r_done b_done u_done g_done gh_done gl_done y_done ye_done fin_done out_done x_stored a_split").split()
        (w_loaded, w_split, const, dconst, x_loaded, res_ready, ln_stat, ln_var, ln_log, ln_guess, ln_done, t_done,
         xh_done, xl_done, l_done, lT_done, lt_done, ex_done, route, cw_done, ct_done, ch_done, cl_done, z_done,
         r_done, b_done, u_done, g_done, gh_done, gl_done, y_done, ye_done, fin_done, out_done, x_stored,
         a_split) = [sem(n) for n in names]

        NSTAT, NROUTE = TB + 10, 24
        RES_SLOT = 8
        STAT_SLOT, LN_SLOT, FIN_SLOT, T_SLOT, L_SLOT, LT_SLOT, ROUTE_SLOT, CT_SLOT = 0, 1, 3, 5, 7, 8, 9, 16

        CH = 1152
        pieces = ([(w1h, w1l, k, c) for k in range(KT) for c in range(0, NE * P, CH)] +
                  [(w2h, w2l, None, c) for c in range(0, NE * H, CH)])

        def piece(t, k, c):
            return t[:, c:c + CH] if k is None else t[:, k, c:c + CH]

        with nc.Block() as block:
            @block.sync
            def _(sp):
                for i, (_, _, k, c) in enumerate(pieces):
                    at_least(sp, w_split, i - 1)
                    at_least(sp, w_loaded, 16 * i)
                    src = w2[:, c:c + CH] if k is None else w1[k * P:(k + 1) * P, c:c + CH]
                    sp.dma_start(raw[:, i % 2], src).then_inc(w_loaded, 16)
                sp.wait_ge(w_loaded, 16 * len(pieces))
                sp.dma_start(graw[:], w_gate.rearrange("(k p) e -> p k e", p=P)).then_inc(w_loaded, 16)
                sp.dma_start(bias[:], row_broadcast(bias_corr)).then_inc(w_loaded, 16)
                sp.wait_ge(w_loaded, 16 * (len(pieces) + 2))

            @block.scalar
            def _(act):
                for i, (hi, _, k, c) in enumerate(pieces):
                    act.wait_ge(w_loaded, 16 * (i + 1))
                    nc.scalar.copy(piece(hi, k, c), raw[:, i % 2]).then_inc(a_split, 1)
                act.wait_ge(w_loaded, 16 * (len(pieces) + 2))
                nc.scalar.copy(wgh[:], graw[:]).then_inc(a_split, 1)
                act.wait_ge(const, 6)
                nc.scalar.copy(spread[:], spread0[:]).then_inc(a_split, 1)

            @block.vector
            def _(dve):
                nc.vector.memset(logT[:], 0.0)
                nc.vector.memset(cT0[:], 0.0).then_inc(dconst, 1)
                for i, (hi, lo, k, c) in enumerate(pieces):
                    dve.wait_ge(a_split, i + 1)
                    nc.vector.tensor_tensor(piece(lo, k, c), raw[:, i % 2], piece(hi, k, c).bitcast(F32),
                                            ALU.subtract).then_inc(w_split, 1)
                dve.wait_ge(a_split, len(pieces) + 1)
                nc.vector.tensor_tensor(wgl[:], graw[:], wgh[:].bitcast(F32), ALU.subtract).then_inc(w_split, 1)
                dve.wait_ge(dconst, 1)
                for par in range(2):
                    nc.vector.tensor_copy(cT[:, par], cT0[:]).then_inc(dconst, 1)

            @block.gpsimd
            def _(pool):
                nc.gpsimd.memset(ident[:], 0.0).then_inc(const, 1)
                nc.gpsimd.memset(spread0[:], 0.0).then_inc(const, 1)
                nc.gpsimd.memset(tri[:], 1.0).then_inc(const, 1)
                pool.wait_ge(const, 3)
                nc.gpsimd.affine_select(out=ident[:], in_=ident[:], compare_op=ALU.not_equal, fill=1.0,
                                        base=0, pattern=[[-1, P]], channel_multiplier=1).then_inc(const, 1)
                nc.gpsimd.affine_select(out=spread0[:], in_=spread0[:], compare_op=ALU.not_equal, fill=1.0,
                                        base=0, pattern=[[-1, EXPERTS], [0, P]], channel_multiplier=1
                                        ).then_inc(const, 1)
                pool.wait_ge(const, 5)
                nc.gpsimd.affine_select(out=spread0[:], in_=spread0[:], compare_op=ALU.not_equal, fill=1.0,
                                        base=-LO_ROW, pattern=[[-1, EXPERTS], [0, P]], channel_multiplier=1
                                        ).then_inc(const, 1)
                nc.gpsimd.affine_select(out=tri[:], in_=tri[:], compare_op=ALU.is_gt, fill=0.0,
                                        base=0, pattern=[[1, EXPERTS], [-1, EXPERTS]], channel_multiplier=0
                                        ).then_inc(const, 1)
                pool.wait_ge(const, 7)

        with nc.Block() as block:
            def iterations(eng, body):
                body(-1, 1, False, False, True)
                body(0, 0, False, True, True)
                with eng.Fori(1, nseq - 3, 2) as reg:
                    body(reg, 1, True, True, True)
                    body(reg + 1, 0, True, True, True)
                body(nseq - 3, 1, True, True, True)
                body(nseq - 2, 0, True, True, True)
                body(nseq - 1, 1, True, True, False)
                body(nseq, 0, True, False, False)

            @block.sync
            def _(sp):
                def load(s, par):
                    rows = seq_rows(sp, x_in, s)
                    need = [in_register(sp, v) for v in (ev(s - 2, 1, 0), ev(s - 2, 1, 0), 16 * s,)]
                    at_least(sp, ln_done, need[0])
                    at_least(sp, res_ready, need[1])
                    at_least(sp, x_loaded, need[2])
                    sp.dma_start(xin[:, par], rows).then_inc(x_loaded, 16)

                def body(s, par, end, core, front):
                    if end:
                        rows = seq_rows(sp, x_out, s - 1)
                        summed, stored = in_register(sp, ev(s - 1, 2, 1)), in_register(sp, 16 * s)
                        at_least(sp, out_done, summed)
                        sp.dma_start(rows, xres[:, 1 - par]).then_inc(x_stored, 16)
                        at_least(sp, x_stored, stored)
                    if isinstance(s, int) and s == -1:
                        load(0, 0)
                        load(1, 1)
                    elif not isinstance(s, int) or s + 2 < nseq:
                        load(s + 2, par)

                iterations(sp, body)
                sp.wait_ge(x_stored, 16 * nseq)

            @block.gpsimd
            def _(pool):
                def gate(s, e):
                    at_least(pool, r_done, ev(s, NE, e))
                    if e < EXPERTS:
                        at_least(pool, u_done, ev(s, EXPERTS, e))
                    at_least(pool, gl_done, ev(s, NE, e - 2))
                    a = u if e < EXPERTS else r
                    nc.gpsimd.tensor_tensor(g[:, e % 2], a[:, e % 2], r[:, e % 2], ALU.mult).then_inc(g_done, 1)

                def body(s, par, end, core, front):
                    for e in range(NE):
                        if core:
                            gate(s, e)

                iterations(pool, body)

            @block.scalar
            def _(act):
                def body(s, par, end, core, front):
                    for e in range(NE):
                        if end and e == 2:
                            at_least(act, y_done, ev(s - 1, NE, NE - 1))
                            for k in range(KT):
                                ins = nc.scalar.copy(yT[:, k], Y[:, k])
                            ins.then_inc(ye_done, 1)
                        if core:
                            at_least(act, z_done, ev(s, NE, e))
                            at_least(act, g_done, ev(s, NE, e - 2))
                            nc.scalar.activation(r[:, e % 2], Z[:, e % 2], ACT.Relu).then_inc(r_done, 1)
                        if end and e == 0:
                            high(s - 1, NE - 1)
                        if core and e >= 1:
                            high(s, e - 1)
                        if not front:
                            continue
                        n, np_ = s + 1, 1 - par
                        if e == LN_SLOT:
                            at_least(act, ln_var, ev(n, 1, 0))
                            nc.scalar.activation(lnv[:], var[:], ACT.Ln).then_inc(ln_log, 1)
                        if e == LN_SLOT + 1:
                            at_least(act, ln_log, ev(n, 1, 0))
                            nc.scalar.activation(guess[:], lnv[:], ACT.Exp, scale=-0.5).then_inc(ln_guess, 1)
                        if e == RES_SLOT:
                            at_least(act, x_loaded, 16 * (n + 1))
                            at_least(act, x_stored, 16 * (n - 1))
                            nc.scalar.copy(xres[:, np_], xin[:, np_]).then_inc(res_ready, 1)
                        if e in (T_SLOT, T_SLOT + 1):
                            k = e - T_SLOT
                            at_least(act, t_done, ev(n, KT, k))
                            at_least(act, z_done, ev(n - 2, NE, NE - 1))
                            nc.scalar.copy(xh[:, np_, k], FB[:, k]).then_inc(xh_done, 1)
                        if e == L_SLOT:
                            at_least(act, l_done, ev(n, 1, 0))
                            nc.scalar.copy(logT[0:EXPERTS], FB[0:EXPERTS, 0]).then_inc(lT_done, 1)
                        if e == LT_SLOT:
                            at_least(act, lt_done, ev(n, 1, 0))
                            nc.scalar.activation(sc[:], FB[:, 1].rearrange("p (b e) -> p b e", b=TB)[:, :, 0:EXPERTS],
                                                 ACT.Exp, scale=-1.0).then_inc(ex_done, 1)
                        if e == CT_SLOT:
                            at_least(act, ct_done, ev(n, 1, 0))
                            at_least(act, b_done, ev(n - 2, EXPERTS, EXPERTS - 1))
                            nc.scalar.copy(cT[0:EXPERTS, np_], FB[0:EXPERTS, 0]).then_inc(ch_done, 1)

                def high(s, e):
                    at_least(act, g_done, ev(s, NE, e))
                    at_least(act, y_done, ev(s, NE, e - 3))
                    nc.scalar.copy(gh[:, e % 3], g[:, e % 2]).then_inc(gh_done, 1)

                iterations(act, body)

            @block.vector
            def _(dve):
                def low(s, e):
                    at_least(dve, gh_done, ev(s, NE, e))
                    nc.vector.tensor_tensor(gl[:, e % 3], g[:, e % 2], gh[:, e % 3].bitcast(F32),
                                            ALU.subtract).then_inc(gl_done, 1)

                def statistics(s, par):
                    at_least(dve, x_loaded, 16 * (s + 1))
                    for b in range(TB):
                        nc.vector.bn_stats(stats[:, b, :], xin[:, par, b, :]).then_inc(ln_stat, 1)

                def variance(s):
                    m0, m1, q0, q1 = (stats[:, :, c] for c in (1, 4, 2, 5))
                    dve.wait_ge(ln_stat, ev(s, NSTAT, TB - 1))
                    nc.vector.tensor_tensor(mean[:], m0, m1, ALU.add).then_inc(ln_stat, 1)
                    nc.vector.tensor_tensor(yy[:], m0, m1, ALU.subtract).then_inc(ln_stat, 1)
                    nc.vector.tensor_tensor(var[:], q0, q1, ALU.add).then_inc(ln_stat, 1)
                    dve.wait_ge(ln_stat, ev(s, NSTAT, TB + 2))
                    nc.vector.tensor_scalar(mean[:], mean[:], 0.5, None, ALU.mult).then_inc(ln_stat, 1)
                    nc.vector.tensor_tensor(yy[:], yy[:], yy[:], ALU.mult).then_inc(ln_stat, 1)
                    nc.vector.tensor_scalar(var[:], var[:], 1.0 / H, EPS, ALU.mult, ALU.add).then_inc(ln_stat, 1)
                    dve.wait_ge(ln_stat, ev(s, NSTAT, TB + 5))
                    nc.vector.scalar_tensor_tensor(out=var[:], in0=yy[:], scalar=0.25, in1=var[:],
                                                   op0=ALU.mult, op1=ALU.add).then_inc(ln_var, 1)

                def inverse_deviation(s):
                    at_least(dve, ln_guess, ev(s, 1, 0))
                    nc.vector.tensor_tensor(yy[:], guess[:], guess[:], ALU.mult).then_inc(ln_stat, 1)
                    dve.wait_ge(ln_stat, ev(s, NSTAT, TB + 6))
                    nc.vector.tensor_tensor(yy[:], yy[:], var[:], ALU.mult).then_inc(ln_stat, 1)
                    dve.wait_ge(ln_stat, ev(s, NSTAT, TB + 7))
                    nc.vector.tensor_scalar(yy[:], yy[:], -0.5, 1.5, ALU.mult, ALU.add).then_inc(ln_stat, 1)
                    dve.wait_ge(ln_stat, ev(s, NSTAT, TB + 8))
                    nc.vector.tensor_tensor(rstd[:], guess[:], yy[:], ALU.mult).then_inc(ln_stat, 1)

                def normalise(s, par):
                    dve.wait_ge(ln_stat, ev(s, NSTAT, TB + 9))
                    at_least(dve, t_done, ev(s - 1, KT, KT - 1))
                    for b in range(TB):
                        ins = nc.vector.tensor_scalar(xn[:, b, :], xin[:, par, b, :], mean[:, b:b + 1],
                                                      rstd[:, b:b + 1], ALU.subtract, ALU.mult)
                    ins.then_inc(ln_done, 1)

                def routing(s, part):
                    n = [0, 9, 15, 16, 17, 18, 20][part]

                    def step(ins):
                        nonlocal n
                        ins.then_inc(route, 1)
                        n += 1

                    def seen():
                        dve.wait_ge(route, ev(s, NROUTE, n - 1))

                    bg = "p (b g) -> p b g"
                    if part == 0:
                        at_least(dve, ex_done, ev(s, 1, 0))
                        step(nc.vector.tensor_scalar(sc[:], sc[:], 1.0, None, ALU.add))
                        seen()
                        step(nc.vector.reciprocal(sc[:], sc[:]))
                        seen()
                        step(nc.vector.tensor_tensor(choice[:], sc[:], bias[:].unsqueeze(1).to_broadcast([P, TB, EXPERTS]),
                                                     ALU.add))
                        v = choice[:].rearrange("p b (g q t) -> p (b g) q t", g=GROUPS, t=2)
                        seen()
                        step(nc.vector.tensor_tensor(pair_hi[:], v[:, :, :, 0], v[:, :, :, 1], ALU.max))
                        step(nc.vector.tensor_tensor(pair_lo[:], v[:, :, :, 0], v[:, :, :, 1], ALU.min))
                        seen()
                        step(nc.vector.tensor_tensor(g1[:], pair_hi[:, :, 0], pair_hi[:, :, 1], ALU.max))
                        step(nc.vector.tensor_tensor(g2[:], pair_hi[:, :, 0], pair_hi[:, :, 1], ALU.min))
                        step(nc.vector.tensor_tensor(g3[:], pair_lo[:, :, 0], pair_lo[:, :, 1], ALU.max))
                        seen()
                        step(nc.vector.tensor_tensor(g2[:], g2[:], g3[:], ALU.max))
                        assert n == 9
                    if part == 1:
                        seen()
                        step(nc.vector.tensor_tensor(g1[:], g1[:], g2[:], ALU.add))
                        seen()
                        mine = g1[:].unsqueeze(2).to_broadcast([P, TB * GROUPS, GROUPS])
                        for b in range(TB):
                            other = g1[:, b * GROUPS:(b + 1) * GROUPS].unsqueeze(1).to_broadcast([P, GROUPS, GROUPS])
                            w = slice(b * GROUPS, (b + 1) * GROUPS)
                            nc.vector.tensor_tensor(gcmp[:, w], other, mine[:, w], ALU.is_gt)
                            i2 = nc.vector.tensor_tensor(geq[:, w], other, mine[:, w], ALU.is_equal)
                        step(i2)
                        seen()
                        t4 = tri[:, 0:GROUPS, 0:GROUPS].unsqueeze(1).to_broadcast([P, TB, GROUPS, GROUPS])
                        step(nc.vector.tensor_tensor(geq[:].rearrange("p (b g) f -> p b g f", b=TB),
                                                     geq[:].rearrange("p (b g) f -> p b g f", b=TB), t4, ALU.mult))
                        seen()
                        step(nc.vector.tensor_tensor(gcmp[:], gcmp[:], geq[:], ALU.add))
                        seen()
                        step(nc.vector.tensor_reduce(gsel[:], gcmp[:], AX.X, ALU.add))
                        seen()
                        step(nc.vector.tensor_scalar(gsel[:], gsel[:], TOP_GROUPS - 0.5, None, ALU.is_lt))
                        assert n == 15
                    if part == 2:
                        seen()
                        v = choice[:].rearrange("p b (g q) -> p (b g) q", g=GROUPS)
                        step(nc.vector.tensor_tensor(v, v, gsel[:].unsqueeze(2).to_broadcast([P, TB * GROUPS, PER_GROUP]),
                                                     ALU.mult))
                    if part in (2, 3):
                        if part == 2:
                            seen()
                        for b in range(2 * (part - 2), 2 * (part - 1)):
                            w = slice(b * EXPERTS, (b + 1) * EXPERTS)
                            other = choice[:, b].unsqueeze(1).to_broadcast([P, EXPERTS, EXPERTS])
                            mine = choice[:, b].unsqueeze(2).to_broadcast([P, EXPERTS, EXPERTS])
                            nc.vector.tensor_tensor(cmp_[:, w], other, mine, ALU.is_gt)
                            i2 = nc.vector.tensor_tensor(eq[:, w], other, mine, ALU.is_equal)
                        if part == 3:
                            step(i2)
                    if part == 4:
                        seen()
                        t4 = tri[:].unsqueeze(1).to_broadcast([P, TB, EXPERTS, EXPERTS])
                        e4 = eq[:].rearrange("p (b g) f -> p b g f", b=TB)
                        step(nc.vector.tensor_tensor(e4, e4, t4, ALU.mult))
                    if part == 5:
                        seen()
                        step(nc.vector.tensor_tensor(cmp_[:], cmp_[:], eq[:], ALU.add))
                        seen()
                        step(nc.vector.tensor_reduce(rank[:].rearrange("p b e -> p (b e)"), cmp_[:], AX.X, ALU.add))
                        assert n == 20
                    if part == 6:
                        seen()
                        step(nc.vector.scalar_tensor_tensor(out=rank[:], in0=rank[:], scalar=TOP_K - 0.5, in1=sc[:],
                                                            op0=ALU.is_lt, op1=ALU.mult))
                        seen()
                        step(nc.vector.tensor_reduce(wsum[:], rank[:], AX.X, ALU.add))
                        seen()
                        step(nc.vector.tensor_scalar(wsum[:], wsum[:], 1e-20, None, ALU.add))
                        seen()
                        step(nc.vector.reciprocal(winv[:], wsum[:]))
                        seen()
                        assert n == NROUTE
                        nc.vector.scalar_tensor_tensor(out=cw[:], in0=rank[:], scalar=SCALE,
                                                       in1=winv[:].unsqueeze(2).to_broadcast([P, TB, EXPERTS]),
                                                       op0=ALU.mult, op1=ALU.mult).then_inc(cw_done, 1)

                def body(s, par, end, core, front):
                    n, np_ = s + 1, 1 - par
                    for e in range(NE):
                        if core and e < EXPERTS:
                            at_least(dve, r_done, ev(s, NE, e))
                            at_least(dve, b_done, ev(s, EXPERTS, e))
                            nc.vector.tensor_tensor(u[:, e % 2], r[:, e % 2], B[:, e % 2], ALU.mult).then_inc(u_done, 1)
                        if end and e == 0:
                            low(s - 1, NE - 1)
                        if core and e >= 1:
                            low(s, e - 1)
                        if end and e in (FIN_SLOT, FIN_SLOT + 1):
                            k = e - FIN_SLOT
                            at_least(dve, fin_done, ev(s - 1, 2, k))
                            at_least(dve, res_ready, ev(s - 1, 1, 0))
                            xr = xres[:, np_, 2 * k:2 * k + 2, :]
                            nc.vector.tensor_tensor(xr, FB[:, k].rearrange("p (b h) -> p b h", b=2), xr,
                                                    ALU.add).then_inc(out_done, 1)
                        if not front:
                            continue
                        if e == STAT_SLOT:
                            statistics(n, np_)
                        if e == STAT_SLOT + 1:
                            variance(n)
                        if e == LN_SLOT + 2:
                            inverse_deviation(n)
                        if e == LN_SLOT + 3:
                            normalise(n, np_)
                        if e in (T_SLOT, T_SLOT + 1):
                            k = e - T_SLOT
                            at_least(dve, xh_done, ev(n, KT, k))
                            nc.vector.tensor_tensor(xl[:, np_, k], FB[:, k], xh[:, np_, k].bitcast(F32),
                                                    ALU.subtract).then_inc(xl_done, 1)
                        if ROUTE_SLOT <= e < ROUTE_SLOT + 7:
                            routing(n, e - ROUTE_SLOT)
                        if e == CT_SLOT:
                            at_least(dve, ch_done, ev(n, 1, 0))
                            nc.vector.tensor_tensor(cT[LO_ROW:LO_ROW + EXPERTS, np_], FB[0:EXPERTS, 0],
                                                    cT[0:EXPERTS, np_].bitcast(F32), ALU.subtract).then_inc(cl_done, 1)

                iterations(dve, body)

            @block.tensor
            def _(pe):
                def three(out, wh, wl, vh, vl, first, last):
                    pe.matmul(out, wl, vh, start=first, stop=False)
                    pe.matmul(out, wh, vl, start=False, stop=False)
                    return pe.matmul(out, wh, vh, start=False, stop=last)

                def hidden(s, par, e):
                    at_least(pe, r_done, ev(s, NE, e - 2))
                    if e == 0:
                        at_least(pe, xl_done, ev(s, KT, KT - 1))
                    c = slice(e * P, (e + 1) * P)
                    for k in range(KT):
                        ins = three(Z[:, e % 2], w1h[:, k, c], w1l[:, k, c], xh[:, par, k], xl[:, par, k],
                                    k == 0, k == KT - 1)
                    ins.then_inc(z_done, 1)
                    if e < EXPERTS:
                        at_least(pe, u_done, ev(s, EXPERTS, e - 2))
                        if e == 0:
                            at_least(pe, cl_done, ev(s, 1, 0))
                        pe.matmul(B[:, e % 2], spread[:, e], cT[:, par], start=True, stop=True).then_inc(b_done, 1)

                def out_(s, e):
                    at_least(pe, gl_done, ev(s, NE, e))
                    if e == 0:
                        at_least(pe, ye_done, ev(s - 1, 1, 0))
                    for k in range(KT):
                        c = slice(e * H + k * P, e * H + (k + 1) * P)
                        ins = three(Y[:, k], w2h[:, c], w2l[:, c], gh[:, e % 3], gl[:, e % 3], e == 0, e == NE - 1)
                    ins.then_inc(y_done, 1)

                def body(s, par, end, core, front):
                    n, np_ = s + 1, 1 - par
                    for e in range(NE):
                        if core:
                            hidden(s, par, e)
                        if end and e < 2:
                            out_(s - 1, NE - 2 + e)
                        if core and e >= 2:
                            out_(s, e - 2)
                        if end and e in (FIN_SLOT, FIN_SLOT + 1):
                            k = e - FIN_SLOT
                            at_least(pe, ye_done, ev(s - 1, 1, 0))
                            if k == 0:
                                at_least(pe, cl_done, ev(s, 1, 0) if core else ev(s - 1, 1, 0))
                            else:
                                at_least(pe, ex_done, ev(s, 1, 0) if core else ev(s - 1, 1, 0))
                            for b in range(2):
                                for c in range(KT):
                                    ins = pe.transpose(FB[:, k, b * H + c * P:b * H + (c + 1) * P],
                                                       yT[:, c, (2 * k + b) * P:(2 * k + b + 1) * P], ident[:])
                            ins.then_inc(fin_done, 1)
                        if not front:
                            continue
                        if e in (T_SLOT, T_SLOT + 1):
                            k = e - T_SLOT
                            at_least(pe, ln_done, ev(n, 1, 0))
                            if end:
                                at_least(pe, out_done, ev(s - 1, 2, k))
                            elif not isinstance(s, int) or s >= 0:
                                at_least(pe, cl_done, ev(s, 1, 0))
                            for b in range(TB):
                                ins = pe.transpose(FB[:, k, b * P:(b + 1) * P], xn[:, b, k * P:(k + 1) * P], ident[:])
                            ins.then_inc(t_done, 1)
                        if e == L_SLOT:
                            at_least(pe, xl_done, ev(n, KT, KT - 1))
                            for k in range(KT):
                                ins = three(FB[0:EXPERTS, 0], wgh[:, k], wgl[:, k], xh[:, np_, k], xl[:, np_, k],
                                            k == 0, k == KT - 1)
                            ins.then_inc(l_done, 1)
                        if e == LT_SLOT:
                            at_least(pe, lT_done, ev(n, 1, 0))
                            for b in range(TB):
                                ins = pe.transpose(FB[:, 1, b * P:(b + 1) * P], logT[:, b * P:(b + 1) * P], ident[:])
                            ins.then_inc(lt_done, 1)
                        if e == CT_SLOT:
                            at_least(pe, cw_done, ev(n, 1, 0))
                            for b in range(TB):
                                ins = pe.transpose(FB[0:EXPERTS, 0, b * P:(b + 1) * P], cw[:, b, :], ident[:])
                            ins.then_inc(ct_done, 1)

                iterations(pe, body)


D = 512
DT = D // P
NC = SEQ // P


def phase_b(nc, x_in, x_out, w_in, b_q, b_k, b_v, b_g, w_o, b_o, nseq):
    NP = 4 * DT
    FRONT = [("T", 0), ("T", 1)] + [(c, i) for c in "qkvg" for i in range(DT)]
    NF = len(FRONT)
    FRONT_AT = {2: [0], 3: [1], **{4 + i: [2 + i] for i in range(NP)}}
    NSLOT = 4 + NP
    by_act = [c in "qkg" for c, _ in FRONT]
    act_no = [sum(by_act[:i]) for i in range(NF)]
    dve_no = [i - act_no[i] for i in range(NF)]
    NFA, NFD = sum(by_act), NF - sum(by_act)
    STAT_SLOT = 7
    D_SLOT, O_SLOT, PT_SLOT, PV_SLOT, W_SLOT, FIN_SLOT = 0, 1, 4, 5, 7, 13
    OFF = [P * (NC - 1 - kb) for kb in range(NC - 1)]
    START = [0, NC * P, NC * P + (NC - 1) * P, NC * P + (2 * NC - 3) * P]

    with ExitStack() as ctx:
        def sb(name, shape, dt=F32):
            return ctx.enter_context(nc.sbuf_tensor("b_" + name, shape, dt))

        def ps(name, shape):
            return ctx.enter_context(nc.psum_tensor("b_" + name, shape, F32))

        def sem(name):
            return ctx.enter_context(nc.semaphore("b_" + name))

        ident, maskc = sb("ident", [P, P]), sb("maskc", [P, P])
        raw = sb("raw", [P, 2, 1024])
        wh, wl = sb("wh", [P, KT, 4 * D], F32R), sb("wl", [P, KT, 4 * D], F32R)
        woh, wol = sb("woh", [P, DT * H], F32R), sb("wol", [P, DT * H], F32R)
        bq, bk, bg = sb("bq", [P, DT]), sb("bk", [P, DT]), sb("bg", [P, DT])
        bv, bo = sb("bv", [P, D]), sb("bo", [P, H])
        xin, xres = sb("xin", [P, 2, TB, H]), sb("xres", [P, 2, TB, H])
        stats, mean, var = sb("stats", [P, TB, 6]), sb("mean", [P, TB]), sb("var", [P, TB])
        lnv, guess, yy, rstd = sb("lnv", [P, TB]), sb("guess", [P, TB]), sb("yy", [P, TB]), sb("rstd", [P, TB])
        xn = sb("xn", [P, TB, H])
        xh, xl = sb("xh", [P, KT, SEQ], F32R), sb("xl", [P, KT, SEQ], F32R)
        qT, kT = sb("qT", [P, 2, DT, SEQ]), sb("kT", [P, 2, DT, SEQ])
        v = sb("v", [P, 2, TB, D])
        gate = sb("gate", [P, 2, DT, SEQ])
        sm = sb("sm", [P, NC, P])
        nmax, rsum, rinv = sb("nmax", [P, NC]), sb("rsum", [P, NC]), sb("rinv", [P, NC])
        st = sb("st", [P, START[-1] + P])
        o = sb("o", [P, 2, SEQ])
        oh, ol = sb("oh", [P, 2, SEQ], F32R), sb("ol", [P, 2, SEQ], F32R)
        yT = sb("yT", [P, KT, SEQ])

        FB = ps("FB", [P, 2, 512])
        DB = ps("DB", [P, 2, 512])
        PV = ps("PV", [P, 2, 512])
        Y = ps("Y", [P, KT, 512])

        names = ("w_loaded w_split const a_split x_loaded res_ready ln_stat ln_var ln_log ln_guess ln_done f_done "
                 "f_act f_dve xh_done d_done soft_step masked exp_done soft_done o_done o_out pt_done pt_out "
                 "pv_done gated oh_done ol_done y_done ye_done fin_done out_done x_stored b_ready").split()
        (w_loaded, w_split, const, a_split, x_loaded, res_ready, ln_stat, ln_var, ln_log, ln_guess, ln_done, f_done,
         f_act, f_dve, xh_done, d_done, soft_step, masked, exp_done, soft_done, o_done, o_out, pt_done,
         pt_out, pv_done, gated, oh_done, ol_done, y_done, ye_done, fin_done, out_done, x_stored,
         b_ready) = [sem(n) for n in names]
        NSTAT = TB + 10

        pieces = ([(wh, wl, k, c) for k in range(KT) for c in range(0, 4 * D, 1024)] + [(woh, wol, None, 0)])

        def piece(t, k, c):
            return t[:, c:c + 1024] if k is None else t[:, k, c:c + 1024]

        with nc.Block() as block:
            @block.sync
            def _(sp):
                for i, (_, _, k, c) in enumerate(pieces):
                    at_least(sp, w_split, i - 1)
                    at_least(sp, w_loaded, 16 * i)
                    if k is None:
                        dst, src = raw[:, i % 2].rearrange("p (c n) -> p c n", n=H), w_o.rearrange("(c p) n -> p c n", p=P)
                    else:
                        dst, src = raw[:, i % 2], w_in[k * P:(k + 1) * P, c:c + 1024]
                    sp.dma_start(dst, src).then_inc(w_loaded, 16)
                for b, src in ((bq, b_q), (bk, b_k), (bg, b_g)):
                    for c in range(DT):
                        sp.dma_start(b[:, c:c + 1], src[c * P:(c + 1) * P].rearrange("(p o) -> p o", o=1)
                                     ).then_inc(b_ready, 16)
                sp.dma_start(bv[:], row_broadcast(b_v)).then_inc(b_ready, 16)
                sp.dma_start(bo[:], row_broadcast(b_o)).then_inc(b_ready, 16)
                sp.wait_ge(b_ready, 16 * (3 * DT + 2))
                sp.wait_ge(w_loaded, 16 * len(pieces))

            @block.scalar
            def _(act):
                for i, (hi, _, k, c) in enumerate(pieces):
                    act.wait_ge(w_loaded, 16 * (i + 1))
                    nc.scalar.copy(piece(hi, k, c), raw[:, i % 2]).then_inc(a_split, 1)

            @block.vector
            def _(dve):
                for i, (hi, lo, k, c) in enumerate(pieces):
                    dve.wait_ge(a_split, i + 1)
                    nc.vector.tensor_tensor(piece(lo, k, c), raw[:, i % 2], piece(hi, k, c).bitcast(F32),
                                            ALU.subtract).then_inc(w_split, 1)

            @block.gpsimd
            def _(pool):
                nc.gpsimd.memset(ident[:], 0.0).then_inc(const, 1)
                nc.gpsimd.memset(maskc[:], 0.0).then_inc(const, 1)
                pool.wait_ge(const, 2)
                nc.gpsimd.affine_select(out=ident[:], in_=ident[:], compare_op=ALU.not_equal, fill=1.0,
                                        base=0, pattern=[[-1, P]], channel_multiplier=1).then_inc(const, 1)
                nc.gpsimd.affine_select(out=maskc[:], in_=maskc[:], compare_op=ALU.is_ge, fill=MASKED,
                                        base=0, pattern=[[-1, P]], channel_multiplier=1).then_inc(const, 1)
                pool.wait_ge(const, 4)

        with nc.Block() as block:
            def iterations(eng, body):
                body(-2, 0, False, False, True)
                body(-1, 1, False, True, True)
                body(0, 0, True, True, True)
                with eng.Fori(1, nseq - 3, 2) as reg:
                    body(reg, 1, True, True, True)
                    body(reg + 1, 0, True, True, True)
                body(nseq - 3, 1, True, True, True)
                body(nseq - 2, 0, True, True, False)
                body(nseq - 1, 1, True, False, False)

            @block.sync
            def _(sp):
                def load(s, par):
                    rows = seq_rows(sp, x_in, s)
                    need = [in_register(sp, v) for v in (ev(s - 2, 1, 0), ev(s - 2, 1, 0), 16 * s,)]
                    at_least(sp, ln_done, need[0])
                    at_least(sp, res_ready, need[1])
                    at_least(sp, x_loaded, need[2])
                    sp.dma_start(xin[:, par], rows).then_inc(x_loaded, 16)

                def body(s, par, core, front, ahead):
                    if core:
                        rows = seq_rows(sp, x_out, s)
                        summed, stored = in_register(sp, ev(s, 2, 1)), in_register(sp, 16 * s)
                    if ahead:
                        load(s + 2, par)
                    if core:
                        at_least(sp, out_done, summed)
                        at_least(sp, x_stored, stored)
                        sp.dma_start(rows, xres[:, par]).then_inc(x_stored, 16)

                iterations(sp, body)
                sp.wait_ge(x_stored, 16 * nseq)

            @block.gpsimd
            def _(pool):
                def body(s, par, core, front, ahead):
                    if front:
                        at_least(pool, x_loaded, 16 * (s + 2))
                        at_least(pool, x_stored, 16 * s)
                        nc.gpsimd.tensor_tensor(xres[:, 1 - par], xin[:, 1 - par],
                                                bo[:].unsqueeze(1).to_broadcast([P, TB, H]),
                                                ALU.add).then_inc(res_ready, 1)

                iterations(pool, body)

            @block.scalar
            def _(act):
                def front_use(s, par, i):
                    c, k = FRONT[i]
                    if c == "v":
                        return
                    at_least(act, f_done, ev(s, NF, i))
                    src = FB[:, i % 2]
                    if c == "T":
                        nc.scalar.copy(xh[:, k], src).then_inc(xh_done, 1)
                    elif c == "g":
                        at_least(act, gated, ev(s - 2, DT, DT - 1))
                        nc.scalar.activation(gate[:, par, k], src, ACT.Sigmoid,
                                             bias=bg[:, k:k + 1]).then_inc(f_act, 1)
                    else:
                        dst, b = (qT, bq) if c == "q" else (kT, bk)
                        at_least(act, o_done, ev(s - 2, 2, 1))
                        nc.scalar.activation(dst[:, par, k], src, ACT.Identity, bias=b[:, k:k + 1]).then_inc(f_act, 1)

                def body(s, par, core, front, ahead):
                    for e in range(NSLOT):
                        if core and O_SLOT <= e < O_SLOT + 2:
                            k = e - O_SLOT
                            at_least(act, o_done, ev(s, 2, k))
                            at_least(act, pv_done, ev(s - 1, DT, DT - 1))
                            if k == 0:
                                ins = nc.scalar.copy(st[:, START[0] + P:START[0] + P + OFF[0]], PV[:, 0, 0:OFF[0]])
                            else:
                                nc.scalar.copy(st[:, START[1] + P:START[1] + P + OFF[1]], PV[:, 1, 0:OFF[1]])
                                ins = nc.scalar.copy(st[:, START[2] + P:START[2] + P + OFF[2]],
                                                     PV[:, 1, OFF[1]:OFF[1] + OFF[2]])
                            ins.then_inc(o_out, 1)
                        if core and e == D_SLOT + 1:
                            at_least(act, masked, ev(s, 1, 0))
                            for b in range(NC):
                                ins = nc.scalar.activation(sm[:, b], sm[:, b], ACT.Exp, bias=nmax[:, b:b + 1],
                                                           accum_out=rsum[:, b:b + 1])
                            ins.then_inc(exp_done, 1)
                        if core and e == PT_SLOT:
                            at_least(act, pt_done, ev(s, 1, 0))
                            for kb in range(NC):
                                ins = nc.scalar.copy(st[:, START[kb]:START[kb] + P], DB[:, 1, kb * P:(kb + 1) * P])
                            ins.then_inc(pt_out, 1)
                        if core and PV_SLOT <= e < PV_SLOT + DT:
                            k = e - PV_SLOT
                            at_least(act, gated, ev(s, DT, k))
                            if k >= 2:
                                at_least(act, y_done, ev(s, DT, k - 2))
                            nc.scalar.copy(oh[:, k % 2], o[:, k % 2]).then_inc(oh_done, 1)
                        if core and e == W_SLOT + DT:
                            at_least(act, y_done, ev(s, DT, DT - 1))
                            for k in range(KT):
                                ins = nc.scalar.copy(yT[:, k], Y[:, k])
                            ins.then_inc(ye_done, 1)
                        if ahead and e == STAT_SLOT + 3:
                            at_least(act, ln_var, ev(s + 2, 1, 0))
                            nc.scalar.activation(lnv[:], var[:], ACT.Ln).then_inc(ln_log, 1)
                        if ahead and e == STAT_SLOT + 4:
                            at_least(act, ln_log, ev(s + 2, 1, 0))
                            nc.scalar.activation(guess[:], lnv[:], ACT.Exp, scale=-0.5).then_inc(ln_guess, 1)
                        if not front:
                            continue
                        for i in FRONT_AT.get(e, ()):
                            front_use(s + 1, 1 - par, i)

                iterations(act, body)

            @block.vector
            def _(dve):
                def statistics(s, par):
                    at_least(dve, x_loaded, 16 * (s + 1))
                    for b in range(TB):
                        nc.vector.bn_stats(stats[:, b, :], xin[:, par, b, :]).then_inc(ln_stat, 1)

                def variance(s):
                    m0, m1, q0, q1 = (stats[:, :, c] for c in (1, 4, 2, 5))
                    dve.wait_ge(ln_stat, ev(s, NSTAT, TB - 1))
                    nc.vector.tensor_tensor(mean[:], m0, m1, ALU.add).then_inc(ln_stat, 1)
                    nc.vector.tensor_tensor(yy[:], m0, m1, ALU.subtract).then_inc(ln_stat, 1)
                    nc.vector.tensor_tensor(var[:], q0, q1, ALU.add).then_inc(ln_stat, 1)
                    dve.wait_ge(ln_stat, ev(s, NSTAT, TB + 2))
                    nc.vector.tensor_scalar(mean[:], mean[:], 0.5, None, ALU.mult).then_inc(ln_stat, 1)
                    nc.vector.tensor_tensor(yy[:], yy[:], yy[:], ALU.mult).then_inc(ln_stat, 1)
                    nc.vector.tensor_scalar(var[:], var[:], 1.0 / H, EPS, ALU.mult, ALU.add).then_inc(ln_stat, 1)
                    dve.wait_ge(ln_stat, ev(s, NSTAT, TB + 5))
                    nc.vector.scalar_tensor_tensor(out=var[:], in0=yy[:], scalar=0.25, in1=var[:],
                                                   op0=ALU.mult, op1=ALU.add).then_inc(ln_var, 1)

                def inverse_deviation(s):
                    at_least(dve, ln_guess, ev(s, 1, 0))
                    nc.vector.tensor_tensor(yy[:], guess[:], guess[:], ALU.mult).then_inc(ln_stat, 1)
                    dve.wait_ge(ln_stat, ev(s, NSTAT, TB + 6))
                    nc.vector.tensor_tensor(yy[:], yy[:], var[:], ALU.mult).then_inc(ln_stat, 1)
                    dve.wait_ge(ln_stat, ev(s, NSTAT, TB + 7))
                    nc.vector.tensor_scalar(yy[:], yy[:], -0.5, 1.5, ALU.mult, ALU.add).then_inc(ln_stat, 1)
                    dve.wait_ge(ln_stat, ev(s, NSTAT, TB + 8))
                    nc.vector.tensor_tensor(rstd[:], guess[:], yy[:], ALU.mult).then_inc(ln_stat, 1)

                def normalise(s, par):
                    dve.wait_ge(ln_stat, ev(s, NSTAT, TB + 9))
                    at_least(dve, f_done, ev(s - 1, NF, KT - 1))
                    for b in range(TB):
                        ins = nc.vector.tensor_scalar(xn[:, b, :], xin[:, par, b, :], mean[:, b:b + 1],
                                                      rstd[:, b:b + 1], ALU.subtract, ALU.mult)
                    ins.then_inc(ln_done, 1)

                def front_use(s, par, i):
                    c, k = FRONT[i]
                    src = FB[:, i % 2]
                    if c == "T":
                        at_least(dve, xh_done, ev(s, KT, k))
                        nc.vector.tensor_tensor(xl[:, k], src, xh[:, k].bitcast(F32), ALU.subtract).then_inc(f_dve, 1)
                    if c == "v":
                        at_least(dve, f_done, ev(s, NF, i))
                        at_least(dve, pv_done, ev(s - 2, DT, DT - 1))
                        nc.vector.tensor_tensor(v[:, par, k], src, bv[:], ALU.add).then_inc(f_dve, 1)

                def body(s, par, core, front, ahead):
                    for e in range(NSLOT):
                        if core and e == D_SLOT:
                            at_least(dve, d_done, ev(s, 1, 0))
                            at_least(dve, pt_done, ev(s - 1, 1, 0))
                            nc.vector.scalar_tensor_tensor(
                                out=sm[:], in0=DB[:, 0].rearrange("p (b c) -> p b c", b=NC), scalar=float(D) ** -0.5,
                                in1=maskc[:].unsqueeze(1).to_broadcast([P, NC, P]), op0=ALU.mult,
                                op1=ALU.add).then_inc(soft_step, 1)
                            dve.wait_ge(soft_step, ev(s, 2, 0))
                            nc.vector.tensor_reduce(nmax[:], sm[:], AX.X, ALU.max, negate=True).then_inc(masked, 1)
                        if core and e == D_SLOT + 1:
                            at_least(dve, exp_done, ev(s, 1, 0))
                            nc.vector.reciprocal(rinv[:], rsum[:]).then_inc(soft_step, 1)
                            dve.wait_ge(soft_step, ev(s, 2, 1))
                            nc.vector.tensor_tensor(sm[:], sm[:], rinv[:].unsqueeze(2).to_broadcast([P, NC, P]),
                                                    ALU.mult).then_inc(soft_done, 1)
                        if core and PV_SLOT <= e < PV_SLOT + DT:
                            k = e - PV_SLOT
                            at_least(dve, pv_done, ev(s, DT, k))
                            at_least(dve, f_act, ev(s, NFA, act_no[2 + 3 * DT + k]))
                            at_least(dve, oh_done, ev(s, DT, k - 2) if k >= 2 else ev(s - 1, DT, DT + k - 2))
                            nc.vector.tensor_tensor(o[:, k % 2], PV[:, k % 2], gate[:, par, k], ALU.mult).then_inc(gated, 1)
                            at_least(dve, oh_done, ev(s, DT, k))
                            nc.vector.tensor_tensor(ol[:, k % 2], o[:, k % 2], oh[:, k % 2].bitcast(F32),
                                                    ALU.subtract).then_inc(ol_done, 1)
                        if core and FIN_SLOT <= e < FIN_SLOT + 2:
                            k = e - FIN_SLOT
                            at_least(dve, fin_done, ev(s, 2, k))
                            at_least(dve, res_ready, ev(s, 1, 0))
                            xr = xres[:, par, 2 * k:2 * k + 2, :]
                            nc.vector.tensor_tensor(xr, DB[:, k].rearrange("p (b h) -> p b h", b=2), xr,
                                                    ALU.add).then_inc(out_done, 1)
                        if ahead and e == STAT_SLOT:
                            statistics(s + 2, par)
                        if ahead and e == STAT_SLOT + 2:
                            variance(s + 2)
                        if ahead and e == STAT_SLOT + 5:
                            inverse_deviation(s + 2)
                        if ahead and e == STAT_SLOT + 6:
                            normalise(s + 2, par)
                        if not front:
                            continue
                        for i in FRONT_AT.get(e, ()):
                            front_use(s + 1, 1 - par, i)

                iterations(dve, body)

            @block.tensor
            def _(pe):
                def three(out, ah, al, bh, bl, first, last):
                    pe.matmul(out, al, bh, start=first, stop=False)
                    pe.matmul(out, ah, bl, start=False, stop=False)
                    return pe.matmul(out, ah, bh, start=False, stop=last)

                def front_use(s, par, i):
                    c, k = FRONT[i]
                    dst = FB[:, i % 2]
                    j, sj = (i - 2, s) if i >= 2 else (i - 2 + NF, s - 1)
                    if by_act[j]:
                        at_least(pe, f_act, ev(sj, NFA, act_no[j]))
                    else:
                        at_least(pe, f_dve, ev(sj, NFD, dve_no[j]))
                    if c == "T":
                        at_least(pe, ln_done, ev(s, 1, 0))
                        for b in range(TB):
                            ins = pe.transpose(dst[:, b * P:(b + 1) * P], xn[:, b, k * P:(k + 1) * P], ident[:])
                    elif c == "v":
                        for t in range(KT):
                            ins = three(dst, xh[:, t, k * P:(k + 1) * P], xl[:, t, k * P:(k + 1) * P],
                                        wh[:, t, 2 * D:3 * D], wl[:, t, 2 * D:3 * D], t == 0, t == KT - 1)
                    else:
                        at_least(pe, f_dve, ev(s, NFD, KT - 1))
                        w = slice("qkvg".index(c) * D + k * P, "qkvg".index(c) * D + (k + 1) * P)
                        for t in range(KT):
                            ins = three(dst, wh[:, t, w], wl[:, t, w], xh[:, t], xl[:, t], t == 0, t == KT - 1)
                    ins.then_inc(f_done, 1)

                def body(s, par, core, front, ahead):
                    for e in range(NSLOT):
                        if core and e == D_SLOT:
                            at_least(pe, f_act, ev(s, NFA, 2 * DT - 1))
                            at_least(pe, out_done, ev(s - 1, 2, 0))
                            for b in range(NC):
                                for t in range(DT):
                                    ins = pe.matmul(DB[:, 0, b * P:(b + 1) * P], qT[:, par, t, b * P:(b + 1) * P],
                                                    kT[:, par, t, b * P:(b + 1) * P], start=(t == 0), stop=(t == DT - 1))
                            ins.then_inc(d_done, 1)
                        if core and O_SLOT <= e < O_SLOT + 2:
                            at_least(pe, gated, ev(s - 1, DT, DT - 1))
                            c = 0
                            for kb in ((0,) if e == O_SLOT else (1, 2)):
                                for t in range(DT):
                                    ins = pe.matmul(PV[:, e - O_SLOT, c:c + OFF[kb]], kT[:, par, t, kb * P:(kb + 1) * P],
                                                    qT[:, par, t, (kb + 1) * P:SEQ], start=(t == 0), stop=(t == DT - 1))
                                c += OFF[kb]
                            ins.then_inc(o_done, 1)
                        if core and e == PT_SLOT:
                            at_least(pe, soft_done, ev(s, 1, 0))
                            at_least(pe, out_done, ev(s - 1, 2, 1))
                            for b in range(NC):
                                ins = pe.transpose(DB[:, 1, b * P:(b + 1) * P], sm[:, b], ident[:])
                            ins.then_inc(pt_done, 1)
                        if core and PV_SLOT <= e < PV_SLOT + DT:
                            k = e - PV_SLOT
                            if k == 0:
                                at_least(pe, pt_out, ev(s, 1, 0))
                                at_least(pe, o_out, ev(s, 2, 1))
                                at_least(pe, f_dve, ev(s, NFD, NFD - 1))
                            if k >= 2:
                                at_least(pe, gated, ev(s, DT, k - 2))
                            for kb in range(NC):
                                n = SEQ - kb * P
                                ins = pe.matmul(PV[:, k % 2, kb * P:SEQ], v[:, par, kb, k * P:(k + 1) * P],
                                                st[:, START[kb]:START[kb] + n], start=(kb == 0), stop=(kb == NC - 1))
                            ins.then_inc(pv_done, 1)
                        if core and W_SLOT <= e < W_SLOT + DT:
                            k = e - W_SLOT
                            at_least(pe, ol_done, ev(s, DT, k))
                            at_least(pe, ye_done, ev(s - 1, 1, 0))
                            for h in range(KT):
                                w = slice(k * H + h * P, k * H + (h + 1) * P)
                                ins = three(Y[:, h], woh[:, w], wol[:, w], oh[:, k % 2], ol[:, k % 2], k == 0, k == DT - 1)
                            ins.then_inc(y_done, 1)
                        if core and FIN_SLOT <= e < FIN_SLOT + 2:
                            k = e - FIN_SLOT
                            at_least(pe, ye_done, ev(s, 1, 0))
                            if k:
                                at_least(pe, pt_out, ev(s, 1, 0))
                            else:
                                at_least(pe, masked, ev(s, 1, 0))
                            for b in range(2):
                                for c in range(KT):
                                    ins = pe.transpose(DB[:, k, b * H + c * P:b * H + (c + 1) * P],
                                                       yT[:, c, (2 * k + b) * P:(2 * k + b + 1) * P], ident[:])
                            ins.then_inc(fin_done, 1)
                        if front:
                            for i in FRONT_AT.get(e, ()):
                                front_use(s + 1, 1 - par, i)

                iterations(pe, body)

def transformer_block(nc, w, out):
    x = w["x"].rearrange("b s h -> (b s) h")
    nseq = x.shape[0] // SEQ
    x1 = nc.dram_tensor("x_after_a", x.shape, F32, kind="Internal").ap()
    x2 = nc.dram_tensor("x_after_f", x.shape, F32, kind="Internal").ap()
    x3 = nc.dram_tensor("x_after_b", x.shape, F32, kind="Internal").ap()
    phase_a(nc, x, x1, w["w_qkv"], w["b_qkv"], w["w_out"], w["b_out"], nseq)
    phase_f(nc, "f1_", x1, x2, w["w_gate"], w["bias_corr"], w["w1"], w["w2"], nseq)
    phase_b(nc, x2, x3, w["w_in"], w["b_q"], w["b_k"], w["b_v"], w["b_g"], w["w_o"], w["b_o"], nseq)
    phase_f(nc, "f2_", x3, out.rearrange("b s h -> (b s) h"), w["w_gate"], w["bias_corr"], w["w1"], w["w2"], nseq)


def kernel(**inputs):
    import numpy as np
    import concourse.bacc as bacc
    from concourse.bass_utils import run_bass_kernel_spmd

    def get(name):
        return np.asarray(inputs[name])

    W1, W2 = get("L0_ffn_W1"), get("L0_ffn_W2")
    Ws1, Ws2 = get("L0_ffn_Ws1"), get("L0_ffn_Ws2")
    h = Ws1.shape[1]
    arrays = {
        "x": get("L0_attn_a_x"),
        "w_qkv": get("L0_attn_a_w_qkv"), "b_qkv": get("L0_attn_a_b_qkv"),
        "w_out": get("L0_attn_a_w_out"), "b_out": get("L0_attn_a_b_out"),
        "w_in": np.concatenate([get("L0_attn_b_W" + c) for c in "qkvg"], axis=1),
        "b_q": get("L0_attn_b_bq"), "b_k": get("L0_attn_b_bk"), "b_v": get("L0_attn_b_bv"), "b_g": get("L0_attn_b_bg"),
        "w_o": get("L0_attn_b_Wo"), "b_o": get("L0_attn_b_bo"),
        "w_gate": get("L0_ffn_Wg").T, "bias_corr": get("L0_ffn_bias_corr"),
        "w1": np.concatenate([W1.transpose(2, 0, 1).reshape(h, -1), Ws1.T], axis=1),
        "w2": np.concatenate([W2.transpose(2, 0, 1).reshape(P, -1),
                              Ws2.T.reshape(-1, P, h).transpose(1, 0, 2).reshape(P, -1)], axis=1),
    }
    arrays = {k: np.ascontiguousarray(a) for k, a in arrays.items()}
    nc = bacc.Bacc("TRN2", target_bir_lowering=False, num_devices=1)
    w = {k: nc.dram_tensor("in_" + k, a.shape, mybir.dt.from_np(a.dtype), kind="ExternalInput").ap() for k, a in arrays.items()}
    out = nc.dram_tensor("out", arrays["x"].shape, F32, kind="ExternalOutput").ap()
    transformer_block(nc, w, out)
    r = run_bass_kernel_spmd(nc, [{"in_" + k: a for k, a in arrays.items()}], core_ids=[0])
    return r.results[0]["out"]
```

```python
from contextlib import ExitStack

import concourse.bass as bass
from concourse import mybir

P = 128
F32 = mybir.dt.float32
F32R = mybir.dt.float32r
BF16 = mybir.dt.bfloat16
ALU = mybir.AluOpType
ACT = mybir.ActivationFunctionType
AX = mybir.AxisListType

H = 256
KT = H // P
SEQ = 512
TB = SEQ // P
EPS = 1e-5
MASKED = -1e30


def at_least(eng, sem, value):
    if isinstance(value, int) and value <= 0:
        return
    eng.wait_ge(sem, value)


def in_register(eng, value):
    return value if isinstance(value, int) else eng.to_reg(value)


def wait_apart(eng, sem, value, past, past_value):
    value = in_register(eng, value)
    if isinstance(value, int) and value <= 0:
        return
    eng.wait_ge(past, past_value)
    eng.wait_ge(sem, value)


def ev(s, per_seq, i):
    if isinstance(s, int) and s < 0:
        return 0
    return s * per_seq + (i + 1)


def seq_rows(eng, dram, s):
    row = s * SEQ if isinstance(s, int) else eng.snap(s * SEQ)
    return dram[bass.ds(row, SEQ), :].rearrange("(b p) h -> p b h", p=P)


def row_broadcast(vec):
    return vec.partition_broadcast(P)


HEADS, GLOBAL, DH, WINDOW = 16, 4, 16, 64
HT = P // DH
QT = HEADS // HT
PAIR = 2 * DH
PT = HT // 2
PAIRS = HEADS // 2
ONES = 3 * PAIR
BAND = P + WINDOW
VW = 32


def units_of_scores():
    out = []
    for kb in range(TB):
        for half in range(2):
            out.append((0, kb, (2 * half, 2 * half + 1), SEQ - P * kb))
    for t in range(1, HEADS // 4):
        for kb in range(TB):
            out.append((t, kb, tuple(range(4 * t, 4 * t + 4)), min(BAND, SEQ - P * kb)))
    return out


def units_of_max():
    glob, loc = [], []
    for qb in range(TB):
        n = P * (qb + 1)
        per = SEQ // n
        for h in range(0, GLOBAL, per):
            glob.append((tuple(range(h, h + per)), qb, 0, n))
    for four in range(GLOBAL, HEADS, 4):
        for qb in range(TB):
            n = P if qb == 0 else BAND
            per = 4 if qb == 0 else 2
            for h in range(four, four + 4, per):
                loc.append((tuple(range(h, h + per)), qb, P * (qb + 1) - n, n))
    return glob, loc


def rotation(n, banks):
    bank = [i % banks for i in range(n)]
    if n % banks:
        assert banks == 3 and n % banks == 1
        bank[-1] = 1
    before = []
    for i in range(n):
        j = next(j for j in range(i - 1, i - n - 1, -1) if bank[j % n] == bank[i])
        before.append((j % n, 0 if j >= 0 else 1))
    return bank, before


def phase_a(nc, x_in, x_out, w_qkv, b_qkv, w_out, b_out, nseq):
    UNITS = units_of_scores()
    NU = len(UNITS)
    MAXG, MAXL = units_of_max()

    def spread(first, slots, uses):
        return [(first + int(i * slots / len(uses)), ("m", u)) for i, u in enumerate(uses)]

    timed = ([(4, ("T", 0)), (4, ("T", 1)), (5, ("q", 0)), (6, ("k", 0)), (6, ("q", 1)), (6, ("k", 1)),
              (10, ("v", 0)), (8, ("v", 1))] +
             spread(9, 5.5, MAXG) + [(15, ("mT", 0))] + spread(13, 10.0, MAXL) + [(23, ("mT", 1))])
    for p, slot in enumerate((15, 15, 16, 16, 18, 18, 21, 22)):
        timed += [(slot, ("rk", p)), (slot, ("rq", p))]
    BY_ACT = (1, 5, 7)
    timed.sort(key=lambda x: x[0])
    FRONT = [use for _, use in timed]
    NF = len(FRONT)
    assert NU % 4 == 0
    f_bank, f_before = rotation(NF, 3)
    s_bank, s_before = rotation(2 * NU, 3)
    by_act = [kind == "rk" or (kind == "rq" and k in BY_ACT) for kind, k in FRONT]
    act_no = [sum(by_act[:i]) for i in range(NF)]
    dve_no = [i - act_no[i] for i in range(NF)]
    NFA, NFD = sum(by_act), NF - sum(by_act)
    at = {use: i for i, use in enumerate(FRONT)}
    slot_front = {u: [i for i in range(NF) if timed[i][0] == u] for u in range(2 * NU)}
    assert timed[-1][0] - NU < timed[0][0]
    HIGH = [("T", 0), ("T", 1)] + [(c, t) for t in range(QT) for c in ("q", "k")]
    NH = len(HIGH)
    TAIL = [("N", 0), ("N", 1), ("C", 0), ("N", 2), ("N", 3), ("C", 1), ("O", 0), ("O", 1)]
    NTAIL = len(TAIL)
    TAIL_AT = {11: [0], 16: [1], 17: [2], 19: [3]}
    LATE_AT = {3: [4], 4: [5], 5: [6], 7: [7]}
    t_first = {0: 0, 1: 8, 2: 12, 3: 16}
    t_last = {0: 7, 1: 11, 2: 15, 3: 19}

    with ExitStack() as ctx:
        def sb(name, shape, dt=F32):
            return ctx.enter_context(nc.sbuf_tensor("a_" + name, shape, dt))

        def sem(name):
            return ctx.enter_context(nc.semaphore("a_" + name))

        ident = sb("ident", [P, P])
        identb = sb("identb", [P, P], BF16)
        mask_g = sb("mask_g", [P, P], BF16)
        mask_l = sb("mask_l", [P, BAND], BF16)
        headmask = sb("headmask", [P, HT])
        pairmask = sb("pairmask", [P, 2])
        sel0 = sb("sel0", [P, PT, 3, PAIR])
        selz = sb("selz", [P, PT, PAIR])
        sel = {n: sb("sel_" + n, [P, PT, 3, PAIR], F32R) for n in ("kh", "kl", "qh", "ql")}
        wraw, oraw = sb("wraw", [P, KT, 3 * H]), sb("oraw", [P, KT, H])
        wh, wl = sb("wh", [P, KT, 3 * H], F32R), sb("wl", [P, KT, 3 * H], F32R)
        woh, wol = sb("woh", [P, KT, H], F32R), sb("wol", [P, KT, H], F32R)
        bq = sb("bq", [P, QT])
        bk = sb("bk", [P, QT])
        bv = sb("bv", [P, H])
        bo = sb("bo", [P, H])
        xin = sb("xin", [P, 2, TB, H])
        xres = sb("xres", [P, 2, TB, H])
        stats = sb("stats", [P, TB, 6])
        mean = sb("mean", [P, TB])
        var, guess, yy, rstd = sb("var", [P, TB]), sb("guess", [P, TB]), sb("yy", [P, TB]), sb("rstd", [P, TB])
        lnv = sb("lnv", [P, TB])
        xn = sb("xn", [P, TB, H])
        xh, xl = sb("xh", [P, KT, SEQ], F32R), sb("xl", [P, KT, SEQ], F32R)
        qh, ql = sb("qh", [P, QT, SEQ], F32R), sb("ql", [P, QT, SEQ], F32R)
        kh, kl = sb("kh", [P, QT, SEQ], F32R), sb("kl", [P, QT, SEQ], F32R)
        ks = sb("ks", [P, PAIRS, SEQ], F32R)
        qs = sb("qs", [P, HEADS, SEQ], F32R)
        qb16 = sb("qb16", [P, HEADS, SEQ], BF16)
        kb16 = sb("kb16", [P, QT, SEQ], BF16)
        vv = sb("vv", [P, 2, TB, HEADS, VW])
        pt = sb("pt", [P, 4, 1024])
        pvs = sb("pvs", [P, 2, SEQ])
        rden = sb("rden", [P, TB, 4])
        ctxn = sb("ctxn", [P, TB, HEADS, DH])
        ch, cl = sb("ch", [P, KT, SEQ], F32R), sb("cl", [P, KT, SEQ], F32R)
        mx = sb("mx", [P, HEADS, TB])
        mTg = sb("mTg", [GLOBAL, SEQ], F32R)
        mTl = sb("mTl", [HEADS - GLOBAL, SEQ], F32R)

        S = ctx.enter_context(nc.psum_tensor("a_S", [P, 3, 512], F32))
        FB = ctx.enter_context(nc.psum_tensor("a_FB", [P, 3, 512], F32))
        PV = ctx.enter_context(nc.psum_tensor("a_PV", [P, 512], F32))
        TL = ctx.enter_context(nc.psum_tensor("a_TL", [P, 512], F32))

        w_loaded, w_ready = sem("w_loaded"), sem("w_ready")
        w_high = sem("w_high")
        dve_ready = sem("dve_ready")
        x_loaded = sem("x_loaded")
        res_ready = sem("res_ready")
        ln_stat = sem("ln_stat")
        ln_var = sem("ln_var")
        ln_log = sem("ln_log")
        ln_guess = sem("ln_guess")
        ln_done = sem("ln_done")
        f_done = sem("f_done")
        f_act = sem("f_act")
        f_dve = sem("f_dve")
        hi_done = sem("hi_done")
        ch_done = sem("ch_done")
        q_masked = sem("q_masked")
        k_half = sem("k_half")
        m_row = sem("m_row")
        s_done = sem("s_done")
        e_done = sem("e_done")
        p_first = sem("p_first")
        p_done = sem("p_done")
        pv_done = sem("pv_done")
        pv_out = sem("pv_out")
        t_done = sem("t_done")
        t_dve = sem("t_dve")
        r_done = sem("r_done")
        x_stored = sem("x_stored")

        N_AT = [TAIL.index(("N", t)) for t in range(4)]
        C_AT = [TAIL.index(("C", t)) for t in range(2)]
        STAT_SLOT, VAR_SLOT, LOG_SLOT, GUESS_SLOT, ROOT_SLOT, NORM_SLOT = 0, 0, 1, 2, 3, 3
        ACT_FIRST = (8, 10)
        PE_FIRST = (3, 7)
        RES_SLOT = 9
        WEIGHTS_SLOT = 4
        MASK_AT = (5, 5, 8, 7)
        K_AT = (6, 7)
        NLOC = NU - 8
        NSTAT = TB + 10
        W_DMAS = 16 * (4 + 2 * QT)
        mt_at = [FRONT.index(("mT", g)) for g in range(2)]

        with nc.Block() as block:

            def iterations(eng, body):
                body(-1, 1, False, False, True)
                body(0, 0, False, True, True)
                with eng.Fori(1, nseq - 3, 2) as r:
                    body(r, 1, True, True, True)
                    body(r + 1, 0, True, True, True)
                body(nseq - 3, 1, True, True, True)
                body(nseq - 2, 0, True, True, True)
                body(nseq - 1, 1, True, True, False)
                body(nseq, 0, True, False, False)

            @block.sync
            def _(sp):
                def load(s, par):
                    rows = seq_rows(sp, x_in, s)
                    read, loaded = in_register(sp, ev(s - 2, 1, 0)), in_register(sp, 16 * s)
                    at_least(sp, ln_done, read)
                    at_least(sp, res_ready, read)
                    at_least(sp, x_loaded, loaded)
                    sp.dma_start(xin[:, par], rows).then_inc(x_loaded, 16)

                def m_rows(s, g):
                    src, h0, h1 = (mTg, 0, GLOBAL) if g == 0 else (mTl, GLOBAL, HEADS)
                    last = 2 * t_last[0] + 1 if g == 0 else 2 * NU - 1
                    made = in_register(sp, ev(s, NFD, dve_no[mt_at[g]]))
                    used = in_register(sp, ev(s - 1, 2 * NU, last))
                    copied = in_register(sp, 16 * (2 * s + g))
                    at_least(sp, f_dve, made)
                    at_least(sp, s_done, used)
                    at_least(sp, m_row, copied)
                    sp.dma_start(qs[ONES:ONES + 1, h0:h1, :].bitcast(F32), src[:].bitcast(F32)).then_inc(m_row, 16)

                def body(s, par, tail, core, front):
                    if tail:
                        rows = seq_rows(sp, x_out, s - 1)
                        summed, stored = in_register(sp, ev(s - 1, NTAIL, NTAIL - 1)), in_register(sp, 16 * s)
                    if not isinstance(s, int) or 2 <= s + 2 < nseq:
                        load(s + 2, par)
                    if core:
                        m_rows(s, 1)
                    if tail:
                        at_least(sp, t_dve, summed)
                        sp.dma_start(rows, xres[:, 1 - par]).then_inc(x_stored, 16)
                        at_least(sp, x_stored, stored)
                    if front:
                        m_rows(s + 1, 0)

                sp.dma_start(xin[:, 0], seq_rows(sp, x_in, 0)).then_inc(x_loaded, 16)
                sp.dma_start(wraw[:], w_qkv.rearrange("(k p) n -> p k n", p=P)).then_inc(w_loaded, 16)
                sp.dma_start(oraw[:], w_out.rearrange("(k p) n -> p k n", p=P)).then_inc(w_loaded, 16)
                for b, c0 in ((bq, 0), (bk, H)):
                    for t in range(QT):
                        sp.dma_start(b[:, t:t + 1], b_qkv[c0 + t * P:c0 + (t + 1) * P].rearrange("(p o) -> p o", o=1)
                                     ).then_inc(w_loaded, 16)
                sp.dma_start(bv[:], row_broadcast(b_qkv[2 * H:3 * H])).then_inc(w_loaded, 16)
                sp.dma_start(bo[:], row_broadcast(b_out)).then_inc(w_loaded, 16)
                sp.wait_ge(x_loaded, 16)
                sp.dma_start(xin[:, 1], seq_rows(sp, x_in, 1)).then_inc(x_loaded, 16)
                iterations(sp, body)
                sp.wait_ge(x_stored, 16 * nseq)

            @block.gpsimd
            def _(pool):
                def select(s, u):
                    t, kb, heads, n = UNITS[u]
                    wait_apart(pool, e_done, ev(s, 2 * NU, 2 * u + 1), w_ready, 14)
                    nh = len(heads)
                    v = pt[:, u % 4, 0:nh * n].rearrange("p (h q) -> p h q", q=n)
                    ins = nc.gpsimd.affine_select(out=v[:, :, 0:P], in_=v[:, :, 0:P], compare_op=ALU.is_ge,
                                                  fill=0.0, base=0, pattern=[[0, nh], [1, P]],
                                                  channel_multiplier=-1)
                    if t > 0:
                        ins.then_inc(p_first, 1)
                        wait_apart(pool, p_first, ev(s, NLOC, u - 8), w_ready, 14)
                        ins = nc.gpsimd.affine_select(out=v[:, :, WINDOW:n], in_=v[:, :, WINDOW:n],
                                                      compare_op=ALU.is_ge, fill=0.0, base=0,
                                                      pattern=[[0, nh], [-1, n - WINDOW]],
                                                      channel_multiplier=1)
                    ins.then_inc(p_done, 1)

                def residual(s, par):
                    at_least(pool, x_loaded, 16 * (s + 1))
                    at_least(pool, x_stored, 16 * (s - 1))
                    nc.gpsimd.tensor_tensor(xres[:, par], xin[:, par],
                                            bo[:].unsqueeze(1).to_broadcast([P, TB, H]),
                                            ALU.add).then_inc(res_ready, 1)

                def body(s, par, tail, core, front):
                    for u in range(NU):
                        if core:
                            select(s, u)
                        if front and u == RES_SLOT:
                            residual(s + 1, 1 - par)

                nc.gpsimd.memset(ident[:], 0.0).then_inc(w_ready, 1)
                nc.gpsimd.memset(mask_g[:], 0.0).then_inc(w_ready, 1)
                nc.gpsimd.memset(mask_l[:], 0.0).then_inc(w_ready, 1)
                nc.gpsimd.memset(headmask[:], DH ** -0.5).then_inc(w_ready, 1)
                nc.gpsimd.memset(sel0[:], 0.0).then_inc(w_ready, 1)
                pool.wait_ge(w_ready, 5)
                nc.gpsimd.affine_select(out=ident[:], in_=ident[:], compare_op=ALU.not_equal, fill=1.0,
                                        base=0, pattern=[[-1, P]], channel_multiplier=1).then_inc(w_ready, 1)
                nc.gpsimd.affine_select(out=mask_g[:], in_=mask_g[:], compare_op=ALU.is_ge, fill=MASKED,
                                        base=0, pattern=[[-1, P]], channel_multiplier=1).then_inc(w_ready, 1)
                nc.gpsimd.affine_select(out=mask_l[:], in_=mask_l[:], compare_op=ALU.is_ge, fill=MASKED,
                                        base=WINDOW, pattern=[[-1, BAND]], channel_multiplier=1).then_inc(w_ready, 1)
                nc.gpsimd.affine_select(out=headmask[:], in_=headmask[:], compare_op=ALU.is_ge, fill=0.0,
                                        base=0, pattern=[[-DH, HT]], channel_multiplier=1).then_inc(w_ready, 1)
                pool.wait_ge(w_ready, 9)
                nc.gpsimd.affine_select(out=mask_l[:], in_=mask_l[:], compare_op=ALU.is_ge, fill=MASKED,
                                        base=0, pattern=[[1, BAND]], channel_multiplier=-1).then_inc(w_ready, 1)
                nc.gpsimd.affine_select(out=headmask[:], in_=headmask[:], compare_op=ALU.is_ge, fill=0.0,
                                        base=DH - 1, pattern=[[DH, HT]], channel_multiplier=-1).then_inc(w_ready, 1)
                nc.gpsimd.affine_select(out=sel0[:], in_=sel0[:], compare_op=ALU.not_equal, fill=1.0,
                                        base=0, pattern=[[-PAIR, PT], [0, 3], [-1, PAIR]],
                                        channel_multiplier=1).then_inc(w_ready, 1)
                nc.gpsimd.tensor_copy(identb[:], ident[:]).then_inc(w_ready, 1)
                nc.gpsimd.memset(vv[:, :, :, :, DH:VW], 1.0).then_inc(w_ready, 1)
                pool.wait_ge(w_ready, 14)
                pool.wait_ge(w_loaded, W_DMAS)
                iterations(pool, body)

            @block.scalar
            def _(act):
                def front_use(s, par, i):
                    kind, k = FRONT[i]
                    if kind in ("T", "q", "k", "rk", "rq") and not (kind == "rq" and not by_act[i]):
                        at_least(act, f_done, ev(s, NF, i))
                    src = FB[:, f_bank[i], :]
                    if kind == "T":
                        at_least(act, f_done, ev(s - 1, NF, at["v", 1]))
                        nc.scalar.copy(xh[:, k, :], src).then_inc(hi_done, 1)
                    elif kind in ("q", "k"):
                        dst, b = (qh, bq) if kind == "q" else (kh, bk)
                        at_least(act, f_done, ev(s - 1, NF, NF - 1))
                        nc.scalar.activation(dst[:, k, :], src, ACT.Identity, bias=b[:, k:k + 1]).then_inc(hi_done, 1)
                    elif kind == "rk":
                        at_least(act, s_done, ev(s - 1, 2 * NU, 2 * t_last[k // 2] + 1))
                        nc.scalar.copy(ks[0:ONES, k, :], src[0:ONES]).then_inc(f_act, 1)
                    elif kind == "rq" and by_act[i]:
                        at_least(act, s_done, ev(s - 1, 2 * NU, 2 * t_last[k // 2] + 1))
                        for j in range(2):
                            ins = nc.scalar.activation(qs[0:ONES, 2 * k + j, :], src[0:ONES], ACT.Copy,
                                                       scale=pairmask[0:ONES, j:j + 1])
                        ins.then_inc(f_act, 1)

                def log_variance(s):
                    at_least(act, ln_var, ev(s, 1, 0))
                    nc.scalar.activation(lnv[:], var[:], ACT.Ln).then_inc(ln_log, 1)

                def rsqrt_guess(s):
                    at_least(act, ln_log, ev(s, 1, 0))
                    nc.scalar.activation(guess[:], lnv[:], ACT.Exp, scale=-0.5).then_inc(ln_guess, 1)

                def exps(s, u):
                    _, _, heads, n = UNITS[u]
                    nh = len(heads)
                    w = nh * n // 2
                    at_least(act, pv_done, ev(s, NU, u - 4))
                    for b in range(2):
                        at_least(act, s_done, ev(s, 2 * NU, 2 * u + b))
                        nc.scalar.activation(pt[:, u % 4, b * w:(b + 1) * w], S[:, s_bank[2 * u + b], 0:w],
                                             ACT.Exp).then_inc(e_done, 1)

                def pv_copy(s, t):
                    at_least(act, pv_done, ev(s, NU, t_last[t]))
                    at_least(act, t_done, ev(s, NTAIL, N_AT[t - 2]) if t >= 2 else ev(s - 1, NTAIL, N_AT[t + 2]))
                    nc.scalar.copy(pvs[:, t % 2, :], PV[:]).then_inc(pv_out, 1)

                def tail_use(s, i):
                    kind, k = TAIL[i]
                    if kind != "C":
                        return
                    at_least(act, t_done, ev(s, NTAIL, i))
                    nc.scalar.copy(ch[:, k, :], TL[:]).then_inc(ch_done, 1)

                def body(s, par, tail, core, front):
                    for u in range(NU):
                        def fronts():
                            for i in slot_front[NU + u] if core else ():
                                front_use(s, par, i)
                            if front:
                                for i in slot_front[u]:
                                    front_use(s + 1, 1 - par, i)

                        if u in ACT_FIRST:
                            fronts()
                        if tail and u == 1:
                            pv_copy(s - 1, 3)
                        if front and u == LOG_SLOT:
                            log_variance(s + 1)
                        if front and u == GUESS_SLOT:
                            rsqrt_guess(s + 1)
                        if isinstance(s, int) and s == -1 and u == WEIGHTS_SLOT:
                            act.wait_ge(w_loaded, W_DMAS)
                            nc.scalar.copy(wh[:], wraw[:]).then_inc(w_high, 1)
                            nc.scalar.copy(woh[:], oraw[:]).then_inc(w_high, 1)
                            act.wait_ge(dve_ready, 17)
                        if core:
                            exps(s, u)
                            for t in range(3):
                                if u == t_last[t] + 2:
                                    pv_copy(s, t)
                        for i in TAIL_AT.get(u, ()) if core else ():
                            tail_use(s, i)
                        for i in LATE_AT.get(u, ()) if tail else ():
                            tail_use(s - 1, i)
                        if u not in ACT_FIRST:
                            fronts()

                iterations(act, body)

            @block.vector
            def _(dve):
                def statistics(s, par):
                    at_least(dve, x_loaded, 16 * (s + 1))
                    for b in range(TB):
                        nc.vector.bn_stats(stats[:, b, :], xin[:, par, b, :]).then_inc(ln_stat, 1)

                def variance(s):
                    m0, m1, q0, q1 = (stats[:, :, c] for c in (1, 4, 2, 5))
                    dve.wait_ge(ln_stat, ev(s, NSTAT, TB - 1))
                    nc.vector.tensor_tensor(mean[:], m0, m1, ALU.add).then_inc(ln_stat, 1)
                    nc.vector.tensor_tensor(yy[:], m0, m1, ALU.subtract).then_inc(ln_stat, 1)
                    nc.vector.tensor_tensor(var[:], q0, q1, ALU.add).then_inc(ln_stat, 1)
                    dve.wait_ge(ln_stat, ev(s, NSTAT, TB + 2))
                    nc.vector.tensor_scalar(mean[:], mean[:], 0.5, None, ALU.mult).then_inc(ln_stat, 1)
                    nc.vector.tensor_tensor(yy[:], yy[:], yy[:], ALU.mult).then_inc(ln_stat, 1)
                    nc.vector.tensor_scalar(var[:], var[:], 1.0 / H, EPS, ALU.mult, ALU.add).then_inc(ln_stat, 1)
                    dve.wait_ge(ln_stat, ev(s, NSTAT, TB + 5))
                    nc.vector.scalar_tensor_tensor(out=var[:], in0=yy[:], scalar=0.25, in1=var[:],
                                                   op0=ALU.mult, op1=ALU.add).then_inc(ln_var, 1)

                def inverse_deviation(s):
                    at_least(dve, ln_guess, ev(s, 1, 0))
                    nc.vector.tensor_tensor(yy[:], guess[:], guess[:], ALU.mult).then_inc(ln_stat, 1)
                    dve.wait_ge(ln_stat, ev(s, NSTAT, TB + 6))
                    nc.vector.tensor_tensor(yy[:], yy[:], var[:], ALU.mult).then_inc(ln_stat, 1)
                    dve.wait_ge(ln_stat, ev(s, NSTAT, TB + 7))
                    nc.vector.tensor_scalar(yy[:], yy[:], -0.5, 1.5, ALU.mult, ALU.add).then_inc(ln_stat, 1)
                    dve.wait_ge(ln_stat, ev(s, NSTAT, TB + 8))
                    nc.vector.tensor_tensor(rstd[:], guess[:], yy[:], ALU.mult).then_inc(ln_stat, 1)

                def normalise(s, par):
                    dve.wait_ge(ln_stat, ev(s, NSTAT, TB + 9))
                    at_least(dve, f_done, ev(s - 1, NF, at["T", 1]))
                    for b in range(TB):
                        ins = nc.vector.tensor_scalar(xn[:, b, :], xin[:, par, b, :], mean[:, b:b + 1],
                                                      rstd[:, b:b + 1], ALU.subtract, ALU.mult)
                    ins.then_inc(ln_done, 1)

                def mask_q(s, four):
                    t = 4 * four // HT
                    at_least(dve, hi_done, ev(s, NH, HIGH.index(("q", t))))
                    at_least(dve, f_done, ev(s - 1, NF, mt_at[1]))
                    for h in range(4 * four, 4 * four + 4):
                        ins = nc.vector.tensor_scalar(qb16[:, h, :], qh[:, t, :].bitcast(F32),
                                                      headmask[:, h % HT:h % HT + 1], None, ALU.mult)
                    ins.then_inc(q_masked, 1)

                def half_k(s, t):
                    at_least(dve, hi_done, ev(s, NH, HIGH.index(("k", t))))
                    at_least(dve, f_done, ev(s - 1, NF, mt_at[1]))
                    nc.vector.tensor_copy(kb16[:, t, :], kh[:, t, :].bitcast(F32)).then_inc(k_half, 1)

                def front_use(s, par, i):
                    kind, k = FRONT[i]
                    if by_act[i]:
                        return
                    src = FB[:, f_bank[i], :]
                    if kind in ("T", "q", "k"):
                        at_least(dve, hi_done, ev(s, NH, HIGH.index((kind, k))))
                        if kind == "T":
                            nc.vector.tensor_tensor(xl[:, k, :], src, xh[:, k, :].bitcast(F32), ALU.subtract
                                                    ).then_inc(f_dve, 1)
                        else:
                            lo, hi, b = (ql, qh, bq) if kind == "q" else (kl, kh, bk)
                            nc.vector.scalar_tensor_tensor(out=lo[:, k, :], in0=src, scalar=b[:, k:k + 1],
                                                           in1=hi[:, k, :].bitcast(F32), op0=ALU.add,
                                                           op1=ALU.subtract).then_inc(f_dve, 1)
                        return
                    at_least(dve, f_done, ev(s, NF, i))
                    if kind == "rq":
                        at_least(dve, s_done, ev(s - 1, 2 * NU, 2 * t_last[k // 2] + 1))
                        for j in range(2):
                            ins = nc.vector.tensor_scalar(qs[0:ONES, 2 * k + j, :], src[0:ONES],
                                                          pairmask[0:ONES, j:j + 1], None, ALU.mult)
                        ins.then_inc(f_dve, 1)
                        return
                    if kind == "v":
                        at_least(dve, pv_done, ev(s - 2, NU, NU - 1))
                        for b in range(2):
                            ins = nc.vector.tensor_tensor(
                                vv[:, par, 2 * k + b, :, 0:DH],
                                src[:, b * H:(b + 1) * H].rearrange("p (h d) -> p h d", d=DH),
                                bv[:].rearrange("p (h d) -> p h d", d=DH), ALU.add)
                        ins.then_inc(f_dve, 1)
                    elif kind == "m":
                        heads, qb, _, n = k
                        nh = len(heads)
                        at_least(dve, f_done, ev(s - 1, NF, mt_at[1]))
                        nc.vector.tensor_reduce(mx[:, heads[0]:heads[0] + nh, qb],
                                                src[:, 0:nh * n].rearrange("p (h c) -> p h c", c=n),
                                                AX.X, ALU.max).then_inc(f_dve, 1)
                    else:
                        dst, n = (mTg, GLOBAL) if k == 0 else (mTl, HEADS - GLOBAL)
                        at_least(dve, m_row, 16 * (2 * (s - 1) + k + 1))
                        nc.vector.tensor_scalar(dst[:], src[0:n, :], -1.0, None, ALU.mult).then_inc(f_dve, 1)

                def tail_use(s, par, i):
                    kind, k = TAIL[i]
                    if kind == "C":
                        at_least(dve, ch_done, ev(s, 2, k))
                        nc.vector.tensor_tensor(cl[:, k, :], TL[:], ch[:, k, :].bitcast(F32), ALU.subtract
                                                ).then_inc(t_dve, 1)
                        return
                    at_least(dve, t_done, ev(s, NTAIL, i))
                    if kind == "N":
                        v = TL[:].rearrange("p (b h c) -> p b h c", b=TB, h=4)
                        nc.vector.reciprocal(rden[:], v[:, :, :, DH]).then_inc(r_done, 1)
                        dve.wait_ge(r_done, ev(s, 4, k))
                        nc.vector.tensor_tensor(ctxn[:, :, 4 * k:4 * k + 4, :], v[:, :, :, 0:DH],
                                                rden[:].unsqueeze(3).to_broadcast([P, TB, 4, DH]),
                                                ALU.mult).then_inc(t_dve, 1)
                    else:
                        at_least(dve, res_ready, ev(s, 1, 0))
                        nc.vector.tensor_tensor(xres[:, par, 2 * k:2 * k + 2, :],
                                                TL[:].rearrange("p (b h) -> p b h", b=2),
                                                xres[:, par, 2 * k:2 * k + 2, :], ALU.add).then_inc(t_dve, 1)

                def body(s, par, tail, core, front):
                    for u in range(NU):
                        if front and u == STAT_SLOT:
                            statistics(s + 1, 1 - par)
                        if front and u == VAR_SLOT:
                            variance(s + 1)
                        if front and u == ROOT_SLOT:
                            inverse_deviation(s + 1)
                        if front and u == NORM_SLOT:
                            normalise(s + 1, 1 - par)
                        for i in TAIL_AT.get(u, ()) if core else ():
                            tail_use(s, par, i)
                        for i in LATE_AT.get(u, ()) if tail else ():
                            tail_use(s - 1, 1 - par, i)
                        if isinstance(s, int) and s == -1 and u == WEIGHTS_SLOT:
                            dve.wait_ge(w_ready, 14)
                            for name, parts in (("kh", (1, 1, 0)), ("kl", (0, 0, 1)), ("qh", (1, 0, 1)), ("ql", (0, 1, 0))):
                                for i, used in enumerate(parts):
                                    nc.vector.tensor_copy(sel[name][:, :, i], sel0[:, :, i] if used else selz[:]).then_inc(dve_ready, 1)
                            nc.vector.tensor_reduce(pairmask[:], headmask[:].rearrange("p (a j) -> p j a", j=2), AX.X, ALU.add
                                                    ).then_inc(dve_ready, 1)
                            dve.wait_ge(w_high, 2)
                            nc.vector.tensor_tensor(wl[:], wraw[:], wh[:].bitcast(F32), ALU.subtract).then_inc(dve_ready, 1)
                            nc.vector.tensor_tensor(wol[:], oraw[:], woh[:].bitcast(F32), ALU.subtract).then_inc(dve_ready, 1)
                        for i in slot_front[NU + u] if core else ():
                            front_use(s, par, i)
                        if front:
                            for i in slot_front[u]:
                                front_use(s + 1, 1 - par, i)
                            for t in range(QT):
                                if u == K_AT[t]:
                                    half_k(s + 1, t)
                            for four in range(4):
                                if u == MASK_AT[four]:
                                    mask_q(s + 1, four)

                nc.vector.memset(selz[:], 0.0).then_inc(dve_ready, 1)
                nc.vector.memset(ks[ONES:ONES + 1].bitcast(F32), 1.0).then_inc(dve_ready, 1)
                dve.wait_ge(dve_ready, 2)
                iterations(dve, body)

            @block.tensor
            def _(pe):
                def three(out, ah, al, bh, bl, first, last):
                    pe.matmul(out, al, bh, start=first, stop=False)
                    pe.matmul(out, ah, bl, start=False, stop=False)
                    return pe.matmul(out, ah, bh, start=False, stop=last)

                def front_use(s, par, i):
                    kind, k = FRONT[i]
                    dst = FB[:, f_bank[i], :]
                    j, sj = f_before[i][0], s - f_before[i][1]
                    if by_act[j]:
                        at_least(pe, f_act, ev(sj, NFA, act_no[j]))
                    else:
                        at_least(pe, f_dve, ev(sj, NFD, dve_no[j]))
                    if kind == "T":
                        at_least(pe, ln_done, ev(s, 1, 0))
                        for b in range(TB):
                            ins = pe.transpose(dst[:, b * P:(b + 1) * P], xn[:, b, k * P:(k + 1) * P], ident[:])
                    elif kind in ("q", "k"):
                        if isinstance(s, int) and s == 0 and i == at["q", 0]:
                            pe.wait_ge(dve_ready, 17)
                        at_least(pe, f_dve, ev(s, NFD, dve_no[at["T", 1]]))
                        w = slice(k * P, (k + 1) * P) if kind == "q" else slice(H + k * P, H + (k + 1) * P)
                        for c in range(KT):
                            ins = three(dst, wh[:, c, w], wl[:, c, w], xh[:, c, :], xl[:, c, :], c == 0, c == KT - 1)
                    elif kind == "v":
                        for b in range(2):
                            w = slice((2 * k + b) * P, (2 * k + b + 1) * P)
                            for c in range(KT):
                                ins = three(dst[:, b * H:(b + 1) * H], xh[:, c, w], xl[:, c, w],
                                            wh[:, c, 2 * H:3 * H], wl[:, c, 2 * H:3 * H], c == 0, c == KT - 1)
                    elif kind in ("rk", "rq"):
                        c, t, a = kind[1], k // PT, k % PT
                        hi, lo = (kh, kl) if c == "k" else (qh, ql)
                        at_least(pe, f_dve, ev(s, NFD, dve_no[at[c, t]]))
                        pe.matmul(dst[0:ONES, :], sel[c + "h"][:, a].rearrange("p b c -> p (b c)"), hi[:, t, :],
                                  start=True, stop=False)
                        ins = pe.matmul(dst[0:ONES, :], sel[c + "l"][:, a].rearrange("p b c -> p (b c)"), lo[:, t, :],
                                        start=False, stop=True)
                    elif kind == "m":
                        heads, qb, k0, n = k
                        at_least(pe, q_masked, ev(s, 4, heads[-1] // 4))
                        at_least(pe, k_half, ev(s, QT, heads[-1] // HT))
                        for j, h in enumerate(heads):
                            o = dst[:, j * n:(j + 1) * n]
                            pe.matmul(o, qb16[:, h, qb * P:(qb + 1) * P], kb16[:, h // HT, k0:k0 + n],
                                      start=True, stop=(h < GLOBAL))
                            if h < GLOBAL:
                                ins = pe.matmul(o[:, n - P:n], identb[:], mask_g[:], start=False, stop=True,
                                                skip_group_check=True)
                            else:
                                ins = pe.matmul(o, identb[:], mask_l[:, BAND - n:BAND], start=False, stop=True)
                    else:
                        h0, h1 = (0, GLOBAL) if k == 0 else (GLOBAL, HEADS)
                        at_least(pe, f_dve, ev(s, NFD, dve_no[at["m", (MAXG, MAXL)[k][-1]]]))
                        for b in range(TB):
                            ins = pe.transpose(dst[0:h1 - h0, b * P:(b + 1) * P], mx[:, h0:h1, b], ident[:])
                    ins.then_inc(f_done, 1)

                def scores(s, par, u):
                    t, kb, heads, n = UNITS[u]
                    at_least(pe, m_row, 16 * (2 * s + (1 if heads[0] < GLOBAL else 2)))
                    if u == t_first[t]:
                        by = [i for i in range(NF) if FRONT[i][0] in ("rk", "rq") and FRONT[i][1] // 2 == t]
                        at_least(pe, f_act, ev(s, NFA, act_no[[i for i in by if by_act[i]][-1]]))
                        if not all(by_act[i] for i in by):
                            at_least(pe, f_dve, ev(s, NFD, dve_no[[i for i in by if not by_act[i]][-1]]))
                    for b in range(2):
                        h = heads[b * len(heads) // 2]
                        nh = len(heads) // 2
                        i = 2 * u + b
                        j, sj = s_before[i][0], s - s_before[i][1]
                        at_least(pe, e_done, ev(sj, 2 * NU, j))
                        ins = pe.matmul(S[:, s_bank[i], 0:nh * n], ks[0:ONES + 1, h // 2, kb * P:(kb + 1) * P],
                                        qs[0:ONES + 1, h:h + nh, kb * P:kb * P + n], start=True, stop=True)
                        ins.then_inc(s_done, 1)

                def context(s, par, u):
                    t, kb, heads, n = UNITS[u]
                    at_least(pe, p_done, ev(s, NU, u))
                    if u == t_first[t]:
                        at_least(pe, pv_out, ev(s, 4, t - 1) if t else ev(s - 1, 4, 3))
                    at_least(pe, f_dve, ev(s, NFD, dve_no[at["v", 1]]))
                    for j, h in enumerate(heads):
                        r = VW * (h % 4)
                        ins = pe.matmul(PV[r:r + VW, kb * P:kb * P + n], vv[:, par, kb, h, :],
                                        pt[:, u % 4, j * n:(j + 1) * n], start=(kb == 0), stop=(kb == TB - 1),
                                        skip_group_check=True)
                    ins.then_inc(pv_done, 1)

                def tail_use(s, i):
                    kind, k = TAIL[i]
                    j, sj = (i - 1, s) if i else (NTAIL - 1, s - 1)
                    at_least(pe, t_dve, ev(sj, NTAIL, j))
                    if kind == "N":
                        at_least(pe, pv_out, ev(s, 4, k))
                        for b in range(TB):
                            ins = pe.transpose(TL[:, b * P:(b + 1) * P], pvs[:, k % 2, b * P:(b + 1) * P], ident[:])
                    elif kind == "C":
                        cn = ctxn[:].rearrange("p b h d -> p b (h d)")
                        at_least(pe, t_dve, ev(s, NTAIL, N_AT[2 * k + 1]))
                        for b in range(TB):
                            ins = pe.transpose(TL[:, b * P:(b + 1) * P], cn[:, b, k * P:(k + 1) * P], ident[:])
                    else:
                        at_least(pe, t_dve, ev(s, NTAIL, C_AT[1]))
                        for b in range(2):
                            w = slice((2 * k + b) * P, (2 * k + b + 1) * P)
                            for c in range(KT):
                                ins = three(TL[:, b * H:(b + 1) * H], ch[:, c, w], cl[:, c, w], woh[:, c, :],
                                            wol[:, c, :], c == 0, c == KT - 1)
                    ins.then_inc(t_done, 1)

                def body(s, par, tail, core, front):
                    for u in range(NU):
                        def fronts():
                            for i in slot_front[NU + u] if core else ():
                                front_use(s, par, i)
                            if front:
                                for i in slot_front[u]:
                                    front_use(s + 1, 1 - par, i)

                        if u in PE_FIRST:
                            fronts()
                        if core:
                            scores(s, par, u)
                        if tail and u < 2:
                            context(s - 1, 1 - par, NU - 2 + u)
                        if core and u >= 2:
                            context(s, par, u - 2)
                        for i in TAIL_AT.get(u, ()) if core else ():
                            tail_use(s, i)
                        for i in LATE_AT.get(u, ()) if tail else ():
                            tail_use(s - 1, i)
                        if u not in PE_FIRST:
                            fronts()

                pe.wait_ge(w_ready, 14)
                iterations(pe, body)


F32R = mybir.dt.float32r

EXPERTS, GROUPS, TOP_GROUPS, TOP_K, SCALE = 16, 4, 2, 4, 2.5
NE = EXPERTS + 2
PER_GROUP = EXPERTS // GROUPS
RAW = 4
LO_ROW = 32


def phase_f(nc, tag, x_in, x_out, w_gate, bias_corr, w1, w2, nseq):
    with ExitStack() as ctx:
        def sb(name, shape, dt=F32):
            return ctx.enter_context(nc.sbuf_tensor(tag + name, shape, dt))

        def ps(name, shape):
            return ctx.enter_context(nc.psum_tensor(tag + name, shape, F32))

        def sem(name):
            return ctx.enter_context(nc.semaphore(tag + name))

        ident = sb("ident", [P, P])
        raw = sb("raw", [P, RAW, 1152])
        w1h, w1l = sb("w1h", [P, KT, NE * P], F32R), sb("w1l", [P, KT, NE * P], F32R)
        w2h, w2l = sb("w2h", [P, NE * H], F32R), sb("w2l", [P, NE * H], F32R)
        graw = sb("graw", [P, KT, EXPERTS])
        wgh, wgl = sb("wgh", [P, KT, EXPERTS], F32R), sb("wgl", [P, KT, EXPERTS], F32R)
        bias = sb("bias", [P, EXPERTS])
        spread0 = sb("spread0", [P, EXPERTS, P])
        spread = sb("spread", [P, EXPERTS, P], F32R)
        tri = sb("tri", [P, EXPERTS, EXPERTS])
        xin, xres = sb("xin", [P, 2, TB, H]), sb("xres", [P, 2, TB, H])
        stats, mean, var = sb("stats", [P, TB, 6]), sb("mean", [P, TB]), sb("var", [P, TB])
        lnv, guess, yy, rstd = sb("lnv", [P, TB]), sb("guess", [P, TB]), sb("yy", [P, TB]), sb("rstd", [P, TB])
        xn = sb("xn", [P, TB, H])
        xh, xl = sb("xh", [P, 2, KT, SEQ], F32R), sb("xl", [P, 2, KT, SEQ], F32R)
        logT = sb("logT", [P, SEQ])
        sc = sb("sc", [P, TB, EXPERTS])
        choice = sb("choice", [P, TB, EXPERTS])
        pair_hi, pair_lo = sb("pair_hi", [P, TB * GROUPS, 2]), sb("pair_lo", [P, TB * GROUPS, 2])
        g1, g2, g3 = sb("g1", [P, TB * GROUPS]), sb("g2", [P, TB * GROUPS]), sb("g3", [P, TB * GROUPS])
        gcmp, geq = sb("gcmp", [P, TB * GROUPS, GROUPS]), sb("geq", [P, TB * GROUPS, GROUPS])
        gsel = sb("gsel", [P, TB * GROUPS])
        cmp_, eq = sb("cmp", [P, TB * EXPERTS, EXPERTS]), sb("eq", [P, TB * EXPERTS, EXPERTS])
        rank = sb("rank", [P, TB, EXPERTS])
        wsum, winv = sb("wsum", [P, TB]), sb("winv", [P, TB])
        cw = sb("cw", [P, TB, EXPERTS])
        cT0 = sb("cT0", [P, SEQ])
        cT = sb("cT", [P, 2, SEQ], F32R)
        r = sb("r", [P, 2, SEQ])
        u = sb("u", [P, 2, SEQ])
        g = sb("g", [P, 2, SEQ])
        gh, gl = sb("gh", [P, 3, SEQ], F32R), sb("gl", [P, 3, SEQ], F32R)
        yT = sb("yT", [P, KT, SEQ])

        p_loaded = [sem("p_loaded%d" % i) for i in range(RAW)]
        g_loaded = sem("g_loaded")
        g_high, g_low = sem("g_high"), sem("g_low")
        Z = ps("Z", [P, 2, 512])
        B = ps("B", [P, 2, 512])
        Y = ps("Y", [P, KT, 512])
        FB = ps("FB", [P, 2, 512])

        names = ("w_split const dconst x_loaded res_ready ln_stat ln_var ln_log ln_guess ln_done t_done "
                 "xh_done xl_done l_done lT_done lt_done ex_done route cw_done ct_done ch_done cl_done z_done "
                 "r_done b_done u_done g_done gh_done gl_done y_done ye_done fin_done out_done x_stored a_split").split()
        (w_split, const, dconst, x_loaded, res_ready, ln_stat, ln_var, ln_log, ln_guess, ln_done, t_done,
         xh_done, xl_done, l_done, lT_done, lt_done, ex_done, route, cw_done, ct_done, ch_done, cl_done, z_done,
         r_done, b_done, u_done, g_done, gh_done, gl_done, y_done, ye_done, fin_done, out_done, x_stored,
         a_split) = [sem(n) for n in names]

        NSTAT, NROUTE = TB + 10, 24
        RES_SLOT = 8
        STAT_SLOT, LN_SLOT, FIN_SLOT, T_SLOT, L_SLOT, LT_SLOT, ROUTE_SLOT, CT_SLOT = 0, 1, 3, 5, 7, 8, 9, 16
        PIECE_SLOT = (3, 5, 6, 7, 9, 10, 11, 12)

        CH = 1152
        pieces = ([(w1h, w1l, k, c) for k in range(KT) for c in range(0, NE * P, CH)] +
                  [(w2h, w2l, None, c) for c in range(0, NE * H, CH)])

        def piece(t, k, c):
            return t[:, c:c + CH] if k is None else t[:, k, c:c + CH]

        with nc.Block() as block:
            def iterations(eng, body):
                body(-1, 1, False, False, True)
                body(0, 0, False, True, True)
                with eng.Fori(1, nseq - 3, 2) as reg:
                    body(reg, 1, True, True, True)
                    body(reg + 1, 0, True, True, True)
                body(nseq - 3, 1, True, True, True)
                body(nseq - 2, 0, True, True, True)
                body(nseq - 1, 1, True, True, False)
                body(nseq, 0, True, False, False)

            def pieces_at(s, e):
                return [i for i in range(len(pieces)) if isinstance(s, int) and s == -1 and PIECE_SLOT[i] == e]

            @block.sync
            def _(sp):
                def load(s, par):
                    rows = seq_rows(sp, x_in, s)
                    read, loaded = in_register(sp, ev(s - 2, 1, 0)), in_register(sp, 16 * s)
                    at_least(sp, ln_done, read)
                    at_least(sp, res_ready, read)
                    at_least(sp, x_loaded, loaded)
                    sp.dma_start(xin[:, par], rows).then_inc(x_loaded, 16)

                def body(s, par, end, core, front):
                    if end:
                        rows = seq_rows(sp, x_out, s - 1)
                        summed, stored = in_register(sp, ev(s - 1, 2, 1)), in_register(sp, 16 * s)
                        at_least(sp, out_done, summed)
                        sp.dma_start(rows, xres[:, 1 - par]).then_inc(x_stored, 16)
                        at_least(sp, x_stored, stored)
                    if not isinstance(s, int) or 2 <= s + 2 < nseq:
                        load(s + 2, par)

                sp.dma_start(xin[:, 0], seq_rows(sp, x_in, 0)).then_inc(x_loaded, 16)
                sp.dma_start(graw[:], w_gate.rearrange("(k p) e -> p k e", p=P)).then_inc(g_loaded, 16)
                sp.dma_start(bias[:], row_broadcast(bias_corr)).then_inc(g_loaded, 16)
                for i, (_, _, k, c) in enumerate(pieces):
                    at_least(sp, w_split, i + 1 - RAW)
                    src = w2[:, c:c + CH] if k is None else w1[k * P:(k + 1) * P, c:c + CH]
                    sp.dma_start(raw[:, i % RAW], src).then_inc(p_loaded[i % RAW], 16)
                sp.wait_ge(x_loaded, 16)
                sp.dma_start(xin[:, 1], seq_rows(sp, x_in, 1)).then_inc(x_loaded, 16)
                iterations(sp, body)
                sp.wait_ge(x_stored, 16 * nseq)

            @block.gpsimd
            def _(pool):
                def gate(s, e):
                    at_least(pool, r_done, ev(s, NE, e))
                    if e < EXPERTS:
                        at_least(pool, u_done, ev(s, EXPERTS, e))
                    at_least(pool, gl_done, ev(s, NE, e - 2))
                    a = u if e < EXPERTS else r
                    nc.gpsimd.tensor_tensor(g[:, e % 2], a[:, e % 2], r[:, e % 2], ALU.mult).then_inc(g_done, 1)

                def body(s, par, end, core, front):
                    for e in range(NE):
                        if core:
                            gate(s, e)

                nc.gpsimd.memset(ident[:], 0.0).then_inc(const, 1)
                nc.gpsimd.memset(tri[:], 1.0).then_inc(const, 1)
                pool.wait_ge(const, 2)
                nc.gpsimd.affine_select(out=ident[:], in_=ident[:], compare_op=ALU.not_equal, fill=1.0,
                                        base=0, pattern=[[-1, P]], channel_multiplier=1).then_inc(const, 1)
                nc.gpsimd.affine_select(out=tri[:], in_=tri[:], compare_op=ALU.is_gt, fill=0.0,
                                        base=0, pattern=[[1, EXPERTS], [-1, EXPERTS]], channel_multiplier=0
                                        ).then_inc(const, 1)
                pool.wait_ge(const, 4)
                nc.gpsimd.memset(spread0[:], 0.0).then_inc(const, 1)
                for row in (0, LO_ROW):
                    pool.wait_ge(const, 6 if row else 5)
                    nc.gpsimd.affine_select(out=spread0[:], in_=spread0[:], compare_op=ALU.not_equal, fill=1.0,
                                            base=-row, pattern=[[-1, EXPERTS], [0, P]], channel_multiplier=1
                                            ).then_inc(const, 1)
                for i, (hi, lo, k, c) in enumerate(pieces):
                    pool.wait_ge(a_split, i + 1)
                    nc.gpsimd.tensor_tensor(piece(lo, k, c), raw[:, i % RAW], piece(hi, k, c).bitcast(F32),
                                            ALU.subtract).then_inc(w_split, 1)
                iterations(pool, body)

            @block.scalar
            def _(act):
                def body(s, par, end, core, front):
                    for e in range(NE):
                        if end and e == 2:
                            at_least(act, y_done, ev(s - 1, NE, NE - 1))
                            nc.scalar.copy(yT[:, 0], Y[:, 0]).then_inc(ye_done, 1)
                        if core:
                            at_least(act, z_done, ev(s, NE, e))
                            at_least(act, g_done, ev(s, NE, e - 2))
                            nc.scalar.activation(r[:, e % 2], Z[:, e % 2], ACT.Relu).then_inc(r_done, 1)
                        if end and e == 0:
                            high(s - 1, NE - 1)
                        if core and e >= 1:
                            high(s, e - 1)
                        if isinstance(s, int) and s == -1 and e == LT_SLOT:
                            act.wait_ge(const, 7)
                            nc.scalar.copy(spread[:], spread0[:]).then_inc(g_high, 1)
                        for i in pieces_at(s, e):
                            hi, _, k, c = pieces[i]
                            act.wait_ge(p_loaded[i % RAW], 16 * (i // RAW + 1))
                            nc.scalar.copy(piece(hi, k, c), raw[:, i % RAW]).then_inc(a_split, 1)
                        if not front:
                            continue
                        n, np_ = s + 1, 1 - par
                        if e == LN_SLOT:
                            at_least(act, ln_var, ev(n, 1, 0))
                            nc.scalar.activation(lnv[:], var[:], ACT.Ln).then_inc(ln_log, 1)
                        if e == LN_SLOT + 1:
                            at_least(act, ln_log, ev(n, 1, 0))
                            nc.scalar.activation(guess[:], lnv[:], ACT.Exp, scale=-0.5).then_inc(ln_guess, 1)
                        if e == RES_SLOT:
                            at_least(act, x_loaded, 16 * (n + 1))
                            at_least(act, x_stored, 16 * (n - 1))
                            nc.scalar.copy(xres[:, np_], xin[:, np_]).then_inc(res_ready, 1)
                        if e in (T_SLOT, T_SLOT + 1):
                            k = e - T_SLOT
                            at_least(act, t_done, ev(n, KT, k))
                            at_least(act, z_done, ev(n - 2, NE, NE - 1))
                            nc.scalar.copy(xh[:, np_, k], FB[:, k]).then_inc(xh_done, 1)
                        if e == L_SLOT:
                            at_least(act, l_done, ev(n, 1, 0))
                            nc.scalar.copy(logT[0:EXPERTS], FB[0:EXPERTS, 0]).then_inc(lT_done, 1)
                        if e == LT_SLOT:
                            at_least(act, lt_done, ev(n, 1, 0))
                            nc.scalar.activation(sc[:], FB[:, 1].rearrange("p (b e) -> p b e", b=TB)[:, :, 0:EXPERTS],
                                                 ACT.Exp, scale=-1.0).then_inc(ex_done, 1)
                        if e == CT_SLOT:
                            at_least(act, ct_done, ev(n, 1, 0))
                            at_least(act, b_done, ev(n - 2, EXPERTS, EXPERTS - 1))
                            nc.scalar.copy(cT[0:EXPERTS, np_], FB[0:EXPERTS, 0]).then_inc(ch_done, 1)

                def high(s, e):
                    at_least(act, g_done, ev(s, NE, e))
                    at_least(act, y_done, ev(s, NE, e - 3))
                    nc.scalar.copy(gh[:, e % 3], g[:, e % 2]).then_inc(gh_done, 1)

                act.wait_ge(g_loaded, 32)
                nc.scalar.copy(wgh[:], graw[:]).then_inc(g_high, 1)
                act.wait_ge(dconst, 4)
                iterations(act, body)

            @block.vector
            def _(dve):
                def low(s, e):
                    at_least(dve, gh_done, ev(s, NE, e))
                    nc.vector.tensor_tensor(gl[:, e % 3], g[:, e % 2], gh[:, e % 3].bitcast(F32),
                                            ALU.subtract).then_inc(gl_done, 1)

                def statistics(s, par):
                    at_least(dve, x_loaded, 16 * (s + 1))
                    for b in range(TB):
                        nc.vector.bn_stats(stats[:, b, :], xin[:, par, b, :]).then_inc(ln_stat, 1)

                def variance(s):
                    m0, m1, q0, q1 = (stats[:, :, c] for c in (1, 4, 2, 5))
                    dve.wait_ge(ln_stat, ev(s, NSTAT, TB - 1))
                    nc.vector.tensor_tensor(mean[:], m0, m1, ALU.add).then_inc(ln_stat, 1)
                    nc.vector.tensor_tensor(yy[:], m0, m1, ALU.subtract).then_inc(ln_stat, 1)
                    nc.vector.tensor_tensor(var[:], q0, q1, ALU.add).then_inc(ln_stat, 1)
                    dve.wait_ge(ln_stat, ev(s, NSTAT, TB + 2))
                    nc.vector.tensor_scalar(mean[:], mean[:], 0.5, None, ALU.mult).then_inc(ln_stat, 1)
                    nc.vector.tensor_tensor(yy[:], yy[:], yy[:], ALU.mult).then_inc(ln_stat, 1)
                    nc.vector.tensor_scalar(var[:], var[:], 1.0 / H, EPS, ALU.mult, ALU.add).then_inc(ln_stat, 1)
                    dve.wait_ge(ln_stat, ev(s, NSTAT, TB + 5))
                    nc.vector.scalar_tensor_tensor(out=var[:], in0=yy[:], scalar=0.25, in1=var[:],
                                                   op0=ALU.mult, op1=ALU.add).then_inc(ln_var, 1)

                def inverse_deviation(s):
                    at_least(dve, ln_guess, ev(s, 1, 0))
                    nc.vector.tensor_tensor(yy[:], guess[:], guess[:], ALU.mult).then_inc(ln_stat, 1)
                    dve.wait_ge(ln_stat, ev(s, NSTAT, TB + 6))
                    nc.vector.tensor_tensor(yy[:], yy[:], var[:], ALU.mult).then_inc(ln_stat, 1)
                    dve.wait_ge(ln_stat, ev(s, NSTAT, TB + 7))
                    nc.vector.tensor_scalar(yy[:], yy[:], -0.5, 1.5, ALU.mult, ALU.add).then_inc(ln_stat, 1)
                    dve.wait_ge(ln_stat, ev(s, NSTAT, TB + 8))
                    nc.vector.tensor_tensor(rstd[:], guess[:], yy[:], ALU.mult).then_inc(ln_stat, 1)

                def normalise(s, par):
                    dve.wait_ge(ln_stat, ev(s, NSTAT, TB + 9))
                    at_least(dve, t_done, ev(s - 1, KT, KT - 1))
                    for b in range(TB):
                        ins = nc.vector.tensor_scalar(xn[:, b, :], xin[:, par, b, :], mean[:, b:b + 1],
                                                      rstd[:, b:b + 1], ALU.subtract, ALU.mult)
                    ins.then_inc(ln_done, 1)

                def routing(s, part):
                    n = [0, 9, 15, 16, 17, 18, 20][part]

                    def step(ins):
                        nonlocal n
                        ins.then_inc(route, 1)
                        n += 1

                    def seen():
                        dve.wait_ge(route, ev(s, NROUTE, n - 1))

                    bg = "p (b g) -> p b g"
                    if part == 0:
                        at_least(dve, ex_done, ev(s, 1, 0))
                        step(nc.vector.tensor_scalar(sc[:], sc[:], 1.0, None, ALU.add))
                        seen()
                        step(nc.vector.reciprocal(sc[:], sc[:]))
                        seen()
                        step(nc.vector.tensor_tensor(choice[:], sc[:], bias[:].unsqueeze(1).to_broadcast([P, TB, EXPERTS]),
                                                     ALU.add))
                        v = choice[:].rearrange("p b (g q t) -> p (b g) q t", g=GROUPS, t=2)
                        seen()
                        step(nc.vector.tensor_tensor(pair_hi[:], v[:, :, :, 0], v[:, :, :, 1], ALU.max))
                        step(nc.vector.tensor_tensor(pair_lo[:], v[:, :, :, 0], v[:, :, :, 1], ALU.min))
                        seen()
                        step(nc.vector.tensor_tensor(g1[:], pair_hi[:, :, 0], pair_hi[:, :, 1], ALU.max))
                        step(nc.vector.tensor_tensor(g2[:], pair_hi[:, :, 0], pair_hi[:, :, 1], ALU.min))
                        step(nc.vector.tensor_tensor(g3[:], pair_lo[:, :, 0], pair_lo[:, :, 1], ALU.max))
                        seen()
                        step(nc.vector.tensor_tensor(g2[:], g2[:], g3[:], ALU.max))
                        assert n == 9
                    if part == 1:
                        if isinstance(s, int) and s == 0:
                            dve.wait_ge(const, 4)
                        seen()
                        step(nc.vector.tensor_tensor(g1[:], g1[:], g2[:], ALU.add))
                        seen()
                        mine = g1[:].unsqueeze(2).to_broadcast([P, TB * GROUPS, GROUPS])
                        for b in range(TB):
                            other = g1[:, b * GROUPS:(b + 1) * GROUPS].unsqueeze(1).to_broadcast([P, GROUPS, GROUPS])
                            w = slice(b * GROUPS, (b + 1) * GROUPS)
                            nc.vector.tensor_tensor(gcmp[:, w], other, mine[:, w], ALU.is_gt)
                            i2 = nc.vector.tensor_tensor(geq[:, w], other, mine[:, w], ALU.is_equal)
                        step(i2)
                        seen()
                        t4 = tri[:, 0:GROUPS, 0:GROUPS].unsqueeze(1).to_broadcast([P, TB, GROUPS, GROUPS])
                        step(nc.vector.tensor_tensor(geq[:].rearrange("p (b g) f -> p b g f", b=TB),
                                                     geq[:].rearrange("p (b g) f -> p b g f", b=TB), t4, ALU.mult))
                        seen()
                        step(nc.vector.tensor_tensor(gcmp[:], gcmp[:], geq[:], ALU.add))
                        seen()
                        step(nc.vector.tensor_reduce(gsel[:], gcmp[:], AX.X, ALU.add))
                        seen()
                        step(nc.vector.tensor_scalar(gsel[:], gsel[:], TOP_GROUPS - 0.5, None, ALU.is_lt))
                        assert n == 15
                    if part == 2:
                        seen()
                        v = choice[:].rearrange("p b (g q) -> p (b g) q", g=GROUPS)
                        step(nc.vector.tensor_tensor(v, v, gsel[:].unsqueeze(2).to_broadcast([P, TB * GROUPS, PER_GROUP]),
                                                     ALU.mult))
                    if part in (2, 3):
                        if part == 2:
                            seen()
                        for b in range(2 * (part - 2), 2 * (part - 1)):
                            w = slice(b * EXPERTS, (b + 1) * EXPERTS)
                            other = choice[:, b].unsqueeze(1).to_broadcast([P, EXPERTS, EXPERTS])
                            mine = choice[:, b].unsqueeze(2).to_broadcast([P, EXPERTS, EXPERTS])
                            nc.vector.tensor_tensor(cmp_[:, w], other, mine, ALU.is_gt)
                            i2 = nc.vector.tensor_tensor(eq[:, w], other, mine, ALU.is_equal)
                        if part == 3:
                            step(i2)
                    if part == 4:
                        seen()
                        t4 = tri[:].unsqueeze(1).to_broadcast([P, TB, EXPERTS, EXPERTS])
                        e4 = eq[:].rearrange("p (b g) f -> p b g f", b=TB)
                        step(nc.vector.tensor_tensor(e4, e4, t4, ALU.mult))
                    if part == 5:
                        seen()
                        step(nc.vector.tensor_tensor(cmp_[:], cmp_[:], eq[:], ALU.add))
                        seen()
                        step(nc.vector.tensor_reduce(rank[:].rearrange("p b e -> p (b e)"), cmp_[:], AX.X, ALU.add))
                        assert n == 20
                    if part == 6:
                        seen()
                        step(nc.vector.scalar_tensor_tensor(out=rank[:], in0=rank[:], scalar=TOP_K - 0.5, in1=sc[:],
                                                            op0=ALU.is_lt, op1=ALU.mult))
                        seen()
                        step(nc.vector.tensor_reduce(wsum[:], rank[:], AX.X, ALU.add))
                        seen()
                        step(nc.vector.tensor_scalar(wsum[:], wsum[:], 1e-20, None, ALU.add))
                        seen()
                        step(nc.vector.reciprocal(winv[:], wsum[:]))
                        seen()
                        assert n == NROUTE
                        nc.vector.scalar_tensor_tensor(out=cw[:], in0=rank[:], scalar=SCALE,
                                                       in1=winv[:].unsqueeze(2).to_broadcast([P, TB, EXPERTS]),
                                                       op0=ALU.mult, op1=ALU.mult).then_inc(cw_done, 1)

                def body(s, par, end, core, front):
                    n, np_ = s + 1, 1 - par
                    for e in range(NE):
                        if end and e == 2:
                            at_least(dve, y_done, ev(s - 1, NE, NE - 1))
                            nc.vector.tensor_copy(yT[:, 1], Y[:, 1]).then_inc(ye_done, 1)
                        if core and e < EXPERTS:
                            at_least(dve, r_done, ev(s, NE, e))
                            at_least(dve, b_done, ev(s, EXPERTS, e))
                            nc.vector.tensor_tensor(u[:, e % 2], r[:, e % 2], B[:, e % 2], ALU.mult).then_inc(u_done, 1)
                        if end and e == 0:
                            low(s - 1, NE - 1)
                        if core and e >= 1:
                            low(s, e - 1)
                        if end and e in (FIN_SLOT, FIN_SLOT + 1):
                            k = e - FIN_SLOT
                            at_least(dve, fin_done, ev(s - 1, 2, k))
                            at_least(dve, res_ready, ev(s - 1, 1, 0))
                            xr = xres[:, np_, 2 * k:2 * k + 2, :]
                            nc.vector.tensor_tensor(xr, FB[:, k].rearrange("p (b h) -> p b h", b=2), xr,
                                                    ALU.add).then_inc(out_done, 1)
                        if not front:
                            continue
                        if e == STAT_SLOT:
                            statistics(n, np_)
                        if e == STAT_SLOT + 1:
                            variance(n)
                        if e == LN_SLOT + 2:
                            inverse_deviation(n)
                        if e == LN_SLOT + 3:
                            normalise(n, np_)
                        if e in (T_SLOT, T_SLOT + 1):
                            k = e - T_SLOT
                            at_least(dve, xh_done, ev(n, KT, k))
                            nc.vector.tensor_tensor(xl[:, np_, k], FB[:, k], xh[:, np_, k].bitcast(F32),
                                                    ALU.subtract).then_inc(xl_done, 1)
                        if ROUTE_SLOT <= e < ROUTE_SLOT + 7:
                            routing(n, e - ROUTE_SLOT)
                        if e == CT_SLOT:
                            at_least(dve, ch_done, ev(n, 1, 0))
                            nc.vector.tensor_tensor(cT[LO_ROW:LO_ROW + EXPERTS, np_], FB[0:EXPERTS, 0],
                                                    cT[0:EXPERTS, np_].bitcast(F32), ALU.subtract).then_inc(cl_done, 1)

                nc.vector.memset(logT[:], 0.0).then_inc(dconst, 1)
                nc.vector.memset(cT0[:], 0.0).then_inc(dconst, 1)
                dve.wait_ge(dconst, 2)
                for par in range(2):
                    nc.vector.tensor_copy(cT[:, par], cT0[:]).then_inc(dconst, 1)
                dve.wait_ge(g_high, 1)
                nc.vector.tensor_tensor(wgl[:], graw[:], wgh[:].bitcast(F32), ALU.subtract).then_inc(g_low, 1)
                iterations(dve, body)

            @block.tensor
            def _(pe):
                def three(out, wh, wl, vh, vl, first, last):
                    pe.matmul(out, wl, vh, start=first, stop=False)
                    pe.matmul(out, wh, vl, start=False, stop=False)
                    return pe.matmul(out, wh, vh, start=False, stop=last)

                def hidden(s, par, e):
                    at_least(pe, r_done, ev(s, NE, e - 2))
                    if isinstance(s, int) and s == 0 and e == 0:
                        pe.wait_ge(w_split, len(pieces))
                        pe.wait_ge(g_high, 2)
                    if e == 0:
                        at_least(pe, xl_done, ev(s, KT, KT - 1))
                    c = slice(e * P, (e + 1) * P)
                    for k in range(KT):
                        ins = three(Z[:, e % 2], w1h[:, k, c], w1l[:, k, c], xh[:, par, k], xl[:, par, k],
                                    k == 0, k == KT - 1)
                    ins.then_inc(z_done, 1)
                    if e < EXPERTS:
                        at_least(pe, u_done, ev(s, EXPERTS, e - 2))
                        if e == 0:
                            at_least(pe, cl_done, ev(s, 1, 0))
                        pe.matmul(B[:, e % 2], spread[:, e], cT[:, par], start=True, stop=True).then_inc(b_done, 1)

                def out_(s, e):
                    at_least(pe, gl_done, ev(s, NE, e))
                    if e == 0:
                        at_least(pe, ye_done, ev(s - 1, 2, 1))
                    for k in range(KT):
                        c = slice(e * H + k * P, e * H + (k + 1) * P)
                        ins = three(Y[:, k], w2h[:, c], w2l[:, c], gh[:, e % 3], gl[:, e % 3], e == 0, e == NE - 1)
                    ins.then_inc(y_done, 1)

                def body(s, par, end, core, front):
                    n, np_ = s + 1, 1 - par
                    for e in range(NE):
                        if core:
                            hidden(s, par, e)
                        if end and e < 2:
                            out_(s - 1, NE - 2 + e)
                        if core and e >= 2:
                            out_(s, e - 2)
                        if end and e in (FIN_SLOT, FIN_SLOT + 1):
                            k = e - FIN_SLOT
                            at_least(pe, ye_done, ev(s - 1, 2, 1))
                            if k == 0:
                                at_least(pe, cl_done, ev(s, 1, 0) if core else ev(s - 1, 1, 0))
                            else:
                                at_least(pe, ex_done, ev(s, 1, 0) if core else ev(s - 1, 1, 0))
                            for b in range(2):
                                for c in range(KT):
                                    ins = pe.transpose(FB[:, k, b * H + c * P:b * H + (c + 1) * P],
                                                       yT[:, c, (2 * k + b) * P:(2 * k + b + 1) * P], ident[:])
                            ins.then_inc(fin_done, 1)
                        if not front:
                            continue
                        if e in (T_SLOT, T_SLOT + 1):
                            k = e - T_SLOT
                            at_least(pe, ln_done, ev(n, 1, 0))
                            if end:
                                at_least(pe, out_done, ev(s - 1, 2, k))
                            elif not isinstance(s, int) or s >= 0:
                                at_least(pe, cl_done, ev(s, 1, 0))
                            for b in range(TB):
                                ins = pe.transpose(FB[:, k, b * P:(b + 1) * P], xn[:, b, k * P:(k + 1) * P], ident[:])
                            ins.then_inc(t_done, 1)
                        if e == L_SLOT:
                            at_least(pe, xl_done, ev(n, KT, KT - 1))
                            for k in range(KT):
                                ins = three(FB[0:EXPERTS, 0], wgh[:, k], wgl[:, k], xh[:, np_, k], xl[:, np_, k],
                                            k == 0, k == KT - 1)
                            ins.then_inc(l_done, 1)
                        if e == LT_SLOT:
                            at_least(pe, lT_done, ev(n, 1, 0))
                            for b in range(TB):
                                ins = pe.transpose(FB[:, 1, b * P:(b + 1) * P], logT[:, b * P:(b + 1) * P], ident[:])
                            ins.then_inc(lt_done, 1)
                        if e == CT_SLOT:
                            at_least(pe, cw_done, ev(n, 1, 0))
                            for b in range(TB):
                                ins = pe.transpose(FB[0:EXPERTS, 0, b * P:(b + 1) * P], cw[:, b, :], ident[:])
                            ins.then_inc(ct_done, 1)

                pe.wait_ge(const, 4)
                pe.wait_ge(g_low, 1)
                iterations(pe, body)


D = 512
DT = D // P
NC = SEQ // P


def phase_b(nc, x_in, x_out, w_in, b_q, b_k, b_v, b_g, w_o, b_o, nseq):
    NP = 4 * DT
    FRONT = [("T", 0), ("T", 1)] + [(c, i) for c in "qkvg" for i in range(DT)]
    NF = len(FRONT)
    FRONT_SLOT = (2, 3, 4, 5, 6, 7, 8, 9, 10, 11, 12, 13, 14, 15, 16, 17, 18, 19)
    FRONT_AT = {e: [i for i in range(NF) if FRONT_SLOT[i] == e] for e in FRONT_SLOT}
    NSLOT = 4 + NP
    by_act = [c in "qkg" for c, _ in FRONT]
    act_no = [sum(by_act[:i]) for i in range(NF)]
    dve_no = [i - act_no[i] for i in range(NF)]
    NFA, NFD = sum(by_act), NF - sum(by_act)
    RAW = 2
    PIECE_SLOT = (0, 1, 4, 7, 12)
    BIASES = 16 * (3 * DT + 2)
    STAT_SLOT, VAR_SLOT, LOG_SLOT, GUESS_SLOT, ROOT_SLOT, NORM_SLOT = 8, 10, 10, 10, 12, 12
    D_SLOT, O_SLOT, PT_SLOT, PV_SLOT, W_SLOT, FIN_SLOT = 0, 3, 4, 5, 7, 13
    OFF = [P * (NC - 1 - kb) for kb in range(NC - 1)]
    START = [0, NC * P, NC * P + (NC - 1) * P, NC * P + (2 * NC - 3) * P]

    with ExitStack() as ctx:
        def sb(name, shape, dt=F32):
            return ctx.enter_context(nc.sbuf_tensor("b_" + name, shape, dt))

        def ps(name, shape):
            return ctx.enter_context(nc.psum_tensor("b_" + name, shape, F32))

        def sem(name):
            return ctx.enter_context(nc.semaphore("b_" + name))

        ident, maskc = sb("ident", [P, P]), sb("maskc", [P, P])
        raw = sb("raw", [P, RAW, 1024])
        wh, wl = sb("wh", [P, KT, 4 * D], F32R), sb("wl", [P, KT, 4 * D], F32R)
        woh, wol = sb("woh", [P, DT * H], F32R), sb("wol", [P, DT * H], F32R)
        bq, bk, bg = sb("bq", [P, DT]), sb("bk", [P, DT]), sb("bg", [P, DT])
        bv, bo = sb("bv", [P, D]), sb("bo", [P, H])
        xin, xres = sb("xin", [P, 2, TB, H]), sb("xres", [P, 2, TB, H])
        stats, mean, var = sb("stats", [P, TB, 6]), sb("mean", [P, TB]), sb("var", [P, TB])
        lnv, guess, yy, rstd = sb("lnv", [P, TB]), sb("guess", [P, TB]), sb("yy", [P, TB]), sb("rstd", [P, TB])
        xn = sb("xn", [P, TB, H])
        xh, xl = sb("xh", [P, KT, SEQ], F32R), sb("xl", [P, KT, SEQ], F32R)
        qT, kT = sb("qT", [P, 2, DT, SEQ]), sb("kT", [P, 2, DT, SEQ])
        v = sb("v", [P, 2, TB, D])
        gate = sb("gate", [P, 2, DT, SEQ])
        sm = sb("sm", [P, NC, P])
        nmax, rsum, rinv = sb("nmax", [P, NC]), sb("rsum", [P, NC]), sb("rinv", [P, NC])
        st = sb("st", [P, START[-1] + P])
        o = sb("o", [P, 2, SEQ])
        oh, ol = sb("oh", [P, 2, SEQ], F32R), sb("ol", [P, 2, SEQ], F32R)
        yT = sb("yT", [P, KT, SEQ])

        p_loaded = [sem("p_loaded%d" % i) for i in range(RAW)]
        FB = ps("FB", [P, 2, 512])
        DB = ps("DB", [P, 2, 512])
        PV = ps("PV", [P, 2, 512])
        Y = ps("Y", [P, KT, 512])

        names = ("w_split const a_split x_loaded res_ready ln_stat ln_var ln_log ln_guess ln_done f_done "
                 "f_act f_dve xh_done d_done soft_step masked exp_done soft_done o_done o_out pt_done pt_out "
                 "pv_done gated oh_done ol_done y_done ye_done fin_done out_done x_stored b_ready").split()
        (w_split, const, a_split, x_loaded, res_ready, ln_stat, ln_var, ln_log, ln_guess, ln_done, f_done,
         f_act, f_dve, xh_done, d_done, soft_step, masked, exp_done, soft_done, o_done, o_out, pt_done,
         pt_out, pv_done, gated, oh_done, ol_done, y_done, ye_done, fin_done, out_done, x_stored,
         b_ready) = [sem(n) for n in names]
        NSTAT = TB + 10

        pieces = ([(wh, wl, k, c) for c in range(0, 4 * D, 1024) for k in range(KT)] + [(woh, wol, None, 0)])

        def piece(t, k, c):
            return t[:, c:c + 1024] if k is None else t[:, k, c:c + 1024]

        with nc.Block() as block:
            def iterations(eng, body):
                body(-2, 0, False, False, True)
                body(-1, 1, False, True, True)
                body(0, 0, True, True, True)
                with eng.Fori(1, nseq - 3, 2) as reg:
                    body(reg, 1, True, True, True)
                    body(reg + 1, 0, True, True, True)
                body(nseq - 3, 1, True, True, True)
                body(nseq - 2, 0, True, True, False)
                body(nseq - 1, 1, True, False, False)

            @block.sync
            def _(sp):
                def load(s, par):
                    rows = seq_rows(sp, x_in, s)
                    read, loaded = in_register(sp, ev(s - 2, 1, 0)), in_register(sp, 16 * s)
                    at_least(sp, ln_done, read)
                    at_least(sp, res_ready, read)
                    at_least(sp, x_loaded, loaded)
                    sp.dma_start(xin[:, par], rows).then_inc(x_loaded, 16)

                def body(s, par, core, front, ahead):
                    if core:
                        rows = seq_rows(sp, x_out, s)
                        summed, stored = in_register(sp, ev(s, 2, 1)), in_register(sp, 16 * s)
                    if ahead and (not isinstance(s, int) or s >= 0):
                        load(s + 2, par)
                    if core:
                        at_least(sp, out_done, summed)
                        at_least(sp, x_stored, stored)
                        sp.dma_start(rows, xres[:, par]).then_inc(x_stored, 16)

                sp.dma_start(xin[:, 0], seq_rows(sp, x_in, 0)).then_inc(x_loaded, 16)
                for i, (_, _, k, c) in enumerate(pieces):
                    at_least(sp, w_split, i + 1 - RAW)
                    if k is None:
                        dst, src = raw[:, i % RAW].rearrange("p (c n) -> p c n", n=H), w_o.rearrange("(c p) n -> p c n", p=P)
                    else:
                        dst, src = raw[:, i % RAW], w_in[k * P:(k + 1) * P, c:c + 1024]
                    sp.dma_start(dst, src).then_inc(p_loaded[i % RAW], 16)
                    if i == 1:
                        for b, src in ((bq, b_q), (bk, b_k), (bg, b_g)):
                            for c in range(DT):
                                sp.dma_start(b[:, c:c + 1], src[c * P:(c + 1) * P].rearrange("(p o) -> p o", o=1)
                                             ).then_inc(b_ready, 16)
                        sp.dma_start(bv[:], row_broadcast(b_v)).then_inc(b_ready, 16)
                        sp.dma_start(bo[:], row_broadcast(b_o)).then_inc(b_ready, 16)
                sp.wait_ge(x_loaded, 16)
                sp.dma_start(xin[:, 1], seq_rows(sp, x_in, 1)).then_inc(x_loaded, 16)
                iterations(sp, body)
                sp.wait_ge(x_stored, 16 * nseq)

            @block.gpsimd
            def _(pool):
                def body(s, par, core, front, ahead):
                    if front:
                        at_least(pool, x_loaded, 16 * (s + 2))
                        at_least(pool, x_stored, 16 * s)
                        nc.gpsimd.tensor_tensor(xres[:, 1 - par], xin[:, 1 - par],
                                                bo[:].unsqueeze(1).to_broadcast([P, TB, H]),
                                                ALU.add).then_inc(res_ready, 1)

                nc.gpsimd.memset(ident[:], 0.0).then_inc(const, 1)
                nc.gpsimd.memset(maskc[:], 0.0).then_inc(const, 1)
                pool.wait_ge(const, 2)
                nc.gpsimd.affine_select(out=ident[:], in_=ident[:], compare_op=ALU.not_equal, fill=1.0,
                                        base=0, pattern=[[-1, P]], channel_multiplier=1).then_inc(const, 1)
                nc.gpsimd.affine_select(out=maskc[:], in_=maskc[:], compare_op=ALU.is_ge, fill=MASKED,
                                        base=0, pattern=[[-1, P]], channel_multiplier=1).then_inc(const, 1)
                for i, (hi, lo, k, c) in enumerate(pieces):
                    pool.wait_ge(a_split, i + 1)
                    nc.gpsimd.tensor_tensor(piece(lo, k, c), raw[:, i % RAW], piece(hi, k, c).bitcast(F32),
                                            ALU.subtract).then_inc(w_split, 1)
                pool.wait_ge(b_ready, BIASES)
                iterations(pool, body)

            @block.scalar
            def _(act):
                def front_use(s, par, i):
                    c, k = FRONT[i]
                    if c == "v":
                        return
                    if isinstance(s, int) and s == 0 and i == FRONT.index(("q", 0)):
                        act.wait_ge(b_ready, BIASES)
                    at_least(act, f_done, ev(s, NF, i))
                    src = FB[:, i % 2]
                    if c == "T":
                        nc.scalar.copy(xh[:, k], src).then_inc(xh_done, 1)
                    elif c == "g":
                        at_least(act, gated, ev(s - 2, DT, DT - 1))
                        nc.scalar.activation(gate[:, par, k], src, ACT.Sigmoid,
                                             bias=bg[:, k:k + 1]).then_inc(f_act, 1)
                    else:
                        dst, b = (qT, bq) if c == "q" else (kT, bk)
                        at_least(act, o_done, ev(s - 2, 2, 1))
                        nc.scalar.activation(dst[:, par, k], src, ACT.Identity, bias=b[:, k:k + 1]).then_inc(f_act, 1)

                def body(s, par, core, front, ahead):
                    for e in range(NSLOT):
                        for i in range(len(pieces)) if isinstance(s, int) and s == -1 else ():
                            if PIECE_SLOT[i] == e:
                                hi, _, k, c = pieces[i]
                                act.wait_ge(p_loaded[i % RAW], 16 * (i // RAW + 1))
                                nc.scalar.copy(piece(hi, k, c), raw[:, i % RAW]).then_inc(a_split, 1)
                        if core and O_SLOT <= e < O_SLOT + 2:
                            k = e - O_SLOT
                            at_least(act, o_done, ev(s, 2, k))
                            at_least(act, pv_done, ev(s - 1, DT, DT - 1))
                            if k == 0:
                                ins = nc.scalar.copy(st[:, START[0] + P:START[0] + P + OFF[0]], PV[:, 0, 0:OFF[0]])
                            else:
                                nc.scalar.copy(st[:, START[1] + P:START[1] + P + OFF[1]], PV[:, 1, 0:OFF[1]])
                                ins = nc.scalar.copy(st[:, START[2] + P:START[2] + P + OFF[2]],
                                                     PV[:, 1, OFF[1]:OFF[1] + OFF[2]])
                            ins.then_inc(o_out, 1)
                        if core and e == D_SLOT + 1:
                            at_least(act, masked, ev(s, 1, 0))
                            for b in range(NC):
                                ins = nc.scalar.activation(sm[:, b], sm[:, b], ACT.Exp, bias=nmax[:, b:b + 1],
                                                           accum_out=rsum[:, b:b + 1])
                            ins.then_inc(exp_done, 1)
                        if core and e == PT_SLOT:
                            at_least(act, pt_done, ev(s, 1, 0))
                            for kb in range(NC):
                                ins = nc.scalar.copy(st[:, START[kb]:START[kb] + P], DB[:, 1, kb * P:(kb + 1) * P])
                            ins.then_inc(pt_out, 1)
                        if core and PV_SLOT <= e < PV_SLOT + DT:
                            k = e - PV_SLOT
                            at_least(act, gated, ev(s, DT, k))
                            if k >= 2:
                                at_least(act, y_done, ev(s, DT, k - 2))
                            nc.scalar.copy(oh[:, k % 2], o[:, k % 2]).then_inc(oh_done, 1)
                        if core and e == W_SLOT + DT:
                            at_least(act, y_done, ev(s, DT, DT - 1))
                            for k in range(KT):
                                ins = nc.scalar.copy(yT[:, k], Y[:, k])
                            ins.then_inc(ye_done, 1)
                        if ahead and e == LOG_SLOT:
                            at_least(act, ln_var, ev(s + 2, 1, 0))
                            nc.scalar.activation(lnv[:], var[:], ACT.Ln).then_inc(ln_log, 1)
                        if ahead and e == GUESS_SLOT:
                            at_least(act, ln_log, ev(s + 2, 1, 0))
                            nc.scalar.activation(guess[:], lnv[:], ACT.Exp, scale=-0.5).then_inc(ln_guess, 1)
                        if not front:
                            continue
                        for i in FRONT_AT.get(e, ()):
                            front_use(s + 1, 1 - par, i)

                iterations(act, body)

            @block.vector
            def _(dve):
                def statistics(s, par):
                    at_least(dve, x_loaded, 16 * (s + 1))
                    for b in range(TB):
                        nc.vector.bn_stats(stats[:, b, :], xin[:, par, b, :]).then_inc(ln_stat, 1)

                def variance(s):
                    m0, m1, q0, q1 = (stats[:, :, c] for c in (1, 4, 2, 5))
                    dve.wait_ge(ln_stat, ev(s, NSTAT, TB - 1))
                    nc.vector.tensor_tensor(mean[:], m0, m1, ALU.add).then_inc(ln_stat, 1)
                    nc.vector.tensor_tensor(yy[:], m0, m1, ALU.subtract).then_inc(ln_stat, 1)
                    nc.vector.tensor_tensor(var[:], q0, q1, ALU.add).then_inc(ln_stat, 1)
                    dve.wait_ge(ln_stat, ev(s, NSTAT, TB + 2))
                    nc.vector.tensor_scalar(mean[:], mean[:], 0.5, None, ALU.mult).then_inc(ln_stat, 1)
                    nc.vector.tensor_tensor(yy[:], yy[:], yy[:], ALU.mult).then_inc(ln_stat, 1)
                    nc.vector.tensor_scalar(var[:], var[:], 1.0 / H, EPS, ALU.mult, ALU.add).then_inc(ln_stat, 1)
                    dve.wait_ge(ln_stat, ev(s, NSTAT, TB + 5))
                    nc.vector.scalar_tensor_tensor(out=var[:], in0=yy[:], scalar=0.25, in1=var[:],
                                                   op0=ALU.mult, op1=ALU.add).then_inc(ln_var, 1)

                def inverse_deviation(s):
                    at_least(dve, ln_guess, ev(s, 1, 0))
                    nc.vector.tensor_tensor(yy[:], guess[:], guess[:], ALU.mult).then_inc(ln_stat, 1)
                    dve.wait_ge(ln_stat, ev(s, NSTAT, TB + 6))
                    nc.vector.tensor_tensor(yy[:], yy[:], var[:], ALU.mult).then_inc(ln_stat, 1)
                    dve.wait_ge(ln_stat, ev(s, NSTAT, TB + 7))
                    nc.vector.tensor_scalar(yy[:], yy[:], -0.5, 1.5, ALU.mult, ALU.add).then_inc(ln_stat, 1)
                    dve.wait_ge(ln_stat, ev(s, NSTAT, TB + 8))
                    nc.vector.tensor_tensor(rstd[:], guess[:], yy[:], ALU.mult).then_inc(ln_stat, 1)

                def normalise(s, par):
                    dve.wait_ge(ln_stat, ev(s, NSTAT, TB + 9))
                    at_least(dve, f_done, ev(s - 1, NF, KT - 1))
                    for b in range(TB):
                        ins = nc.vector.tensor_scalar(xn[:, b, :], xin[:, par, b, :], mean[:, b:b + 1],
                                                      rstd[:, b:b + 1], ALU.subtract, ALU.mult)
                    ins.then_inc(ln_done, 1)

                def front_use(s, par, i):
                    c, k = FRONT[i]
                    src = FB[:, i % 2]
                    if c == "T":
                        at_least(dve, xh_done, ev(s, KT, k))
                        nc.vector.tensor_tensor(xl[:, k], src, xh[:, k].bitcast(F32), ALU.subtract).then_inc(f_dve, 1)
                    if c == "v":
                        if isinstance(s, int) and s == 0 and k == 0:
                            dve.wait_ge(b_ready, BIASES)
                        at_least(dve, f_done, ev(s, NF, i))
                        at_least(dve, pv_done, ev(s - 2, DT, DT - 1))
                        nc.vector.tensor_tensor(v[:, par, k], src, bv[:], ALU.add).then_inc(f_dve, 1)

                def body(s, par, core, front, ahead):
                    for e in range(NSLOT):
                        if core and e == D_SLOT:
                            at_least(dve, d_done, ev(s, 1, 0))
                            at_least(dve, pt_done, ev(s - 1, 1, 0))
                            nc.vector.scalar_tensor_tensor(
                                out=sm[:], in0=DB[:, 0].rearrange("p (b c) -> p b c", b=NC), scalar=float(D) ** -0.5,
                                in1=maskc[:].unsqueeze(1).to_broadcast([P, NC, P]), op0=ALU.mult,
                                op1=ALU.add).then_inc(soft_step, 1)
                            dve.wait_ge(soft_step, ev(s, 2, 0))
                            nc.vector.tensor_reduce(nmax[:], sm[:], AX.X, ALU.max, negate=True).then_inc(masked, 1)
                        if core and e == D_SLOT + 1:
                            at_least(dve, exp_done, ev(s, 1, 0))
                            nc.vector.reciprocal(rinv[:], rsum[:]).then_inc(soft_step, 1)
                            dve.wait_ge(soft_step, ev(s, 2, 1))
                            nc.vector.tensor_tensor(sm[:], sm[:], rinv[:].unsqueeze(2).to_broadcast([P, NC, P]),
                                                    ALU.mult).then_inc(soft_done, 1)
                        if core and PV_SLOT <= e < PV_SLOT + DT:
                            k = e - PV_SLOT
                            at_least(dve, pv_done, ev(s, DT, k))
                            at_least(dve, f_act, ev(s, NFA, act_no[2 + 3 * DT + k]))
                            at_least(dve, oh_done, ev(s, DT, k - 2) if k >= 2 else ev(s - 1, DT, DT + k - 2))
                            nc.vector.tensor_tensor(o[:, k % 2], PV[:, k % 2], gate[:, par, k], ALU.mult).then_inc(gated, 1)
                            at_least(dve, oh_done, ev(s, DT, k))
                            nc.vector.tensor_tensor(ol[:, k % 2], o[:, k % 2], oh[:, k % 2].bitcast(F32),
                                                    ALU.subtract).then_inc(ol_done, 1)
                        if core and FIN_SLOT <= e < FIN_SLOT + 2:
                            k = e - FIN_SLOT
                            at_least(dve, fin_done, ev(s, 2, k))
                            at_least(dve, res_ready, ev(s, 1, 0))
                            xr = xres[:, par, 2 * k:2 * k + 2, :]
                            nc.vector.tensor_tensor(xr, DB[:, k].rearrange("p (b h) -> p b h", b=2), xr,
                                                    ALU.add).then_inc(out_done, 1)
                        if ahead and e == STAT_SLOT:
                            statistics(s + 2, par)
                        if ahead and e == VAR_SLOT:
                            variance(s + 2)
                        if ahead and e == ROOT_SLOT:
                            inverse_deviation(s + 2)
                        if ahead and e == NORM_SLOT:
                            normalise(s + 2, par)
                        if not front:
                            continue
                        for i in FRONT_AT.get(e, ()):
                            front_use(s + 1, 1 - par, i)

                dve.wait_ge(const, 4)
                iterations(dve, body)

            @block.tensor
            def _(pe):
                def three(out, ah, al, bh, bl, first, last):
                    pe.matmul(out, al, bh, start=first, stop=False)
                    pe.matmul(out, ah, bl, start=False, stop=False)
                    return pe.matmul(out, ah, bh, start=False, stop=last)

                def front_use(s, par, i):
                    c, k = FRONT[i]
                    dst = FB[:, i % 2]
                    j, sj = (i - 2, s) if i >= 2 else (i - 2 + NF, s - 1)
                    if by_act[j]:
                        at_least(pe, f_act, ev(sj, NFA, act_no[j]))
                    else:
                        at_least(pe, f_dve, ev(sj, NFD, dve_no[j]))
                    if c == "T":
                        at_least(pe, ln_done, ev(s, 1, 0))
                        for b in range(TB):
                            ins = pe.transpose(dst[:, b * P:(b + 1) * P], xn[:, b, k * P:(k + 1) * P], ident[:])
                    elif c == "v":
                        if isinstance(s, int) and s == 0:
                            pe.wait_ge(w_split, 2 * KT)
                        for t in range(KT):
                            ins = three(dst, xh[:, t, k * P:(k + 1) * P], xl[:, t, k * P:(k + 1) * P],
                                        wh[:, t, 2 * D:3 * D], wl[:, t, 2 * D:3 * D], t == 0, t == KT - 1)
                    else:
                        if isinstance(s, int) and s == 0 and c == "q":
                            pe.wait_ge(w_split, KT)
                        at_least(pe, f_dve, ev(s, NFD, KT - 1))
                        w = slice("qkvg".index(c) * D + k * P, "qkvg".index(c) * D + (k + 1) * P)
                        for t in range(KT):
                            ins = three(dst, wh[:, t, w], wl[:, t, w], xh[:, t], xl[:, t], t == 0, t == KT - 1)
                    ins.then_inc(f_done, 1)

                def body(s, par, core, front, ahead):
                    for e in range(NSLOT):
                        if core and e == D_SLOT:
                            at_least(pe, f_act, ev(s, NFA, 2 * DT - 1))
                            at_least(pe, out_done, ev(s - 1, 2, 0))
                            for b in range(NC):
                                for t in range(DT):
                                    ins = pe.matmul(DB[:, 0, b * P:(b + 1) * P], qT[:, par, t, b * P:(b + 1) * P],
                                                    kT[:, par, t, b * P:(b + 1) * P], start=(t == 0), stop=(t == DT - 1))
                            ins.then_inc(d_done, 1)
                        if core and O_SLOT <= e < O_SLOT + 2:
                            at_least(pe, gated, ev(s - 1, DT, DT - 1))
                            c = 0
                            for kb in ((0,) if e == O_SLOT else (1, 2)):
                                for t in range(DT):
                                    ins = pe.matmul(PV[:, e - O_SLOT, c:c + OFF[kb]], kT[:, par, t, kb * P:(kb + 1) * P],
                                                    qT[:, par, t, (kb + 1) * P:SEQ], start=(t == 0), stop=(t == DT - 1))
                                c += OFF[kb]
                            ins.then_inc(o_done, 1)
                        if core and e == PT_SLOT:
                            at_least(pe, soft_done, ev(s, 1, 0))
                            at_least(pe, out_done, ev(s - 1, 2, 1))
                            for b in range(NC):
                                ins = pe.transpose(DB[:, 1, b * P:(b + 1) * P], sm[:, b], ident[:])
                            ins.then_inc(pt_done, 1)
                        if core and PV_SLOT <= e < PV_SLOT + DT:
                            k = e - PV_SLOT
                            if k == 0:
                                at_least(pe, pt_out, ev(s, 1, 0))
                                at_least(pe, o_out, ev(s, 2, 1))
                                at_least(pe, f_dve, ev(s, NFD, NFD - 1))
                            if k >= 2:
                                at_least(pe, gated, ev(s, DT, k - 2))
                            for kb in range(NC):
                                n = SEQ - kb * P
                                ins = pe.matmul(PV[:, k % 2, kb * P:SEQ], v[:, par, kb, k * P:(k + 1) * P],
                                                st[:, START[kb]:START[kb] + n], start=(kb == 0), stop=(kb == NC - 1))
                            ins.then_inc(pv_done, 1)
                        if core and W_SLOT <= e < W_SLOT + DT:
                            k = e - W_SLOT
                            at_least(pe, ol_done, ev(s, DT, k))
                            at_least(pe, ye_done, ev(s - 1, 1, 0))
                            if isinstance(s, int) and s == 0:
                                pe.wait_ge(w_split, len(pieces))
                            for h in range(KT):
                                w = slice(k * H + h * P, k * H + (h + 1) * P)
                                ins = three(Y[:, h], woh[:, w], wol[:, w], oh[:, k % 2], ol[:, k % 2], k == 0, k == DT - 1)
                            ins.then_inc(y_done, 1)
                        if core and FIN_SLOT <= e < FIN_SLOT + 2:
                            k = e - FIN_SLOT
                            at_least(pe, ye_done, ev(s, 1, 0))
                            if k:
                                at_least(pe, pt_out, ev(s, 1, 0))
                            else:
                                at_least(pe, masked, ev(s, 1, 0))
                            for b in range(2):
                                for c in range(KT):
                                    ins = pe.transpose(DB[:, k, b * H + c * P:b * H + (c + 1) * P],
                                                       yT[:, c, (2 * k + b) * P:(2 * k + b + 1) * P], ident[:])
                            ins.then_inc(fin_done, 1)
                        if front:
                            for i in FRONT_AT.get(e, ()):
                                front_use(s + 1, 1 - par, i)

                pe.wait_ge(const, 4)
                iterations(pe, body)


def transformer_block(nc, w, out):
    x = w["x"].rearrange("b s h -> (b s) h")
    nseq = x.shape[0] // SEQ
    x1 = nc.dram_tensor("x_after_a", x.shape, F32, kind="Internal").ap()
    x2 = nc.dram_tensor("x_after_f", x.shape, F32, kind="Internal").ap()
    x3 = nc.dram_tensor("x_after_b", x.shape, F32, kind="Internal").ap()
    phase_a(nc, x, x1, w["w_qkv"], w["b_qkv"], w["w_out"], w["b_out"], nseq)
    phase_f(nc, "f1_", x1, x2, w["w_gate"], w["bias_corr"], w["w1"], w["w2"], nseq)
    phase_b(nc, x2, x3, w["w_in"], w["b_q"], w["b_k"], w["b_v"], w["b_g"], w["w_o"], w["b_o"], nseq)
    phase_f(nc, "f2_", x3, out.rearrange("b s h -> (b s) h"), w["w_gate"], w["bias_corr"], w["w1"], w["w2"], nseq)


def kernel(**inputs):
    import numpy as np
    import concourse.bacc as bacc
    from concourse.bass_utils import run_bass_kernel_spmd

    def get(name):
        return np.asarray(inputs[name])

    W1, W2 = get("L0_ffn_W1"), get("L0_ffn_W2")
    Ws1, Ws2 = get("L0_ffn_Ws1"), get("L0_ffn_Ws2")
    h = Ws1.shape[1]
    arrays = {
        "x": get("L0_attn_a_x"),
        "w_qkv": get("L0_attn_a_w_qkv"), "b_qkv": get("L0_attn_a_b_qkv"),
        "w_out": get("L0_attn_a_w_out"), "b_out": get("L0_attn_a_b_out"),
        "w_in": np.concatenate([get("L0_attn_b_W" + c) for c in "qkvg"], axis=1),
        "b_q": get("L0_attn_b_bq"), "b_k": get("L0_attn_b_bk"), "b_v": get("L0_attn_b_bv"), "b_g": get("L0_attn_b_bg"),
        "w_o": get("L0_attn_b_Wo"), "b_o": get("L0_attn_b_bo"),
        "w_gate": get("L0_ffn_Wg").T, "bias_corr": get("L0_ffn_bias_corr"),
        "w1": np.concatenate([W1.transpose(2, 0, 1).reshape(h, -1), Ws1.T], axis=1),
        "w2": np.concatenate([W2.transpose(2, 0, 1).reshape(P, -1),
                              Ws2.T.reshape(-1, P, h).transpose(1, 0, 2).reshape(P, -1)], axis=1),
    }
    arrays = {k: np.ascontiguousarray(a) for k, a in arrays.items()}
    nc = bacc.Bacc("TRN2", target_bir_lowering=False, num_devices=1)
    w = {k: nc.dram_tensor("in_" + k, a.shape, mybir.dt.from_np(a.dtype), kind="ExternalInput").ap() for k, a in arrays.items()}
    out = nc.dram_tensor("out", arrays["x"].shape, F32, kind="ExternalOutput").ap()
    transformer_block(nc, w, out)
    r = run_bass_kernel_spmd(nc, [{"in_" + k: a for k, a in arrays.items()}], core_ids=[0])
    return r.results[0]["out"]
```
